# Optimizing a Trainium2 kernel written in Bass

```python
import numpy as np
import jax
import jax.numpy as jnp

def _softmax(x, axis=-1):
    return jax.nn.softmax(x, axis=axis)

def _gelu(x):
    return jax.nn.gelu(x, approximate=True)

def _silu(x):
    return jax.nn.silu(x)

def _sigmoid(x):
    return jax.nn.sigmoid(x)

def _layernorm(x, axis=-1, eps=1e-05):
    m = jnp.mean(x, axis=axis, keepdims=True)
    v = jnp.var(x, axis=axis, keepdims=True)
    return (x - m) / jnp.sqrt(v + eps)

def _scatter_add(tgt, idx, src, axis=0):
    return tgt.at[idx].add(src)

def _segment_sum(src, seg, n):
    return jax.ops.segment_sum(src, seg, n)
kernel_name = 'mk_gnn_ffn_d4_gnn_r16_e570cf'

def setup_inputs(seed: int=0):
    np.random.seed(seed)
    _w = jnp.asarray

    def _rec_inputs():
        import jax
        import jax.numpy as jnp
        _gk = jax.random.key(seed)
        x = -0.0001126 + 1 * jax.random.normal(jax.random.fold_in(_gk, 1), (1875, 256), jnp.float32)
        _s = jax.random.randint(jax.random.fold_in(_gk, 2), (15000,), 0, 1875, jnp.int32)
        _d = jax.random.randint(jax.random.fold_in(_gk, 3), (15000,), 0, 1875, jnp.int32)
        _loop = jnp.arange(1875, dtype=jnp.int32)
        src = jnp.concatenate([_s, _d, _loop])
        dst = jnp.concatenate([_d, _s, _loop])
        _o = jnp.argsort(dst, stable=True)
        src = src[_o]
        dst = dst[_o]
        edge_attr_32 = 0.000251555 + 0.999981 * jax.random.normal(jax.random.fold_in(_gk, 11), (31875, 32), jnp.float32)
        edge_type_8 = jax.random.randint(jax.random.fold_in(_gk, 13), (31875,), 0, 8, jnp.int32)
        edge_weight = jax.random.uniform(jax.random.fold_in(_gk, 14), (31875,), jnp.float32, 0.0, 0.999998)
        return (x, src, dst, edge_attr_32, edge_type_8, edge_weight)
    x, src, dst, edge_attr_32, edge_type_8, edge_weight = _rec_inputs()

    def _L0_gnn_setup():
        import jax, jax.numpy as jnp
        import numpy as np
        N = 1875
        E = 30000
        D = 256
        ED = 32
        L = 4

        def _layernorm(x, g, b):
            mu = jnp.mean(x, axis=-1, keepdims=True)
            var = jnp.var(x, axis=-1, keepdims=True)
            return (x - mu) * jax.lax.rsqrt(var + 1e-05) * g + b

        def _gine(x, src, dst, edge_attr, W1, b1, W2, b2, eW, eb, eps):
            e = edge_attr @ eW + eb
            m = jax.nn.relu(x[src] + e)
            agg = jax.ops.segment_sum(m, dst, num_segments=N)
            h = (1.0 + eps) * x + agg
            return jax.nn.relu(h @ W1 + b1) @ W2 + b2
        key = jax.random.key(seed)
        ks = jax.random.split(key, 8)
        s = 1.0 / np.sqrt(D)
        return dict(x=jax.random.normal(ks[0], (N, D), jnp.float32), edge_index=jax.random.randint(ks[1], (2, E), 0, N, jnp.int32), edge_attr=jax.random.normal(ks[2], (E, ED), jnp.float32), W1=jax.random.normal(ks[3], (L, D, D), jnp.float32) * s, b1=jnp.zeros((L, D), jnp.float32), W2=jax.random.normal(ks[4], (L, D, D), jnp.float32) * s, b2=jnp.zeros((L, D), jnp.float32), eW=jax.random.normal(ks[5], (L, ED, D), jnp.float32) * (1.0 / np.sqrt(ED)), eb=jnp.zeros((L, D), jnp.float32), eps=jnp.zeros((L,), jnp.float32), gamma=jnp.ones((L, D), jnp.float32), beta=jnp.zeros((L, D), jnp.float32))
    _L0_gnn_all = _L0_gnn_setup()
    _L0_gnn_in = {k: v for k, v in _L0_gnn_all.items() if k in ('W1', 'b1', 'W2', 'b2', 'eW', 'eb', 'eps', 'gamma', 'beta')}
    del _L0_gnn_all

    def _L0_ffn_setup():
        import jax, jax.numpy as jnp
        import numpy as np
        B, S, D = (8, 256, 256)
        H = 4 * D
        CAPACITY = 0.5
        key = jax.random.key(seed)
        ks = jax.random.split(key, 6)
        x = jax.random.normal(ks[0], (B, S, D), dtype=jnp.float32)
        attention_mask = jnp.zeros((B, 1, 1, S), dtype=jnp.float32)
        wr = jax.random.normal(ks[1], (D, 1), dtype=jnp.float32) * 0.02
        br = jnp.zeros((1,), dtype=jnp.float32)
        w1 = jax.random.normal(ks[2], (D, H), dtype=jnp.float32) * 0.02
        b1 = jnp.zeros((H,), dtype=jnp.float32)
        w2 = jax.random.normal(ks[3], (H, D), dtype=jnp.float32) * 0.02
        b2 = jnp.zeros((D,), dtype=jnp.float32)
        return {'x': x, 'attention_mask': attention_mask, 'wr': wr, 'br': br, 'w1': w1, 'b1': b1, 'w2': w2, 'b2': b2}
    _L0_ffn_all = _L0_ffn_setup()
    _L0_ffn_in = {k: v for k, v in _L0_ffn_all.items() if k in ('attention_mask', 'wr', 'br', 'w1', 'b1', 'w2', 'b2')}
    del _L0_ffn_all

    def _L1_gnn_setup():
        import jax, jax.numpy as jnp
        import numpy as np
        N, E, R, H, D = (1875, 18750, 8, 8, 32)
        IN_F = 256
        NEG_SLOPE = 0.2
        key = jax.random.key(seed)
        k = jax.random.split(key, 6)
        x = jax.random.normal(k[0], (N, IN_F), dtype=jnp.float32)
        W = jax.random.normal(k[1], (R, H * D, IN_F), dtype=jnp.float32) * 0.05
        attn_src = jax.random.normal(k[2], (H, D), dtype=jnp.float32) * 0.1
        attn_dst = jax.random.normal(k[3], (H, D), dtype=jnp.float32) * 0.1
        edge_index = jax.random.randint(k[4], (2, E), 0, N, dtype=jnp.int64) if jax.config.read('jax_enable_x64') else jax.random.randint(k[4], (2, E), 0, N, dtype=jnp.int32)
        edge_type = jax.random.randint(k[5], (E,), 0, R, dtype=edge_index.dtype)
        return dict(x=x, W=W, attn_src=attn_src, attn_dst=attn_dst, edge_index=edge_index, edge_type=edge_type)
    _L1_gnn_all = _L1_gnn_setup()
    _L1_gnn_in = {k: v for k, v in _L1_gnn_all.items() if k in ('W', 'attn_src', 'attn_dst')}
    del _L1_gnn_all

    def _L1_ffn_setup():
        import math
        import jax, jax.numpy as jnp
        import numpy as np
        CAPACITY_FACTOR = 1.25
        key = jax.random.key(seed)
        ks = jax.random.split(key, 5)
        B, L, D, F, E = (8, 512, 256, 1024, 8)
        h = jax.random.normal(ks[0], (B, L, D), dtype=jnp.float32)
        gate_w = jax.random.normal(ks[1], (D, E), dtype=jnp.float32) * 0.02
        gate_b = jnp.zeros((E,), dtype=jnp.float32)
        w1 = jax.random.normal(ks[2], (E, D, F), dtype=jnp.float32) * (1.0 / math.sqrt(D))
        b1 = jnp.zeros((E, F), dtype=jnp.float32)
        w2 = jax.random.normal(ks[3], (E, F, D), dtype=jnp.float32) * (1.0 / math.sqrt(F))
        b2 = jnp.zeros((E, D), dtype=jnp.float32)
        return {'h': h, 'gate_w': gate_w, 'gate_b': gate_b, 'w1': w1, 'b1': b1, 'w2': w2, 'b2': b2}
    _L1_ffn_all = _L1_ffn_setup()
    _L1_ffn_in = {k: v for k, v in _L1_ffn_all.items() if k in ('gate_w', 'gate_b', 'w1', 'b1', 'w2', 'b2')}
    del _L1_ffn_all

    def _L2_gnn_setup():
        import jax, jax.numpy as jnp
        import numpy as np
        N_NODES = 625

        def gcn_conv(x, edge_index, edge_weight, W, b, n):
            src = jnp.concatenate([edge_index[0], jnp.arange(n)])
            dst = jnp.concatenate([edge_index[1], jnp.arange(n)])
            ew = jnp.concatenate([edge_weight, jnp.ones((n,), edge_weight.dtype)])
            deg = jax.ops.segment_sum(ew, dst, num_segments=n)
            dinv = jnp.where(deg > 0, jax.lax.rsqrt(deg), 0.0)
            norm = dinv[src] * ew * dinv[dst]
            h = x @ W
            msg = norm[:, None] * h[src]
            return jax.ops.segment_sum(msg, dst, num_segments=n) + b
        key = jax.random.key(seed)
        k1, k2, k3, k4, k5, k6 = jax.random.split(key, 6)
        n, e, d_in, d_out = (N_NODES, 20000, 256, 256)
        x = jax.random.normal(k1, (n, d_in), jnp.float32)
        edge_index = jax.random.randint(k2, (2, e), 0, n, jnp.int64)
        edge_weight = jax.random.uniform(k3, (e,), jnp.float32)
        s1 = 1.0 / np.sqrt(d_in)
        W1 = jax.random.uniform(k4, (d_in, d_in), jnp.float32, -s1, s1)
        b1 = jnp.zeros((d_in,), jnp.float32)
        W2 = jax.random.uniform(k5, (d_in, d_out), jnp.float32, -s1, s1)
        b2 = jnp.zeros((d_out,), jnp.float32)
        return {'x': x, 'edge_index': edge_index, 'edge_weight': edge_weight, 'W1': W1, 'b1': b1, 'W2': W2, 'b2': b2}
    _L2_gnn_all = _L2_gnn_setup()
    _L2_gnn_in = {k: v for k, v in _L2_gnn_all.items() if k in ('W1', 'b1', 'W2', 'b2')}
    del _L2_gnn_all

    def _L2_ffn_setup():
        import jax, jax.numpy as jnp
        import numpy as np
        TOP_K = 2
        LN_EPS = 1e-05
        key = jax.random.key(seed)
        ks = jax.random.split(key, 8)
        B, S, D, E, H = (16, 1024, 256, 8, 1024)
        x = jax.random.normal(ks[0], (B, S, D), dtype=jnp.float32)
        Wr = jax.random.normal(ks[1], (D, E), dtype=jnp.float32) * 0.1
        br = jnp.zeros((E,), dtype=jnp.float32)
        ln_g = jnp.ones((E, D), dtype=jnp.float32)
        ln_b = jnp.zeros((E, D), dtype=jnp.float32)
        W1 = jax.random.normal(ks[2], (E, D, H), dtype=jnp.float32) * (1.0 / np.sqrt(D))
        b1 = jnp.zeros((E, H), dtype=jnp.float32)
        W2 = jax.random.normal(ks[3], (E, H, D), dtype=jnp.float32) * (1.0 / np.sqrt(H))
        b2 = jnp.zeros((E, D), dtype=jnp.float32)
        return {'x': x, 'Wr': Wr, 'br': br, 'ln_g': ln_g, 'ln_b': ln_b, 'W1': W1, 'b1': b1, 'W2': W2, 'b2': b2}
    _L2_ffn_all = _L2_ffn_setup()
    _L2_ffn_in = {k: v for k, v in _L2_ffn_all.items() if k in ('Wr', 'br', 'ln_g', 'ln_b', 'W1', 'b1', 'W2', 'b2')}
    del _L2_ffn_all

    def _L3_gnn_setup():
        import jax, jax.numpy as jnp
        import numpy as np
        from jax.ops import segment_sum
        N_NODES = 3125
        N_EDGES = 20000
        DIM = 256
        key = jax.random.key(seed)
        k1, k2, k3, k4, k5 = jax.random.split(key, 5)
        x = jax.random.normal(k1, (N_NODES, DIM), dtype=jnp.float32)
        edge_index = jax.random.randint(k2, (2, N_EDGES), 0, N_NODES, dtype=jnp.int64)
        edge_attr = jax.random.uniform(k3, (N_EDGES,), dtype=jnp.float32)
        W = jax.random.normal(k4, (DIM, DIM), dtype=jnp.float32) / np.sqrt(DIM)
        b = jnp.zeros((DIM,), dtype=jnp.float32)
        return {'x': x, 'edge_index': edge_index, 'edge_attr': edge_attr, 'W': W, 'b': b}
    _L3_gnn_all = _L3_gnn_setup()
    _L3_gnn_in = {k: v for k, v in _L3_gnn_all.items() if k in ('W', 'b')}
    del _L3_gnn_all

    def _L3_ffn_setup():
        import jax, jax.numpy as jnp
        import numpy as np
        B, S, H, F, E, K = (8, 256, 256, 512, 16, 2)
        EPS = 1e-05
        key = jax.random.key(seed)
        ks = jax.random.split(key, 9)
        sc = 0.02
        return {'x': jax.random.normal(ks[0], (B, S, H), dtype=jnp.float32), 'gate_w': jax.random.normal(ks[1], (H, E), dtype=jnp.float32) * sc, 'gate_b': jnp.zeros((E,), dtype=jnp.float32), 'w1': jax.random.normal(ks[2], (E, H, F), dtype=jnp.float32) * sc, 'b1': jnp.zeros((E, F), dtype=jnp.float32), 'w2': jax.random.normal(ks[3], (E, F, H), dtype=jnp.float32) * sc, 'b2': jnp.zeros((E, H), dtype=jnp.float32), 'gamma': jnp.ones((H,), dtype=jnp.float32), 'beta': jnp.zeros((H,), dtype=jnp.float32)}
    _L3_ffn_all = _L3_ffn_setup()
    _L3_ffn_in = {k: v for k, v in _L3_ffn_all.items() if k in ('gate_w', 'gate_b', 'w1', 'b1', 'w2', 'b2', 'gamma', 'beta')}
    del _L3_ffn_all
    return {'x': x, 'src': src, 'dst': dst, 'edge_attr_32': edge_attr_32, 'edge_type_8': edge_type_8, 'edge_weight': edge_weight, 'L0_gnn_W1': _L0_gnn_in['W1'], 'L0_gnn_b1': _L0_gnn_in['b1'], 'L0_gnn_W2': _L0_gnn_in['W2'], 'L0_gnn_b2': _L0_gnn_in['b2'], 'L0_gnn_eW': _L0_gnn_in['eW'], 'L0_gnn_eb': _L0_gnn_in['eb'], 'L0_gnn_eps': _L0_gnn_in['eps'], 'L0_gnn_gamma': _L0_gnn_in['gamma'], 'L0_gnn_beta': _L0_gnn_in['beta'], 'L0_ffn_attention_mask': _L0_ffn_in['attention_mask'], 'L0_ffn_wr': _L0_ffn_in['wr'], 'L0_ffn_br': _L0_ffn_in['br'], 'L0_ffn_w1': _L0_ffn_in['w1'], 'L0_ffn_b1': _L0_ffn_in['b1'], 'L0_ffn_w2': _L0_ffn_in['w2'], 'L0_ffn_b2': _L0_ffn_in['b2'], 'L1_gnn_W': _L1_gnn_in['W'], 'L1_gnn_attn_src': _L1_gnn_in['attn_src'], 'L1_gnn_attn_dst': _L1_gnn_in['attn_dst'], 'L1_ffn_gate_w': _L1_ffn_in['gate_w'], 'L1_ffn_gate_b': _L1_ffn_in['gate_b'], 'L1_ffn_w1': _L1_ffn_in['w1'], 'L1_ffn_b1': _L1_ffn_in['b1'], 'L1_ffn_w2': _L1_ffn_in['w2'], 'L1_ffn_b2': _L1_ffn_in['b2'], 'L2_gnn_W1': _L2_gnn_in['W1'], 'L2_gnn_b1': _L2_gnn_in['b1'], 'L2_gnn_W2': _L2_gnn_in['W2'], 'L2_gnn_b2': _L2_gnn_in['b2'], 'L2_ffn_Wr': _L2_ffn_in['Wr'], 'L2_ffn_br': _L2_ffn_in['br'], 'L2_ffn_ln_g': _L2_ffn_in['ln_g'], 'L2_ffn_ln_b': _L2_ffn_in['ln_b'], 'L2_ffn_W1': _L2_ffn_in['W1'], 'L2_ffn_b1': _L2_ffn_in['b1'], 'L2_ffn_W2': _L2_ffn_in['W2'], 'L2_ffn_b2': _L2_ffn_in['b2'], 'L3_gnn_W': _L3_gnn_in['W'], 'L3_gnn_b': _L3_gnn_in['b'], 'L3_ffn_gate_w': _L3_ffn_in['gate_w'], 'L3_ffn_gate_b': _L3_ffn_in['gate_b'], 'L3_ffn_w1': _L3_ffn_in['w1'], 'L3_ffn_b1': _L3_ffn_in['b1'], 'L3_ffn_w2': _L3_ffn_in['w2'], 'L3_ffn_b2': _L3_ffn_in['b2'], 'L3_ffn_gamma': _L3_ffn_in['gamma'], 'L3_ffn_beta': _L3_ffn_in['beta']}

def reference(x, src, dst, edge_attr_32, edge_type_8, edge_weight, L0_gnn_W1, L0_gnn_b1, L0_gnn_W2, L0_gnn_b2, L0_gnn_eW, L0_gnn_eb, L0_gnn_eps, L0_gnn_gamma, L0_gnn_beta, L0_ffn_attention_mask, L0_ffn_wr, L0_ffn_br, L0_ffn_w1, L0_ffn_b1, L0_ffn_w2, L0_ffn_b2, L1_gnn_W, L1_gnn_attn_src, L1_gnn_attn_dst, L1_ffn_gate_w, L1_ffn_gate_b, L1_ffn_w1, L1_ffn_b1, L1_ffn_w2, L1_ffn_b2, L2_gnn_W1, L2_gnn_b1, L2_gnn_W2, L2_gnn_b2, L2_ffn_Wr, L2_ffn_br, L2_ffn_ln_g, L2_ffn_ln_b, L2_ffn_W1, L2_ffn_b1, L2_ffn_W2, L2_ffn_b2, L3_gnn_W, L3_gnn_b, L3_ffn_gate_w, L3_ffn_gate_b, L3_ffn_w1, L3_ffn_b1, L3_ffn_w2, L3_ffn_b2, L3_ffn_gamma, L3_ffn_beta):
    import jax
    import jax.numpy as jnp

    def _L0_gnn_ref(x, edge_index, edge_attr, W1, b1, W2, b2, eW, eb, eps, gamma, beta):
        import jax, jax.numpy as jnp
        import numpy as np
        N = 1875
        E = 30000
        D = 256
        ED = 32
        L = 4

        def _layernorm(x, g, b):
            mu = jnp.mean(x, axis=-1, keepdims=True)
            var = jnp.var(x, axis=-1, keepdims=True)
            return (x - mu) * jax.lax.rsqrt(var + 1e-05) * g + b

        def _gine(x, src, dst, edge_attr, W1, b1, W2, b2, eW, eb, eps):
            e = edge_attr @ eW + eb
            m = jax.nn.relu(x[src] + e)
            agg = jax.ops.segment_sum(m, dst, num_segments=N)
            h = (1.0 + eps) * x + agg
            return jax.nn.relu(h @ W1 + b1) @ W2 + b2
        src, dst = (edge_index[0], edge_index[1])
        h = _gine(x, src, dst, edge_attr, W1[0], b1[0], W2[0], b2[0], eW[0], eb[0], eps[0])
        for k in range(1, L):
            y = jax.nn.relu(_layernorm(h, gamma[k], beta[k]))
            h = h + _gine(y, src, dst, edge_attr, W1[k], b1[k], W2[k], b2[k], eW[k], eb[k], eps[k])
        return jax.nn.relu(_layernorm(h, gamma[0], beta[0]))

    def _L0_ffn_ref(x, attention_mask, wr, br, w1, b1, w2, b2):
        import jax, jax.numpy as jnp
        import numpy as np
        B, S, D = (8, 256, 256)
        H = 4 * D
        CAPACITY = 0.5
        b, s, d = x.shape
        weights = (jnp.einsum('bsd,do->bso', x, wr) + br)[..., 0]
        k = max(1, int(CAPACITY * s))
        kk = k - 1 if k > 1 else 1
        _, idx = jax.lax.top_k(weights, k)
        sel_idx = idx[:, :kk]
        sel = jnp.take_along_axis(x, sel_idx[:, :, None], axis=1)
        h = jax.nn.gelu(jnp.einsum('bkd,dh->bkh', sel, w1) + b1)
        y = jnp.einsum('bkh,hd->bkd', h, w2) + b2
        w_sel = jnp.take_along_axis(weights, sel_idx, axis=1)
        y = y * w_sel[..., None]
        batch_idx = jnp.arange(b)[:, None]
        processed = jnp.zeros_like(x).at[batch_idx, sel_idx].set(y)
        return processed + x

    def _L1_gnn_ref(x, W, attn_src, attn_dst, edge_index, edge_type):
        import jax, jax.numpy as jnp
        import numpy as np
        N, E, R, H, D = (1875, 18750, 8, 8, 32)
        IN_F = 256
        NEG_SLOPE = 0.2
        n = x.shape[0]
        r = W.shape[0]
        h, d = attn_src.shape
        h_all = jnp.einsum('nf,rof->rno', x, W).reshape(r, n, h, d)
        src, dst = (edge_index[0], edge_index[1])
        h_src = h_all[edge_type, src]
        h_dst = h_all[edge_type, dst]
        scores = jnp.einsum('ehd,hd->eh', h_src, attn_src) + jnp.einsum('ehd,hd->eh', h_dst, attn_dst)
        scores = jnp.where(scores > 0, scores, NEG_SLOPE * scores)
        amax = jnp.maximum(jax.ops.segment_max(scores, dst, num_segments=n), 0.0)
        w = jnp.exp(scores - amax[dst])
        denom = jax.ops.segment_sum(w, dst, num_segments=n) + 1e-12
        w = w / denom[dst]
        msg = h_src * w[..., None]
        out = jax.ops.segment_sum(msg, dst, num_segments=n)
        return out.reshape(n, h * d)

    def _L1_ffn_ref(h, gate_w, gate_b, w1, b1, w2, b2):
        import math
        import jax, jax.numpy as jnp
        import numpy as np
        CAPACITY_FACTOR = 1.25
        B, L, D = h.shape
        E = gate_w.shape[1]
        T = B * L
        C = max(1, math.ceil(CAPACITY_FACTOR * T / E))
        x = h.reshape(T, D)
        logits = x @ gate_w + gate_b
        probs = jax.nn.softmax(logits, axis=-1)
        idx = jnp.argmax(probs, axis=-1)
        prb = jnp.take_along_axis(probs, idx[:, None], axis=1)[:, 0]
        one_hot = jax.nn.one_hot(idx, E, dtype=jnp.float32)
        pos = (jnp.cumsum(one_hot, axis=0) * one_hot).sum(-1).astype(jnp.int32) - 1
        kept = pos < C
        pos_safe = jnp.where(kept, pos, C)
        buf = jnp.zeros((E, C, D), dtype=h.dtype).at[idx, pos_safe].set(x, mode='drop')
        hmid = jax.nn.relu(jnp.einsum('ecd,edf->ecf', buf, w1) + b1[:, None, :])
        ybuf = jnp.einsum('ecf,efd->ecd', hmid, w2) + b2[:, None, :]
        pos_g = jnp.minimum(pos, C - 1)
        y_tok = ybuf[idx, pos_g] * (prb * kept)[:, None]
        y = y_tok.reshape(B, L, D)
        y = jnp.nan_to_num(y, nan=0.0, posinf=10000.0, neginf=-10000.0)
        return y

    def _L2_gnn_ref(x, edge_index, edge_weight, W1, b1, W2, b2):
        import jax, jax.numpy as jnp
        import numpy as np
        N_NODES = 625

        def gcn_conv(x, edge_index, edge_weight, W, b, n):
            src = jnp.concatenate([edge_index[0], jnp.arange(n)])
            dst = jnp.concatenate([edge_index[1], jnp.arange(n)])
            ew = jnp.concatenate([edge_weight, jnp.ones((n,), edge_weight.dtype)])
            deg = jax.ops.segment_sum(ew, dst, num_segments=n)
            dinv = jnp.where(deg > 0, jax.lax.rsqrt(deg), 0.0)
            norm = dinv[src] * ew * dinv[dst]
            h = x @ W
            msg = norm[:, None] * h[src]
            return jax.ops.segment_sum(msg, dst, num_segments=n) + b
        n = x.shape[0]
        h = gcn_conv(x, edge_index, edge_weight, W1, b1, n)
        h = jax.nn.relu(h)
        h = gcn_conv(h, edge_index, edge_weight, W2, b2, n)
        return jax.nn.softmax(h, axis=1)

    def _L2_ffn_ref(x, Wr, br, ln_g, ln_b, W1, b1, W2, b2):
        import jax, jax.numpy as jnp
        import numpy as np
        TOP_K = 2
        LN_EPS = 1e-05
        B, S, D = x.shape
        N = B * S
        xt = x.reshape(N, D)
        logits = xt @ Wr + br
        probs = jax.nn.softmax(logits, axis=-1)
        top_p, top_idx = jax.lax.top_k(probs, TOP_K)
        weights = top_p / top_p.sum(axis=-1, keepdims=True)
        mu = xt.mean(axis=-1, keepdims=True)
        var = ((xt - mu) ** 2).mean(axis=-1, keepdims=True)
        xn = (xt - mu) * jax.lax.rsqrt(var + LN_EPS)
        xe = xn[None, :, :] * ln_g[:, None, :] + ln_b[:, None, :]
        h = jax.nn.gelu(jnp.einsum('end,edh->enh', xe, W1) + b1[:, None, :], approximate=False)
        y = jnp.einsum('enh,ehd->end', h, W2) + b2[:, None, :]
        y_tok = jnp.transpose(y, (1, 0, 2))
        sel = jnp.take_along_axis(y_tok, top_idx[:, :, None], axis=1)
        out = (weights[:, :, None] * sel).sum(axis=1)
        return out.reshape(B, S, D)

    def _L3_gnn_ref(x, edge_index, edge_attr, W, b):
        import jax, jax.numpy as jnp
        import numpy as np
        from jax.ops import segment_sum
        N_NODES = 3125
        N_EDGES = 20000
        DIM = 256
        n = x.shape[0]
        loop = jnp.arange(n, dtype=edge_index.dtype)
        row = jnp.concatenate([edge_index[0], loop])
        col = jnp.concatenate([edge_index[1], loop])
        w = jnp.concatenate([edge_attr, jnp.ones((n,), dtype=edge_attr.dtype)])
        deg = segment_sum(w, col, num_segments=n)
        dinv = jnp.where(deg > 0, jax.lax.rsqrt(deg), 0.0)
        norm = dinv[row] * w * dinv[col]
        h = x @ W.T
        msg = h[row] * norm[:, None]
        agg = segment_sum(msg, col, num_segments=n) + b
        x1 = jax.nn.relu(agg)
        return x + x1

    def _L3_ffn_ref(x, gate_w, gate_b, w1, b1, w2, b2, gamma, beta):
        import jax, jax.numpy as jnp
        import numpy as np
        B, S, H, F, E, K = (8, 256, 256, 512, 16, 2)
        EPS = 1e-05
        gate_logits = x @ gate_w + gate_b
        topk_vals, topk_idx = jax.lax.top_k(gate_logits, K)
        topk_w = jax.nn.softmax(topk_vals, axis=-1)
        h = jax.nn.relu(jnp.einsum('bsh,ehf->bsef', x, w1) + b1)
        expert_out = jnp.einsum('bsef,efh->bseh', h, w2) + b2
        sel = jnp.take_along_axis(expert_out, topk_idx[:, :, :, None], axis=2)
        moe = jnp.sum(topk_w[..., None] * sel, axis=2)
        y = x + moe
        mu = jnp.mean(y, axis=-1, keepdims=True)
        var = jnp.var(y, axis=-1, keepdims=True)
        return (y - mu) / jnp.sqrt(var + EPS) * gamma + beta
    edge_index = jnp.stack([src, dst])
    x = x + _L0_gnn_ref(_layernorm(x, axis=-1), edge_index, edge_attr_32, L0_gnn_W1, L0_gnn_b1, L0_gnn_W2, L0_gnn_b2, L0_gnn_eW, L0_gnn_eb, L0_gnn_eps, L0_gnn_gamma, L0_gnn_beta)
    x = x + _L0_ffn_ref(_layernorm(x, axis=-1)[None], L0_ffn_attention_mask, L0_ffn_wr, L0_ffn_br, L0_ffn_w1, L0_ffn_b1, L0_ffn_w2, L0_ffn_b2)[0]
    x = x + _L1_gnn_ref(_layernorm(x, axis=-1), L1_gnn_W, L1_gnn_attn_src, L1_gnn_attn_dst, edge_index, edge_type_8)
    x = x + _L1_ffn_ref(_layernorm(x, axis=-1)[None], L1_ffn_gate_w, L1_ffn_gate_b, L1_ffn_w1, L1_ffn_b1, L1_ffn_w2, L1_ffn_b2)[0]
    x = x + _L2_gnn_ref(_layernorm(x, axis=-1), edge_index, edge_weight, L2_gnn_W1, L2_gnn_b1, L2_gnn_W2, L2_gnn_b2)
    x = x + _L2_ffn_ref(_layernorm(x, axis=-1)[None], L2_ffn_Wr, L2_ffn_br, L2_ffn_ln_g, L2_ffn_ln_b, L2_ffn_W1, L2_ffn_b1, L2_ffn_W2, L2_ffn_b2)[0]
    x = x + _L3_gnn_ref(_layernorm(x, axis=-1), edge_index, edge_weight, L3_gnn_W, L3_gnn_b)
    x = x + _L3_ffn_ref(_layernorm(x, axis=-1)[None], L3_ffn_gate_w, L3_ffn_gate_b, L3_ffn_w1, L3_ffn_b1, L3_ffn_w2, L3_ffn_b2, L3_ffn_gamma, L3_ffn_beta)[0]
    return x

_drawn_inputs = setup_inputs


def setup_inputs(seed=0):
    import zlib

    import numpy as np

    out = dict(_drawn_inputs(seed))
    spreads = {'L0_gnn_b1': (0.0, 0.529),
     'L0_gnn_b2': (0.0, 0.41),
     'L0_gnn_eb': (0.0, 0.1),
     'L0_gnn_eps': (0.0, 0.8),
     'L0_gnn_gamma': (1.0, 0.2),
     'L0_gnn_beta': (0.0, 0.1),
     'L0_ffn_b1': (0.0, 0.598),
     'L0_ffn_b2': (0.0, 0.299),
     'L1_ffn_gate_b': (0.0, 0.1),
     'L1_ffn_b1': (0.0, 0.798),
     'L1_ffn_b2': (0.0, 0.586),
     'L2_gnn_b1': (0.0, 0.8),
     'L2_gnn_b2': (0.0, 0.8),
     'L2_ffn_br': (0.0, 0.1),
     'L2_ffn_ln_g': (1.0, 0.2),
     'L2_ffn_ln_b': (0.0, 0.345),
     'L2_ffn_b1': (0.0, 0.353),
     'L2_ffn_b2': (0.0, 0.1),
     'L3_gnn_b': (0.0, 0.391),
     'L3_ffn_gate_b': (0.0, 0.511),
     'L3_ffn_b1': (0.0, 0.8),
     'L3_ffn_b2': (0.0, 0.46),
     'L3_ffn_gamma': (1.0, 0.2),
     'L3_ffn_beta': (0.0, 0.362)}
    factors = {'L2_gnn_W1': 8.0, 'L2_gnn_W2': 8.0, 'L3_ffn_w1': 3.903, 'L3_ffn_w2': 3.079}
    for name, (base, spread) in spreads.items():
        noise = np.random.default_rng([zlib.crc32(name.encode()), seed]).standard_normal(out[name].shape)
        drawn = base * np.exp(spread * noise) if base else spread * noise
        out[name] = jnp.asarray(drawn.astype(out[name].dtype))
    for name, factor in factors.items():
        out[name] = (out[name] * factor).astype(out[name].dtype)
    return out
```

```python
from contextlib import ExitStack

import concourse.bass as bass
from concourse import mybir

F32 = mybir.dt.float32
I32 = mybir.dt.int32
ALU = mybir.AluOpType
ACT = mybir.ActivationFunctionType
AX = mybir.AxisListType

P = 128
N = 1875
D = 256
T = (N + P - 1) // P
NP = T * P
TAIL = N - (T - 1) * P
E = 31875
EP = 125
EJ = E // EP
EC = 264
assert EP * EJ == E and EC * P >= E + T * (P - 1) and EC % 8 == 0
ED = 32
ROW = 40
C_SRC, C_DST, C_W, C_HROW, C_TYPE = 32, 33, 34, 35, 36
R = 8
HD, DH = 8, 32
U = 8
LN_EPS = 1e-5


class Phase:

    count = 0
    spent = []

    def __init__(self, nc, name):
        Phase.count += 1
        self.nc, self.name, self.stack = nc, f"{name}{Phase.count}", ExitStack()

    def __enter__(self):
        return self

    def __exit__(self, *what):
        self.stack.close()
        if len(Phase.spent) > 90:
            self.nc.clear_and_free_semaphores(Phase.spent)
            self.nc.all_engine_barrier(sem_only=True)
            Phase.spent.clear()

    def sb(self, name, shape, dt=F32):
        return self.stack.enter_context(self.nc.sbuf_tensor(f"{self.name}_{name}", shape, dt))

    def ps(self, name, shape, dt=F32):
        return self.stack.enter_context(self.nc.psum_tensor(f"{self.name}_{name}", shape, dt))

    def sem(self, name):
        Phase.spent.append(self.nc.alloc_semaphore(f"{self.name}_{name}"))
        return Phase.spent[-1]

    def block(self):
        return self.stack.enter_context(self.nc.Block())


class Shared:
    pass


def row(ap):
    return ap.partition_broadcast(P)


def constants(nc, g, x):
    with Phase(nc, "const") as ph:
        tail_zeroed, iota_made, loaded = ph.sem("tail_zeroed"), ph.sem("iota_made"), ph.sem("loaded")
        block = ph.block()

        @block.sync
        def _(sp):
            sp.dma_start(g.X[:, 0:T - 1, :], x[0:(T - 1) * P, :].rearrange("(t p) f -> p t f", p=P)).then_inc(loaded, 16)
            sp.wait_ge(tail_zeroed, 1)
            sp.dma_start(g.X[0:TAIL, T - 1, :], x[(T - 1) * P:N, :]).then_inc(loaded, 16)
            sp.wait_ge(loaded, 32)

        @block.gpsimd
        def _(pool):
            nc.gpsimd.iota(g.iota_free[:, :], [[1, P]], base=0, channel_multiplier=0,
                           allow_small_or_imprecise_dtypes=True).then_inc(iota_made, 1)
            nc.gpsimd.iota(g.iota_part[:, :], [[0, 1]], base=0, channel_multiplier=1,
                           allow_small_or_imprecise_dtypes=True).then_inc(iota_made, 1)

        @block.vector
        def _(v):
            nc.vector.memset(g.X[:, T - 1, :], 0.0).then_inc(tail_zeroed, 1)
            nc.vector.memset(g.ones[:, :], 1.0)
            nc.vector.memset(g.zero_row[:, :], 0.0)
            v.wait_ge(iota_made, 2)
            nc.vector.tensor_scalar(g.ident[:, :], g.iota_free[:, :], g.iota_part[:, 0:1], None, ALU.is_equal)
            nc.vector.tensor_scalar(g.upto[:, :], g.iota_free[:, :], g.iota_part[:, 0:1], None, ALU.is_ge)
            nc.vector.tensor_scalar(g.before[:, :], g.iota_free[:, :], g.iota_part[:, 0:1], None, ALU.is_gt)


def sort_edges(nc, g, src, dst, etype, weight, attr, sorted_rows):
    with Phase(nc, "sort") as ph:
        src_i, dst_i, typ_i = (ph.sb(n, [EP, EJ], I32) for n in ("src_i", "dst_i", "typ_i"))
        wgt = ph.sb("wgt", [EP, EJ])
        stage = ph.sb("stage", [EP, EJ, ROW])
        blank = ph.sb("blank", [P, EC, ROW])
        tile_i, local_i = ph.sb("tile_i", [EP, EJ], I32), ph.sb("local_i", [EP, EJ], I32)
        tile_f = ph.sb("tile_f", [EP, EJ])
        member, rank = ph.sb("member", [EP, T, EJ]), ph.sb("rank", [EP, T, EJ])
        zeros = ph.sb("zeros", [EP, EJ])
        below = ph.sb("below", [EP, T])
        padded_i, padded = ph.sb("padded_i", [P, T], I32), ph.sb("padded", [P, T])
        end, base = ph.sb("end", [P, T]), ph.sb("base", [P, T])
        pos, pos_i = ph.sb("pos", [EP, EJ]), ph.sb("pos_i", [EP, EJ], I32)
        lane_i, chunk_i = ph.sb("lane_i", [EP, EJ], I32), ph.sb("chunk_i", [EP, EJ], I32)
        lane, slot_i = ph.sb("lane", [EP, EJ]), ph.sb("slot_i", [EP, EJ], I32)
        chunk0 = ph.sb("chunk0", [1, EC])
        passed, tile_of = ph.sb("passed", [1, EC, T]), ph.sb("tile_of", [1, EC])
        NB = 5
        out_row, out_slot = ph.sb("out_row", [EP, NB, ROW]), ph.sb("out_slot", [EP, NB], I32)
        p_below, p_total = ph.ps("p_below", [P, T]), ph.ps("p_total", [P, T])
        loaded, blanked, prefilled = ph.sem("loaded"), ph.sem("blanked"), ph.sem("prefilled")
        ranked, counted, placed = ph.sem("ranked"), ph.sem("counted"), ph.sem("placed")
        iota_made, turn = ph.sem("iota_made"), ph.sem("turn")
        row_ready, scattered = ph.sem("row_ready"), [ph.sem(f"scattered{u}") for u in range(NB)]
        block = ph.block()
        edges = "(p j) -> p j"

        @block.sync
        def _(sp):
            for tile, ap in ((dst_i, dst), (src_i, src), (typ_i, etype), (wgt, weight)):
                sp.dma_start(tile[:, :], ap.rearrange(edges, p=EP)).then_inc(loaded, 16)
            sp.dma_start(stage[:, :, 0:ED], attr.rearrange("(p j) c -> p j c", p=EP)).then_inc(loaded, 16)
            sp.wait_ge(blanked, 2)
            sp.dma_start(sorted_rows.rearrange("(p c) w -> p c w", p=P), blank[:, :, :]).then_inc(prefilled, 16)
            sp.wait_ge(prefilled, 16)

        @block.tensor
        def _(pe):
            pe.wait_ge(ranked, 1)
            nc.tensor.matmul(p_below[:, :], g.before[0:EP, :], rank[:, :, EJ - 1], start=True, stop=True)
            nc.tensor.matmul(p_total[:, :], g.ones[0:EP, :], rank[:, :, EJ - 1], start=True, stop=True).then_inc(counted, 1)

        @block.gpsimd
        def _(pool):
            nc.gpsimd.iota(chunk0[:, :], [[P, EC]], base=0, channel_multiplier=0,
                           allow_small_or_imprecise_dtypes=True).then_inc(iota_made, 1)
            nc.gpsimd.memset(blank[:, :, :], 0.0).then_inc(blanked, 1)
            pool.wait_ge(blanked, 1)
            nc.gpsimd.memset(blank[:, :, C_DST:C_DST + 1], -1.0).then_inc(blanked, 1)
            pool.wait_ge(prefilled, 16)
            with pool.Fori(0, EJ // NB) as i:
                for u in range(NB):
                    pool.wait_ge(row_ready, i * NB + u + 1)
                    pool.sem_inc(turn, 1)
                    pool.indirect_dma_start(sorted_rows, bass.IndirectOffsetOnAxis(ap=out_slot[:, u:u + 1], axis=0),
                                            out_row[:, u, :], None).then_inc(scattered[u], 16)
            for u in range(NB):
                pool.wait_ge(scattered[u], 16 * (EJ // NB))

        @block.vector
        def _(v):
            nc.vector.memset(zeros[:, :], 0.0)
            v.wait_ge(loaded, 80)
            nc.vector.tensor_scalar(tile_i[:, :], dst_i[:, :], 7, None, ALU.arith_shift_right)
            nc.vector.tensor_scalar(local_i[:, :], dst_i[:, :], P - 1, None, ALU.bitwise_and)
            v.drain()
            nc.vector.tensor_copy(tile_f[:, :], tile_i[:, :])
            nc.vector.tensor_copy(stage[:, :, C_DST], local_i[:, :])
            nc.vector.tensor_copy(stage[:, :, C_TYPE], typ_i[:, :])
            nc.vector.tensor_copy(stage[:, :, C_W], wgt[:, :])
            nc.vector.tensor_copy(stage[:, :, C_SRC].bitcast(I32), src_i[:, :])
            v.drain()
            nc.vector.scalar_tensor_tensor(stage[:, :, C_HROW].bitcast(I32), stage[:, :, C_TYPE], float(NP), src_i[:, :],
                                           ALU.mult, ALU.add)
            nc.vector.memset(stage[:, :, C_TYPE + 1:ROW], 0.0)
            for t in range(T):
                nc.vector.tensor_scalar(member[:, t, :], tile_f[:, :], float(t), None, ALU.is_equal)
            v.drain()
            for t in range(T):
                nc.vector.tensor_tensor_scan(rank[:, t, :], member[:, t, :], zeros[:, :], 0.0, ALU.add, ALU.add)
            v.drain()
            v.sem_inc(ranked, 1)
            v.wait_ge(counted, 1)
            nc.vector.tensor_scalar(padded_i[:, :], p_total[:, :], float(P - 1), None, ALU.add)
            v.drain()
            nc.vector.tensor_scalar(padded_i[:, :], padded_i[:, :], 7, 7, ALU.arith_shift_right, ALU.arith_shift_left)
            v.drain()
            nc.vector.tensor_copy(padded[:, :], padded_i[:, :])
            v.drain()
            nc.vector.tensor_tensor_scan(end[:, :], padded[:, :], g.zero_row[:, 0:T], 0.0, ALU.add, ALU.add)
            v.drain()
            nc.vector.tensor_tensor(base[:, :], end[:, :], padded[:, :], ALU.subtract)
            v.drain()
            nc.vector.scalar_tensor_tensor(below[:, :], p_below[0:EP, :], -1.0, base[0:EP, :], ALU.add, ALU.add)
            v.drain()
            for t in range(T):
                nc.vector.scalar_tensor_tensor(member[:, t, :], rank[:, t, :], below[:, t:t + 1], member[:, t, :],
                                               ALU.add, ALU.mult)
            v.drain()
            nc.vector.tensor_reduce(pos[:, :], member[:, :, :].rearrange("p t j -> p j t"), AX.X, ALU.add)
            v.drain()
            nc.vector.tensor_copy(pos_i[:, :], pos[:, :])
            v.drain()
            nc.vector.tensor_scalar(chunk_i[:, :], pos_i[:, :], 7, None, ALU.arith_shift_right)
            nc.vector.tensor_scalar(lane_i[:, :], pos_i[:, :], P - 1, None, ALU.bitwise_and)
            v.drain()
            nc.vector.tensor_copy(lane[:, :], lane_i[:, :])
            v.drain()
            nc.vector.scalar_tensor_tensor(slot_i[:, :], lane[:, :], float(EC), chunk_i[:, :], ALU.mult, ALU.add)
            v.wait_ge(iota_made, 1)
            nc.vector.tensor_tensor(passed[:, :, :], chunk0[:, :].unsqueeze(2).to_broadcast([1, EC, T]),
                                    end[0:1, :].unsqueeze(1).to_broadcast([1, EC, T]), ALU.is_ge)
            v.drain()
            nc.vector.tensor_reduce(tile_of[:, :], passed[:, :, :], AX.X, ALU.add)
            v.drain()
            nc.vector.tensor_scalar(g.chunk_tile[:, :], tile_of[:, :], float(T - 1), None, ALU.min)
            def fill(i):
                for u in range(NB):
                    if not isinstance(i, int):
                        v.wait_ge(scattered[u], i * 16)
                    nc.vector.tensor_copy(out_row[:, u, :], stage[:, bass.ds(i * NB + u, 1), :].rearrange("p a w -> p (a w)"))
                    nc.vector.tensor_copy(out_slot[:, u:u + 1], slot_i[:, bass.ds(i * NB + u, 1)])
                    v.drain()
                    v.sem_inc(row_ready, 1)

            v.drain()
            fill(0)
            with v.Fori(1, EJ // NB) as i:
                fill(i)


def load_sorted(nc, g, sorted_rows):
    with Phase(nc, "unpack") as ph:
        rows = ph.sb("rows", [P, EC, ROW])
        attrs = ph.sb("attrs", [P, EC, ED])
        p_turned = [ph.ps(f"p_turned{b}", [P, 4, P]) for b in range(4)]
        loaded, packed, turned, stored = ph.sem("loaded"), ph.sem("packed"), ph.sem("turned"), ph.sem("stored")
        block = ph.block()
        groups = EC // 4
        batches = [range(b, min(b + 4, groups)) for b in range(0, groups, 4)]

        @block.sync
        def _(sp):
            sp.dma_start(rows[:, :, :], sorted_rows.rearrange("(p c) w -> p c w", p=P)).then_inc(loaded, 16)

        @block.vector
        def _(v):
            v.wait_ge(loaded, 16)
            nc.vector.tensor_copy(attrs[:, :, :], rows[:, :, 0:ED]).then_inc(packed, 1)
            nc.vector.tensor_copy(g.src[:, :], rows[:, :, C_SRC].bitcast(I32))
            nc.vector.tensor_copy(g.hrow[:, :], rows[:, :, C_HROW].bitcast(I32))
            nc.vector.tensor_copy(g.dst[:, :], rows[:, :, C_DST])
            nc.vector.tensor_copy(g.weight[:, :], rows[:, :, C_W])
            nc.vector.tensor_copy(g.etype[:, :], rows[:, :, C_TYPE])

        @block.tensor
        def _(pe):
            pe.wait_ge(packed, 1)
            for b, batch in enumerate(batches):
                if b >= 4:
                    pe.wait_ge(stored, b - 3)
                for k, q in enumerate(batch):
                    ins = nc.tensor.transpose(p_turned[b % 4][:, k, :], attrs[:, 4 * q:4 * q + 4, :].rearrange("p c w -> p (c w)"),
                                              g.ident[:, :])
                ins.then_inc(turned, 1)

        @block.scalar
        def _(act):
            for b, batch in enumerate(batches):
                act.wait_ge(turned, b + 1)
                nc.scalar.copy(g.attrs_t[:, batch[0]:batch[-1] + 1, :], p_turned[b % 4][:, 0:len(batch), :]).then_inc(stored, 1)


def layernorm(nc, h, y, gamma=None, beta=None, relu=False, add=None, table=None, addrow=None):
    with Phase(nc, "ln") as ph:
        stats, mv = ph.sb("stats", [P, T, 6]), ph.sb("mv", [P, T, 2])
        var, std, rstd = ph.sb("var", [P, T]), ph.sb("std", [P, T]), ph.sb("rstd", [P, T])
        vec = ph.sb("vec", [P, 3, D])
        rows = ph.sb("rows", [P, T, D]) if addrow is not None else y
        loaded, var_ready, std_ready = ph.sem("loaded"), ph.sem("var_ready"), ph.sem("std_ready")
        rows_ready, written = ph.sem("rows_ready"), ph.sem("written")
        block = ph.block()
        wide = [P, T, D]
        given = [(i, a) for i, a in enumerate((gamma, beta, addrow)) if a is not None]

        @block.sync
        def _(sp):
            for i, a in given:
                sp.dma_start(vec[:, i, :], row(a)).then_inc(loaded, 16)
            if table is not None:
                sp.wait_ge(rows_ready, 1)
                sp.dma_start(table.rearrange("(t p) f -> p t f", p=P), rows[:, :, :]).then_inc(written, 16)
                sp.wait_ge(written, 16)

        @block.scalar
        def _(act):
            act.wait_ge(var_ready, 1)
            nc.scalar.activation(std[:, :], var[:, :], ACT.Sqrt).then_inc(std_ready, 1)

        @block.vector
        def _(v):
            for t in range(T):
                nc.vector.bn_stats(stats[:, t, :], h[:, t, :])
            v.drain()
            for t in range(T):
                nc.vector.bn_aggr(mv[:, t, :], stats[:, t, :])
            v.drain()
            nc.vector.tensor_scalar(var[:, :], mv[:, :, 1], LN_EPS, None, ALU.add).then_inc(var_ready, 1)
            v.wait_ge(std_ready, 1)
            nc.vector.reciprocal(rstd[:, :], std[:, :])
            v.drain()
            for t in range(T):
                nc.vector.tensor_scalar(y[:, t, :], h[:, t, :], mv[:, t, 0:1], rstd[:, t:t + 1], ALU.subtract, ALU.mult)
            if given:
                v.wait_ge(loaded, 16 * len(given))
            if gamma is not None:
                v.drain()
                nc.vector.tensor_tensor(y[:, :, :], y[:, :, :], vec[:, 0, :].unsqueeze(1).to_broadcast(wide), ALU.mult)
                v.drain()
                nc.vector.tensor_tensor(y[:, :, :], y[:, :, :], vec[:, 1, :].unsqueeze(1).to_broadcast(wide), ALU.add)
            if relu:
                v.drain()
                nc.vector.tensor_scalar(y[:, :, :], y[:, :, :], 0.0, None, ALU.max)
            v.drain()
            if addrow is not None:
                nc.vector.tensor_tensor(rows[:, :, :], y[:, :, :], vec[:, 2, :].unsqueeze(1).to_broadcast(wide), ALU.add)
                v.drain()
            v.sem_inc(rows_ready, 1)
            if add is not None:
                nc.vector.tensor_tensor(add[:, :, :], add[:, :, :], y[:, :, :], ALU.add)


def self_terms(nc, g, y, acc, eps=None):
    with Phase(nc, "self") as ph:
        scale, scaled = ph.sb("scale", [P, 1]), ph.sb("scaled", [P, P])
        banks = (T + 1) // 2
        p_turned = ph.ps("p_turned", [P, banks, 2, 2, P])
        loaded, scaled_ready, turned = ph.sem("loaded"), ph.sem("scaled_ready"), ph.sem("turned")
        block = ph.block()

        @block.sync
        def _(sp):
            if eps is not None:
                sp.dma_start(scale[:, :], row(eps)).then_inc(loaded, 16)

        @block.vector
        def _(v):
            if eps is not None:
                v.wait_ge(loaded, 16)
                nc.vector.tensor_scalar(scale[:, :], scale[:, :], 1.0, None, ALU.add)
                v.drain()
                nc.vector.tensor_scalar(scaled[:, :], g.ident[:, :], scale[:, 0:1], None, ALU.mult).then_inc(scaled_ready, 1)
            for b in range(1, banks, 2):
                v.wait_ge(turned, b + 1)
                n = min(2, T - 2 * b)
                nc.vector.tensor_copy(acc[:, 2 * b:2 * b + n, :, :], p_turned[:, b, 0:n, :, :])

        @block.scalar
        def _(act):
            for b in range(0, banks, 2):
                act.wait_ge(turned, b + 1)
                n = min(2, T - 2 * b)
                nc.scalar.copy(acc[:, 2 * b:2 * b + n, :, :], p_turned[:, b, 0:n, :, :])

        @block.tensor
        def _(pe):
            if eps is not None:
                pe.wait_ge(scaled_ready, 1)
            diag = g.ident if eps is None else scaled
            for t in range(T):
                for half in range(2):
                    ins = nc.tensor.matmul(p_turned[:, t // 2, t % 2, half, :], y[:, t, half * P:(half + 1) * P], diag[:, :],
                                           start=True, stop=True)
                if t % 2 or t == T - 1:
                    ins.then_inc(turned, 1)


def gine_edges(nc, g, table, edge_w, acc):
    with Phase(nc, "gine") as ph:
        ew = ph.sb("ew", [P, D])
        quad = ph.sb("quad", [P, 2, P])
        idx = ph.sb("idx", [P, U], I32)
        got = ph.sb("got", [P, U, D])
        hot = ph.sb("hot", [P, U, P])
        msg = ph.sb("msg", [P, U, D])
        p_edge = [ph.ps(f"p_edge{b}", [P, 512]) for b in range(4)]
        p_sum = [ph.ps(f"p_sum{b}", [P, 512]) for b in range(4)]
        loaded, idx_ready, quad_ready, turn = ph.sem("loaded"), ph.sem("idx_ready"), ph.sem("quad_ready"), ph.sem("turn")
        gathered = [ph.sem(f"gathered{u}") for u in range(U)]
        edge_done, summed, msg_ready, hot_ready = ph.sem("edge_done"), ph.sem("summed"), ph.sem("msg_ready"), ph.sem("hot_ready")
        agg_done, added = ph.sem("agg_done"), ph.sem("added")
        block = ph.block()

        @block.sync
        def _(sp):
            for q in range(4):
                sp.dma_start(ew[q * ED:(q + 1) * ED, :], edge_w).then_inc(loaded, 16)
            sp.sem_inc(summed, U)
            sp.sem_inc(agg_done, U)
            sp.sem_inc(added, U)
            sp.sem_inc(msg_ready, U)
            sp.wait_ge(loaded, 64)

        @block.gpsimd
        def _(pool):
            with pool.Fori(0, EC // U) as i:
                for u in range(U):
                    pool.wait_ge(msg_ready, i * U + (u + 1))
                    pool.sem_inc(turn, 1)
                    pool.wait_ge(idx_ready, i * U + (u + 1))
                    pool.sem_inc(turn, 1)
                    pool.indirect_dma_start(got[:, u, :], None, table,
                                            bass.IndirectOffsetOnAxis(ap=idx[:, u:u + 1], axis=0)).then_inc(gathered[u], 16)

        @block.tensor
        def _(pe):
            pe.wait_ge(loaded, 64)

            def edge(i, u):
                if u % 4 == 0:
                    pe.wait_ge(quad_ready, i * 2 + (u // 4 + 1))
                pe.wait_ge(summed, i * U + (u - 4 + 1 + U))
                q = u % 4
                nc.tensor.matmul(p_edge[u % 4][:, 0:D], quad[q * ED:(q + 1) * ED, u // 4, :], ew[q * ED:(q + 1) * ED, :],
                                 start=True, stop=True).then_inc(edge_done, 1)

            def aggregate(i, u):
                pe.wait_ge(hot_ready, i * U + (u + 1))
                pe.wait_ge(added, i * U + (u - 4 + 1 + U))
                pe.wait_ge(msg_ready, i * U + (u + 1 + U))
                for half in range(2):
                    ins = nc.tensor.matmul(p_sum[u % 4][:, half * P:(half + 1) * P], msg[:, u, half * P:(half + 1) * P],
                                           hot[:, u, :], start=True, stop=True)
                ins.then_inc(agg_done, 1)

            with pe.Fori(0, EC // U) as i:
                edge(i, 0)
                edge(i, 1)
                for u in range(U):
                    if u + 2 < U:
                        edge(i, u + 2)
                    aggregate(i, u)

        @block.scalar
        def _(act):
            with act.Fori(0, EC // U) as i:
                for u in range(U):
                    act.wait_ge(summed, i * U + (u + 1))
                    act.sem_inc(turn, 1)
                    if u % 4 == 0:
                        act.wait_ge(summed, i * U + (u + 4))
                        act.sem_inc(turn, 1)
                        nc.scalar.copy(quad[:, u // 4, :], g.attrs_t[:, bass.ds(i * 2 + u // 4, 1), :].rearrange("p a e -> p (a e)")).then_inc(quad_ready, 1)
                    nc.scalar.copy(idx[:, u:u + 1], g.src[:, bass.ds(i * U + u, 1)]).then_inc(idx_ready, 1)
                for u in range(U):
                    act.wait_ge(agg_done, i * U + (u + 1))
                    act.wait_ge(summed, i * U + (u + 1 + U))
                    nc.scalar.activation(msg[:, u, :], got[:, u, :], ACT.Relu).then_inc(msg_ready, 1)

        @block.vector
        def _(v):
            tile = [v.alloc_register(f"{ph.name}_tile{u}") for u in range(U)]

            def add(i, u, t):
                v.wait_ge(agg_done, i * U + (u + 1 + U))
                a = acc[:, bass.ds(t, 1), :, :].rearrange("p a h n -> p (a h n)")
                nc.vector.tensor_tensor(a, a, p_sum[u % 4][:, 0:D], ALU.add).then_inc(added, 1)

            with v.Fori(0, EC // U) as i:
                v.load(tile, g.chunk_tile[0:1, bass.ds(i * U, U)])
                tiles = [v.snap(r, min_val=0, max_val=T - 1) for r in tile]
                for u in range(U):
                    v.wait_ge(agg_done, i * U + (u + 1))
                    nc.vector.tensor_scalar(hot[:, u, :], g.iota_free[:, :], g.dst[:, bass.ds(i * U + u, 1)], None,
                                            ALU.is_equal).then_inc(hot_ready, 1)
                for u in range(U):
                    v.wait_ge(edge_done, i * U + (u + 1))
                    v.wait_ge(gathered[u], i * 16 + 16)
                    nc.vector.tensor_tensor(got[:, u, :], got[:, u, :], p_edge[u % 4][:, 0:D], ALU.add).then_inc(summed, 1)
                    if u >= 3:
                        v.drain()
                        add(i, u - 3, tiles[u - 3])
                for u in range(U - 3, U):
                    v.drain()
                    add(i, u, tiles[u])
                v.drain()


def gine_mlp(nc, g, agg, h, w1, b1, w2, b2, first):
    with Phase(nc, "mlp") as ph:
        w1_sb, w2_sb = ph.sb("w1", [P, 2, D]), ph.sb("w2", [P, 2, D])
        b1_sb, b2_row = ph.sb("b1", [P, 2]), ph.sb("b2", [P, D])
        z = ph.sb("z", [P, 2, T, P])
        p_z = [ph.ps(f"p_z{b}", [P, 4, P]) for b in range(4)]
        p_h = [ph.ps(f"p_h{b}", [P, 512]) for b in range(4)]
        loaded, z_done, z_ready, h_done, h_added = (ph.sem(s) for s in ("loaded", "z_done", "z_ready", "h_done", "h_added"))
        block = ph.block()
        groups = [(t, min(4, T - t)) for t in range(0, T, 4)]
        steps = [(t, k, m) for t, k in groups for m in range(2)]

        @block.sync
        def _(sp):
            sp.dma_start(w1_sb[:, :, :], w1.rearrange("(k p) n -> p k n", p=P)).then_inc(loaded, 16)
            sp.dma_start(w2_sb[:, :, :], w2.rearrange("(k p) n -> p k n", p=P)).then_inc(loaded, 16)
            sp.dma_start(b1_sb[:, :], b1).then_inc(loaded, 16)
            sp.dma_start(b2_row[:, :], row(b2)).then_inc(loaded, 16)

        @block.tensor
        def _(pe):
            pe.wait_ge(loaded, 64)
            for s, (t, n, m) in enumerate(steps):
                if s >= 4:
                    pe.wait_ge(z_ready, s - 3)
                for k in range(2):
                    ins = nc.tensor.matmul(p_z[s % 4][:, 0:n, :], w1_sb[:, k, m * P:(m + 1) * P], agg[:, t:t + n, k, :],
                                           start=(k == 0), stop=(k == 1))
                ins.then_inc(z_done, 1)
            for t in range(T):
                pe.wait_ge(z_ready, 2 * (t // 4 + 1))
                if t >= 4:
                    pe.wait_ge(h_added, t - 3)
                for k in range(2):
                    ins = nc.tensor.matmul(p_h[t % 4][:, 0:D], z[:, k, t, :], w2_sb[:, k, :], start=(k == 0), stop=(k == 1))
                ins.then_inc(h_done, 1)

        @block.scalar
        def _(act):
            act.wait_ge(loaded, 64)
            for s, (t, n, m) in enumerate(steps):
                act.wait_ge(z_done, s + 1)
                nc.scalar.activation(z[:, m, t:t + n, :], p_z[s % 4][:, 0:n, :], ACT.Relu, bias=b1_sb[:, m:m + 1]).then_inc(z_ready, 1)

        @block.vector
        def _(v):
            v.wait_ge(loaded, 64)
            if not first:
                nc.vector.tensor_tensor(h[:, :, :], h[:, :, :], b2_row[:, :].unsqueeze(1).to_broadcast([P, T, D]), ALU.add)
                v.drain()
            for t in range(T):
                v.wait_ge(h_done, t + 1)
                nc.vector.tensor_tensor(h[:, t, :], p_h[t % 4][:, 0:D], b2_row[:, :] if first else h[:, t, :],
                                        ALU.add).then_inc(h_added, 1)


def store(nc, x, out):
    with Phase(nc, "store") as ph:
        written = ph.sem("written")
        block = ph.block()

        @block.sync
        def _(sp):
            sp.dma_start(out[0:(T - 1) * P, :].rearrange("(t p) f -> p t f", p=P), x[:, 0:T - 1, :]).then_inc(written, 16)
            sp.dma_start(out[(T - 1) * P:N, :], x[0:TAIL, T - 1, :]).then_inc(written, 16)
            sp.wait_ge(written, 32)


def gine_stack(nc, g, i):
    with Phase(nc, "stack") as ph:
        h, y, acc = ph.sb("h", [P, T, D]), ph.sb("y", [P, T, D]), ph.sb("acc", [P, T, 2, P])
        L = i["L0_gnn_W1"].shape[0]
        for k in range(L):
            table = g.dram(f"gine_table{k}", [NP, D])
            if k == 0:
                layernorm(nc, g.X, y, table=table, addrow=i["L0_gnn_eb"][k, :])
            else:
                layernorm(nc, h, y, gamma=i["L0_gnn_gamma"][k, :], beta=i["L0_gnn_beta"][k, :], relu=True,
                          table=table, addrow=i["L0_gnn_eb"][k, :])
            self_terms(nc, g, y, acc, eps=i["L0_gnn_eps"][k:k + 1])
            gine_edges(nc, g, table, i["L0_gnn_eW"][k, :, :], acc)
            gine_mlp(nc, g, acc, h, i["L0_gnn_W1"][k, :, :], i["L0_gnn_b1"][k, :, :], i["L0_gnn_W2"][k, :, :],
                     i["L0_gnn_b2"][k, :], first=(k == 0))
        layernorm(nc, h, y, gamma=i["L0_gnn_gamma"][0, :], beta=i["L0_gnn_beta"][0, :], relu=True, add=g.X)


class Routes:

    def __init__(self, ph, k, blocks):
        self.slot, self.gate = ph.sb("slot", [P, k, T], I32), ph.sb("gate", [P, k, T])
        self.expert = ph.sb("expert", [1, blocks], I32)
        self.blocks, self.choices = blocks, k


def rank_tokens(nc, g, xn, wr, br, chosen, r):
    weights = g.dram("router_weights", [NP])
    last = r.blocks * P - 1
    with Phase(nc, "rank") as ph:
        prod, wr_row, br_col = ph.sb("prod", [P, T, D]), ph.sb("wr", [P, D]), ph.sb("br", [P, 1])
        w, turned, every = ph.sb("w", [P, T]), ph.sb("turned", [P, P]), ph.sb("every", [P, NP])
        junk, valid, gone = ph.sb("junk", [P, NP]), ph.sb("valid", [P, 1]), ph.sb("gone", [P, 1])
        lower, over, above, ties = ph.sb("lower", [P, P]), ph.sb("over", [P, T]), ph.sb("above", [P, T]), ph.sb("ties", [P, T])
        rank = ph.sb("rank", [P, T])
        p_turned = ph.ps("p_turned", [T, P])
        loaded, w_ready, w_turned, w_copied = (ph.sem(s) for s in ("loaded", "w_ready", "w_turned", "w_copied"))
        w_written, w_spread = ph.sem("w_written"), ph.sem("w_spread")
        block = ph.block()

        @block.sync
        def _(sp):
            sp.dma_start(wr_row[:, :], row(wr)).then_inc(loaded, 16)
            sp.dma_start(br_col[:, :], row(br)).then_inc(loaded, 16)
            sp.wait_ge(w_copied, 1)
            sp.dma_start(weights.rearrange("(t p) -> t p", p=P), turned[0:T, :]).then_inc(w_written, 16)
            sp.wait_ge(w_written, 16)
            sp.dma_start(every[:, :], row(weights)).then_inc(w_spread, 16)

        @block.tensor
        def _(pe):
            pe.wait_ge(w_ready, 1)
            nc.tensor.transpose(p_turned[:, :], w[:, :], g.ident[:, :]).then_inc(w_turned, 1)

        @block.vector
        def _(v):
            nc.vector.tensor_scalar(lower[:, :], g.iota_free[:, :], g.iota_part[:, 0:1], None, ALU.is_lt)
            nc.vector.tensor_scalar(valid[:, :], g.iota_part[:, :], float(TAIL), None, ALU.is_lt)
            nc.vector.tensor_scalar(gone[:, :], g.iota_part[:, :], float(TAIL), -3e38, ALU.is_ge, ALU.mult)
            v.wait_ge(loaded, 32)
            nc.vector.tensor_tensor(prod[:, :, :], xn[:, :, :], wr_row[:, :].unsqueeze(1).to_broadcast([P, T, D]), ALU.mult)
            v.drain()
            nc.vector.tensor_reduce(w[:, :], prod[:, :, :], AX.X, ALU.add)
            v.drain()
            nc.vector.tensor_scalar(w[:, :], w[:, :], br_col[:, 0:1], None, ALU.add)
            v.drain()
            nc.vector.tensor_scalar(w[:, T - 1:T], w[:, T - 1:T], valid[:, 0:1], gone[:, 0:1], ALU.mult, ALU.add).then_inc(w_ready, 1)
            v.wait_ge(w_turned, 1)
            nc.vector.tensor_copy(turned[0:T, :], p_turned[:, :]).then_inc(w_copied, 1)
            v.wait_ge(w_spread, 16)
            nc.vector.memset(over[:, 0:1], 0.0)
            for t in range(T):
                if t:
                    nc.vector.tensor_scalar(junk[:, 0:t * P], every[:, 0:t * P], w[:, t:t + 1], 0.0, ALU.is_ge, ALU.add,
                                            accum_out=over[:, t:t + 1])
                nc.vector.tensor_scalar(junk[:, t * P:NP], every[:, t * P:NP], w[:, t:t + 1], 0.0, ALU.is_gt, ALU.add,
                                        accum_out=above[:, t:t + 1])
                v.drain()
                nc.vector.scalar_tensor_tensor(junk[:, 0:P], every[:, t * P:(t + 1) * P], w[:, t:t + 1], lower[:, :],
                                               ALU.is_equal, ALU.mult, accum_out=ties[:, t:t + 1])
                v.drain()
            nc.vector.tensor_tensor(rank[:, :], over[:, :], above[:, :], ALU.add)
            v.drain()
            nc.vector.tensor_tensor(rank[:, :], rank[:, :], ties[:, :], ALU.add)
            v.drain()
            nc.vector.tensor_copy(r.slot[:, 0, :], rank[:, :])
            nc.vector.tensor_scalar(r.source[:, :], rank[:, :], float(last), None, ALU.min)
            nc.vector.scalar_tensor_tensor(r.gate[:, 0, :], rank[:, :], float(chosen), w[:, :], ALU.is_lt, ALU.mult)


def choose_experts(nc, g, xt, gate_w, gate_b, r, capacity=None):
    ne, k_all, nb = gate_w.shape[1], r.choices, r.blocks
    with Phase(nc, "route") as ph:
        gw, gb = ph.sb("gw", [P, 2, ne]), ph.sb("gb", [P, ne])
        lg, eq, e_idx = ph.sb("lg", [P, T, ne]), ph.sb("eq", [P, T, ne]), ph.sb("e_idx", [P, ne])
        top, first = ph.sb("top", [P, k_all, T]), ph.sb("first", [P, T])
        hot = ph.sb("hot", [P, k_all, T, ne])
        ex, total = ph.sb("ex", [P, T, ne]), ph.sb("total", [P, T])
        count = [ph.sb(f"count{b}", [P, k_all * T, ne]) for b in range(2)]
        before, place = ph.sb("before", [P, k_all * T, ne]), ph.sb("place", [P, k_all * T, ne])
        padded_i, padded, end, base = ph.sb("padded_i", [P, ne], I32), ph.sb("padded", [P, ne]), ph.sb("end", [P, ne]), ph.sb("base", [P, ne])
        slot, pos = ph.sb("slot_f", [P, k_all * T]), ph.sb("pos", [P, k_all * T])
        block0, passed, owner = ph.sb("block0", [1, nb]), ph.sb("passed", [1, nb, ne]), ph.sb("owner", [1, nb])
        p_lg = ph.ps("p_lg", [P, T, ne])
        p_in, p_all = ph.ps("p_in", [P, k_all * T, ne]), ph.ps("p_all", [P, k_all * T, ne])
        loaded, iota_made, lg_done, ex_in, ex_done = (ph.sem(s) for s in ("loaded", "iota_made", "lg_done", "ex_in", "ex_done"))
        hot_ready, counted = ph.sem("hot_ready"), ph.sem("counted")
        block = ph.block()
        big = 1000.0
        wide = [P, T, ne]

        @block.sync
        def _(sp):
            sp.dma_start(gw[:, :, :], gate_w.rearrange("(k p) e -> p k e", p=P)).then_inc(loaded, 16)
            sp.dma_start(gb[:, :], row(gate_b)).then_inc(loaded, 16)

        @block.gpsimd
        def _(pool):
            nc.gpsimd.iota(e_idx[:, :], [[1, ne]], base=0, channel_multiplier=0,
                           allow_small_or_imprecise_dtypes=True).then_inc(iota_made, 1)
            nc.gpsimd.iota(block0[:, :], [[P, nb]], base=0, channel_multiplier=0,
                           allow_small_or_imprecise_dtypes=True).then_inc(iota_made, 1)

        @block.tensor
        def _(pe):
            pe.wait_ge(loaded, 32)
            for t in range(T):
                for k in range(2):
                    ins = nc.tensor.matmul(p_lg[:, t, :], xt[:, t, k, :], gw[:, k, :], start=(k == 0), stop=(k == 1))
            ins.then_inc(lg_done, 1)
            pe.wait_ge(hot_ready, 1)
            flat = hot[:, :, :, :].rearrange("p k t e -> p (k t e)")
            nc.tensor.matmul(p_in[:, :, :].rearrange("p a e -> p (a e)"), g.upto[:, :], flat, start=True, stop=True)
            nc.tensor.matmul(p_all[:, :, :].rearrange("p a e -> p (a e)"), g.ones[:, :], flat, start=True, stop=True).then_inc(counted, 1)

        @block.scalar
        def _(act):
            act.wait_ge(ex_in, 1)
            if k_all == 1:
                nc.scalar.activation(ex[:, :, :], ex[:, :, :], ACT.Exp).then_inc(ex_done, 1)
            else:
                nc.scalar.activation(total[:, :], total[:, :], ACT.Exp).then_inc(ex_done, 1)

        @block.vector
        def _(v):
            v.wait_ge(loaded, 32)
            v.wait_ge(lg_done, 1)
            nc.vector.tensor_tensor(lg[:, :, :], p_lg[:, :, :], gb[:, :].unsqueeze(1).to_broadcast(wide), ALU.add)
            v.wait_ge(iota_made, 2)
            nc.vector.tensor_scalar(e_idx[:, :], e_idx[:, :], -big, None, ALU.add)
            v.drain()
            for k in range(k_all):
                nc.vector.tensor_reduce(top[:, k, :], lg[:, :, :], AX.X, ALU.max)
                v.drain()
                if k_all == 1:
                    nc.vector.tensor_tensor(ex[:, :, :], lg[:, :, :], top[:, k, :].unsqueeze(2).to_broadcast(wide),
                                            ALU.subtract)
                nc.vector.tensor_tensor(eq[:, :, :], lg[:, :, :], top[:, k, :].unsqueeze(2).to_broadcast(wide), ALU.not_equal)
                v.drain()
                nc.vector.scalar_tensor_tensor(eq[:, :, :], eq[:, :, :], big, e_idx[:, :].unsqueeze(1).to_broadcast(wide),
                                               ALU.mult, ALU.add)
                v.drain()
                nc.vector.tensor_reduce(first[:, :], eq[:, :, :], AX.X, ALU.min)
                v.drain()
                nc.vector.tensor_tensor(hot[:, k, :, :], e_idx[:, :].unsqueeze(1).to_broadcast(wide),
                                        first[:, :].unsqueeze(2).to_broadcast(wide), ALU.is_equal)
                v.drain()
                if k + 1 < k_all:
                    nc.vector.scalar_tensor_tensor(lg[:, :, :], hot[:, k, :, :], -1e30, lg[:, :, :], ALU.mult, ALU.add)
                    v.drain()
            if k_all == 2:
                nc.vector.tensor_tensor(total[:, :], top[:, 1, :], top[:, 0, :], ALU.subtract)
                v.drain()
            v.sem_inc(ex_in, 1)
            v.sem_inc(hot_ready, 1)
            v.wait_ge(ex_done, 1)
            if k_all == 1:
                nc.vector.tensor_reduce(total[:, :], ex[:, :, :], AX.X, ALU.add)
                v.drain()
                nc.vector.reciprocal(r.gate[:, 0, :], total[:, :])
            else:
                nc.vector.tensor_scalar(first[:, :], total[:, :], 1.0, None, ALU.add)
                v.drain()
                nc.vector.reciprocal(r.gate[:, 0, :], first[:, :])
                v.drain()
                nc.vector.tensor_tensor(r.gate[:, 1, :], total[:, :], r.gate[:, 0, :], ALU.mult)
            v.wait_ge(counted, 1)
            kt = k_all * T
            nc.vector.tensor_copy(count[0][:, :, :], p_all[:, :, :])
            v.drain()
            s, a = 1, 0
            while s < kt:
                nc.vector.tensor_tensor(count[1 - a][:, s:kt, :], count[a][:, s:kt, :], count[a][:, 0:kt - s, :], ALU.add)
                nc.vector.tensor_copy(count[1 - a][:, 0:s, :], count[a][:, 0:s, :])
                v.drain()
                s, a = 2 * s, 1 - a
            nc.vector.tensor_tensor(before[:, :, :], count[a][:, :, :], p_all[:, :, :], ALU.subtract)
            nc.vector.tensor_scalar(padded_i[:, :], count[a][:, kt - 1, :], float(P - 1), None, ALU.add)
            v.drain()
            nc.vector.tensor_scalar(padded_i[:, :], padded_i[:, :], 7, 7, ALU.arith_shift_right, ALU.arith_shift_left)
            v.drain()
            nc.vector.tensor_copy(padded[:, :], padded_i[:, :])
            v.drain()
            nc.vector.tensor_tensor_scan(end[:, :], padded[:, :], g.zero_row[:, 0:ne], 0.0, ALU.add, ALU.add)
            nc.vector.scalar_tensor_tensor(place[:, :, :], p_in[:, :, :], -1.0, before[:, :, :], ALU.add, ALU.add)
            v.drain()
            nc.vector.tensor_tensor(base[:, :], end[:, :], padded[:, :], ALU.subtract)
            if capacity is not None:
                nc.vector.tensor_tensor(eq[:, :, :], place[:, :, :], hot[:, 0, :, :], ALU.mult)
                v.drain()
                nc.vector.tensor_reduce(pos[:, :], eq[:, :, :], AX.X, ALU.add)
                v.drain()
                nc.vector.scalar_tensor_tensor(r.gate[:, 0, :], pos[:, :], float(capacity), r.gate[:, 0, :], ALU.is_lt, ALU.mult)
            v.drain()
            nc.vector.tensor_tensor(place[:, :, :], place[:, :, :], base[:, :].unsqueeze(1).to_broadcast([P, kt, ne]), ALU.add)
            v.drain()
            nc.vector.tensor_tensor(place[:, :, :], place[:, :, :], hot[:, :, :, :].rearrange("p k t e -> p (k t) e"), ALU.mult)
            v.drain()
            nc.vector.tensor_reduce(slot[:, :], place[:, :, :], AX.X, ALU.add)
            v.drain()
            nc.vector.tensor_copy(r.slot[:, :, :].rearrange("p k t -> p (k t)"), slot[:, :])
            nc.vector.tensor_tensor(passed[:, :, :], block0[:, :].unsqueeze(2).to_broadcast([1, nb, ne]),
                                    end[0:1, :].unsqueeze(1).to_broadcast([1, nb, ne]), ALU.is_ge)
            v.drain()
            nc.vector.tensor_reduce(owner[:, :], passed[:, :, :], AX.X, ALU.add)
            v.drain()
            nc.vector.tensor_scalar(r.expert[:, :], owner[:, :], float(ne - 1), None, ALU.min)


def scatter_tokens(nc, g, rows, r, slots, fill):
    with Phase(nc, "spread") as ph:
        blank = ph.sb("blank", [P, D])
        blanked, filled, sent = ph.sem("blanked"), ph.sem("filled"), ph.sem("sent")
        block = ph.block()
        nb = slots.shape[0] // P

        @block.sync
        def _(sp):
            if fill:
                sp.wait_ge(blanked, 1)
                sp.dma_start(slots.rearrange("(b p) f -> p b f", p=P), blank[:, :].unsqueeze(1).to_broadcast([P, nb, D])).then_inc(filled, 16)

        @block.vector
        def _(v):
            nc.vector.memset(blank[:, :], 0.0).then_inc(blanked, 1)

        @block.gpsimd
        def _(pool):
            if fill:
                pool.wait_ge(filled, 16)
            for k in range(r.choices):
                for t in range(T):
                    pool.indirect_dma_start(slots, bass.IndirectOffsetOnAxis(ap=r.slot[:, k, t:t + 1], axis=0),
                                            rows[:, t, :], None).then_inc(sent, 16)
            pool.wait_ge(sent, 16 * r.choices * T)


def expert_blocks(nc, g, slots, results, r, w1, b1, w2, b2, func, affine=None):
    ne, _, fm = w1.shape
    m_all = fm // P
    banks = m_all // 4
    nb = r.blocks
    assert nb % 2 == 0
    with Phase(nc, "ffn") as ph:
        x = ph.sb("x", [P, 2, D])
        w1_sb, w2_sb = ph.sb("w1", [P, 2, 2, fm]), ph.sb("w2", [P, 2, m_all, D])
        b1_sb, b2_sb, aff = ph.sb("b1", [P, 2, m_all]), ph.sb("b2", [P, 2, D]), ph.sb("aff", [P, 2, 4])
        xt = ph.sb("xt", [P, 2, 2, P])
        ht = ph.sb("ht", [P, 2, m_all, P])
        y = ph.sb("y", [P, 2, D])
        p_x = [ph.ps(f"p_x{u}", [P, 2, 2, P]) for u in range(2)]
        p_h = [[ph.ps(f"p_h{u}{b}", [P, 4, P]) for b in range(2)] for u in range(2)]
        p_y = [ph.ps(f"p_y{u}", [P, 512]) for u in range(2)]
        x_in, w_in = [ph.sem(f"x_in{u}") for u in range(2)], [ph.sem(f"w_in{u}") for u in range(2)]
        turned, xt_ready, h_done, h_ready, y_done, y_ready = (ph.sem(s) for s in ("turned", "xt_ready", "h_done", "h_ready", "y_done", "y_ready"))
        stored = [ph.sem(f"stored{u}") for u in range(2)]
        turn, y_free = ph.sem("turn"), ph.sem("y_free")
        block = ph.block()
        n_w = 4 if affine is None else 6

        @block.sync
        def _(sp):
            sp.sem_inc(y_done, 2)
            sp.sem_inc(y_ready, 2)
            sp.sem_inc(y_free, 2)
            with sp.Fori(0, nb // 2) as i:
                for u in range(2):
                    if ne > 1:
                        e = sp.value_load(r.expert[0:1, bass.ds(i * 2 + u, 1)], min_val=0, max_val=ne - 1)
                    else:
                        e = 0
                    sp.wait_ge(y_ready, i * 2 + (u + 1))
                    sp.sem_inc(turn, 1)
                    sp.dma_start(x[:, u, :], slots[bass.ds((i * 2 + u) * P, P), :]).then_inc(x_in[u], 16)
                    one = bass.ds(e, 1)
                    sp.dma_start(w1_sb[:, u, :, :], w1[one, :, :].rearrange("a (k p) n -> p (a k) n", p=P)).then_inc(w_in[u], 16)
                    sp.dma_start(b1_sb[:, u, :], b1[one, :, :].rearrange("a p m -> p (a m)")).then_inc(w_in[u], 16)
                    sp.dma_start(b2_sb[:, u, :], b2[one, :].rearrange("a n -> (a n)").partition_broadcast(P)).then_inc(w_in[u], 16)
                    if affine is not None:
                        for n in range(2):
                            sp.dma_start(aff[:, u, 2 * n:2 * n + 2], affine[n][one, :, :].rearrange("a p m -> p (a m)")).then_inc(w_in[u], 16)
                    sp.dma_start(w2_sb[:, u, :, :], w2[one, :, :].rearrange("a (k p) n -> p (a k) n", p=P)).then_inc(w_in[u], 16)

        @block.gpsimd
        def _(pool):
            with pool.Fori(0, nb // 2) as i:
                for u in range(2):
                    pool.wait_ge(y_ready, i * 2 + (u + 3))
                    pool.sem_inc(turn, 1)
                    pool.dma_start(results[bass.ds((i * 2 + u) * P, P), :], y[:, u, :]).then_inc(stored[u], 16)
                    pool.wait_ge(stored[u], i * 16 + 16)
                    pool.sem_inc(y_free, 1)

        @block.tensor
        def _(pe):
            with pe.Fori(0, nb // 2) as i:
                for u in range(2):
                    pe.wait_ge(x_in[u], i * 16 + 16)
                    for k in range(2):
                        ins = nc.tensor.transpose(p_x[u][:, 0, k, :], x[:, u, k * P:(k + 1) * P], g.ident[:, :])
                    ins.then_inc(turned, 1)
                for u in range(2):
                    pe.wait_ge(w_in[u], i * (16 * n_w) + 16 * n_w)
                    pe.wait_ge(xt_ready, i * 2 + (u + 1))
                    for m in range(m_all):
                        for k in range(2):
                            ins = nc.tensor.matmul(p_h[u][m // 4][:, m % 4, :], w1_sb[:, u, k, m * P:(m + 1) * P], xt[:, u, k, :],
                                                   start=(k == 0), stop=(k == 1))
                        if m % 4 == 3:
                            ins.then_inc(h_done, 1)
                for u in range(2):
                    for m in range(m_all):
                        if m % 4 == 0:
                            pe.wait_ge(h_ready, i * (2 * banks) + (u * banks + m // 4 + 1))
                        ins = nc.tensor.matmul(p_y[u][:, 0:D], ht[:, u, m, :], w2_sb[:, u, m, :], start=(m == 0), stop=(m == m_all - 1))
                    ins.then_inc(y_done, 1)

        @block.scalar
        def _(act):
            with act.Fori(0, nb // 2) as i:
                for u in range(2):
                    act.wait_ge(y_done, i * 2 + (u + 1))
                    for b in range(banks):
                        act.wait_ge(h_done, i * (2 * banks) + (u * banks + b + 1))
                        for m in range(4 * b, 4 * b + 4):
                            ins = nc.scalar.activation(ht[:, u, m, :], p_h[u][b][:, m % 4, :], func, bias=b1_sb[:, u, m:m + 1])
                        ins.then_inc(h_ready, 1)

        @block.vector
        def _(v):
            with v.Fori(0, nb // 2) as i:
                for u in range(2):
                    v.wait_ge(turned, i * 2 + (u + 1))
                    if affine is None:
                        nc.vector.tensor_copy(xt[:, u, :, :], p_x[u][:, 0, :, :]).then_inc(xt_ready, 1)
                    else:
                        v.wait_ge(w_in[u], i * (16 * n_w) + 16 * n_w)
                        for k in range(2):
                            ins = nc.vector.tensor_scalar(xt[:, u, k, :], p_x[u][:, 0, k, :], aff[:, u, k:k + 1], aff[:, u, 2 + k:3 + k],
                                                          ALU.mult, ALU.add)
                        ins.then_inc(xt_ready, 1)
                for u in range(2):
                    v.wait_ge(y_free, i * 2 + (u + 1))
                    v.wait_ge(y_done, i * 2 + (u + 3))
                    nc.vector.tensor_tensor(y[:, u, :], p_y[u][:, 0:D], b2_sb[:, u, :], ALU.add).then_inc(y_ready, 1)


def combine(nc, g, results, source, r, into, xn=None, guard=False):
    with Phase(nc, "gather") as ph:
        got = ph.sb("got", [P, r.choices, T, D])
        ok, high, low = (ph.sb(s, [P, D], I32) for s in ("ok", "high", "low"))
        clean, top, bottom = ph.sb("clean", [P, T, D]), ph.sb("top", [P, D]), ph.sb("bottom", [P, D])
        arrived = [ph.sem(f"arrived{n}") for n in range(r.choices * T)]
        block = ph.block()

        @block.gpsimd
        def _(pool):
            for k in range(r.choices):
                for t in range(T):
                    pool.indirect_dma_start(got[:, k, t, :], None, results,
                                            bass.IndirectOffsetOnAxis(ap=source[:, k, t:t + 1], axis=0)).then_inc(arrived[k * T + t], 16)

        @block.vector
        def _(v):
            if guard:
                nc.vector.memset(clean[:, :, :], 0.0)
                nc.vector.memset(top[:, :], 1e4)
                nc.vector.memset(bottom[:, :], -1e4)
                v.drain()
            if xn is not None:
                nc.vector.tensor_tensor(into[:, :, :], into[:, :, :], xn[:, :, :], ALU.add)
            for k in range(r.choices):
                v.drain()
                for t in range(T):
                    v.wait_ge(arrived[k * T + t], 16)
                    if not guard:
                        nc.vector.scalar_tensor_tensor(into[:, t, :], got[:, k, t, :], r.gate[:, k, t:t + 1], into[:, t, :], ALU.mult, ALU.add)
                        continue
                    y = got[:, k, t, :]
                    nc.vector.tensor_scalar(y, y, r.gate[:, k, t:t + 1], None, ALU.mult)
                    v.drain()
                    nc.vector.tensor_tensor(ok[:, :], y, y, ALU.is_equal)
                    nc.vector.tensor_scalar(high[:, :], y, 3.4028234e38, None, ALU.is_gt)
                    nc.vector.tensor_scalar(low[:, :], y, -3.4028234e38, None, ALU.is_lt)
                    v.drain()
                    nc.vector.copy_predicated(clean[:, t, :], ok[:, :], y)
                    v.drain()
                    nc.vector.copy_predicated(clean[:, t, :], high[:, :], top[:, :])
                    v.drain()
                    nc.vector.copy_predicated(clean[:, t, :], low[:, :], bottom[:, :])
                    v.drain()
                    nc.vector.tensor_tensor(into[:, t, :], into[:, t, :], clean[:, t, :], ALU.add)


def capacity_ffn(nc, g, i):
    chosen = max(max(1, int(0.5 * N)) - 1, 1)
    with Phase(nc, "cap") as ph:
        xn = ph.sb("xn", [P, T, D])
        r = Routes(ph, 1, (chosen + P - 1) // P)
        source = ph.sb("source_i", [P, 1, T], I32)
        r.source = source[:, 0, :]
        slots, results = g.dram("cap_slots", [NP, D]), g.dram("cap_results", [r.blocks * P, D])
        layernorm(nc, g.X, xn)
        rank_tokens(nc, g, xn, i["L0_ffn_wr"].rearrange("d o -> (d o)"), i["L0_ffn_br"], chosen, r)
        scatter_tokens(nc, g, xn, r, slots, fill=False)
        expert_blocks(nc, g, slots, results, r, i["L0_ffn_w1"].rearrange("(a d) f -> a d f", a=1), i["L0_ffn_b1"],
                      i["L0_ffn_w2"].rearrange("(a d) f -> a d f", a=1), i["L0_ffn_b2"].rearrange("(a d) -> a d", a=1),
                      ACT.Gelu_apprx_tanh)
        combine(nc, g, results, source, r, g.X, xn=xn)


def blocks_for(choices, experts):
    need = (NP * choices + experts * (P - 1)) // P
    return need + need % 2


def switch_ffn(nc, g, i):
    ne = i["L1_ffn_gate_w"].shape[1]
    capacity = -(-5 * N // (4 * ne))
    with Phase(nc, "switch") as ph:
        xn, xt = ph.sb("xn", [P, T, D]), ph.sb("xt", [P, T, 2, P])
        r = Routes(ph, 1, blocks_for(1, ne))
        slots, results = g.dram("switch_slots", [r.blocks * P, D]), g.dram("switch_results", [r.blocks * P, D])
        layernorm(nc, g.X, xn)
        self_terms(nc, g, xn, xt)
        choose_experts(nc, g, xt, i["L1_ffn_gate_w"], i["L1_ffn_gate_b"], r, capacity=capacity)
        scatter_tokens(nc, g, xn, r, slots, fill=True)
        expert_blocks(nc, g, slots, results, r, i["L1_ffn_w1"], i["L1_ffn_b1"], i["L1_ffn_w2"], i["L1_ffn_b2"], ACT.Relu)
        combine(nc, g, results, r.slot, r, g.X, guard=True)


def top2_gelu_ffn(nc, g, i):
    ne = i["L2_ffn_Wr"].shape[1]
    with Phase(nc, "top2") as ph:
        xn, xt = ph.sb("xn", [P, T, D]), ph.sb("xt", [P, T, 2, P])
        r = Routes(ph, 2, blocks_for(2, ne))
        slots, results = g.dram("gelu_slots", [r.blocks * P, D]), g.dram("gelu_results", [r.blocks * P, D])
        layernorm(nc, g.X, xn)
        self_terms(nc, g, xn, xt)
        choose_experts(nc, g, xt, i["L2_ffn_Wr"], i["L2_ffn_br"], r)
        layernorm(nc, xn, xn)
        scatter_tokens(nc, g, xn, r, slots, fill=True)
        expert_blocks(nc, g, slots, results, r, i["L2_ffn_W1"], i["L2_ffn_b1"], i["L2_ffn_W2"], i["L2_ffn_b2"], ACT.Gelu,
                      affine=(i["L2_ffn_ln_g"], i["L2_ffn_ln_b"]))
        combine(nc, g, results, r.slot, r, g.X)


def top2_relu_ffn(nc, g, i):
    ne = i["L3_ffn_gate_w"].shape[1]
    with Phase(nc, "moe") as ph:
        xn, xt = ph.sb("xn", [P, T, D]), ph.sb("xt", [P, T, 2, P])
        r = Routes(ph, 2, blocks_for(2, ne))
        slots, results = g.dram("relu_slots", [r.blocks * P, D]), g.dram("relu_results", [r.blocks * P, D])
        layernorm(nc, g.X, xn)
        self_terms(nc, g, xn, xt)
        choose_experts(nc, g, xt, i["L3_ffn_gate_w"], i["L3_ffn_gate_b"], r)
        scatter_tokens(nc, g, xn, r, slots, fill=True)
        expert_blocks(nc, g, slots, results, r, i["L3_ffn_w1"], i["L3_ffn_b1"], i["L3_ffn_w2"], i["L3_ffn_b2"], ACT.Relu)
        combine(nc, g, results, r.slot, r, xn)
        layernorm(nc, xn, xn, gamma=i["L3_ffn_gamma"], beta=i["L3_ffn_beta"], add=g.X)


def tiles_of(v, g, registers, i):
    v.load(registers, g.chunk_tile[0:1, bass.ds(i * U, U)])
    return [v.snap(r, min_val=0, max_val=T - 1) for r in registers]


def degrees(nc, g):
    with Phase(nc, "deg") as ph:
        hot, deg = ph.sb("hot", [P, U, P]), ph.sb("deg", [P, T])
        positive, root = ph.sb("positive", [P, T]), ph.sb("root", [P, T])
        p_deg = [ph.ps(f"p_deg{u}", [P, 512]) for u in range(U)]
        hot_ready, summed, added, credited = ph.sem("hot_ready"), ph.sem("summed"), ph.sem("added"), ph.sem("credited")
        deg_ready, root_ready = ph.sem("deg_ready"), ph.sem("root_ready")
        block = ph.block()

        @block.tensor
        def _(pe):
            with pe.Fori(0, EC // U) as i:
                for u in range(U):
                    pe.wait_ge(added, i * U + (u + 1))
                    pe.wait_ge(hot_ready, i * U + (u + 1))
                    nc.tensor.matmul(p_deg[u][:, 0:1], hot[:, u, :], g.ones[:, 0:1], start=True, stop=True).then_inc(summed, 1)

        @block.scalar
        def _(act):
            act.sem_inc(added, U)
            act.sem_inc(summed, U)
            act.wait_ge(deg_ready, 1)
            nc.scalar.activation(root[:, :], deg[:, :], ACT.Sqrt).then_inc(root_ready, 1)

        @block.vector
        def _(v):
            tile = [v.alloc_register(f"{ph.name}_tile{u}") for u in range(U)]
            nc.vector.memset(deg[:, :], 1.0)
            with v.Fori(0, EC // U) as i:
                tiles = tiles_of(v, g, tile, i)
                for u in range(U):
                    v.wait_ge(summed, i * U + (u + 1))
                    c = bass.ds(i * U + u, 1)
                    nc.vector.tensor_scalar(hot[:, u, :], g.iota_free[:, :], g.dst[:, c], g.weight[:, c], ALU.is_equal, ALU.mult)\
                        .then_inc(hot_ready, 1)
                for u in range(U):
                    v.drain()
                    v.wait_ge(summed, i * U + (u + 1 + U))
                    d = deg[:, bass.ds(tiles[u], 1)]
                    nc.vector.tensor_tensor(d, d, p_deg[u][:, 0:1], ALU.add).then_inc(added, 1)
                v.drain()
            nc.vector.tensor_scalar(positive[:, :], deg[:, :], 0.0, None, ALU.is_gt)
            nc.vector.tensor_scalar(deg[:, :], deg[:, :], 1e-30, None, ALU.max).then_inc(deg_ready, 1)
            v.wait_ge(root_ready, 1)
            nc.vector.reciprocal(g.dinv[:, :], root[:, :])
            v.drain()
            nc.vector.tensor_tensor(g.dinv[:, :], g.dinv[:, :], positive[:, :], ALU.mult)


def scale_rows(nc, g, x, y, table, relu=False):
    with Phase(nc, "scale") as ph:
        ready, written = ph.sem("ready"), ph.sem("written")
        block = ph.block()

        @block.vector
        def _(v):
            for t in range(T):
                if relu:
                    ins = nc.vector.tensor_scalar(y[:, t, :], x[:, t, :], 0.0, g.dinv[:, t:t + 1], ALU.max, ALU.mult)
                else:
                    ins = nc.vector.tensor_scalar(y[:, t, :], x[:, t, :], g.dinv[:, t:t + 1], None, ALU.mult)
            ins.then_inc(ready, 1)

        @block.sync
        def _(sp):
            sp.wait_ge(ready, 1)
            sp.dma_start(table.rearrange("(t p) f -> p t f", p=P), y[:, :, :]).then_inc(written, 16)
            sp.wait_ge(written, 16)


def gcn_edges(nc, g, table, acc):
    with Phase(nc, "gcn") as ph:
        idx = ph.sb("idx", [P, U], I32)
        got = ph.sb("got", [P, U, D])
        hot = ph.sb("hot", [P, U, P])
        p_sum = [ph.ps(f"p_sum{u}", [P, 512]) for u in range(U)]
        idx_ready, turn, hot_ready, agg_done, added = (ph.sem(s) for s in ("idx_ready", "turn", "hot_ready", "agg_done", "added"))
        gathered = [ph.sem(f"gathered{u}") for u in range(U)]
        block = ph.block()

        @block.sync
        def _(sp):
            sp.sem_inc(agg_done, U)
            sp.sem_inc(added, U)

        @block.scalar
        def _(act):
            with act.Fori(0, EC // U) as i:
                for u in range(U):
                    act.wait_ge(agg_done, i * U + (u + 1))
                    act.sem_inc(turn, 1)
                    nc.scalar.copy(idx[:, u:u + 1], g.src[:, bass.ds(i * U + u, 1)]).then_inc(idx_ready, 1)

        @block.gpsimd
        def _(pool):
            with pool.Fori(0, EC // U) as i:
                for u in range(U):
                    pool.wait_ge(idx_ready, i * U + (u + 1))
                    pool.sem_inc(turn, 1)
                    pool.indirect_dma_start(got[:, u, :], None, table,
                                            bass.IndirectOffsetOnAxis(ap=idx[:, u:u + 1], axis=0)).then_inc(gathered[u], 16)

        @block.tensor
        def _(pe):
            with pe.Fori(0, EC // U) as i:
                for u in range(U):
                    pe.wait_ge(added, i * U + (u + 1))
                    pe.wait_ge(hot_ready, i * U + (u + 1))
                    pe.wait_ge(gathered[u], i * 16 + 16)
                    for half in range(2):
                        ins = nc.tensor.matmul(p_sum[u][:, half * P:(half + 1) * P], got[:, u, half * P:(half + 1) * P],
                                               hot[:, u, :], start=True, stop=True)
                    ins.then_inc(agg_done, 1)

        @block.vector
        def _(v):
            tile = [v.alloc_register(f"{ph.name}_tile{u}") for u in range(U)]
            with v.Fori(0, EC // U) as i:
                tiles = tiles_of(v, g, tile, i)
                for u in range(U):
                    v.wait_ge(agg_done, i * U + (u + 1))
                    c = bass.ds(i * U + u, 1)
                    nc.vector.tensor_scalar(hot[:, u, :], g.iota_free[:, :], g.dst[:, c], g.weight[:, c], ALU.is_equal, ALU.mult)\
                        .then_inc(hot_ready, 1)
                for u in range(U):
                    v.drain()
                    v.wait_ge(agg_done, i * U + (u + 1 + U))
                    a = acc[:, bass.ds(tiles[u], 1), :, :].rearrange("p a h n -> p (a h n)")
                    nc.vector.tensor_tensor(a, a, p_sum[u][:, 0:D], ALU.add).then_inc(added, 1)
                v.drain()


def gcn_linear(nc, g, agg, w, b, z):
    with Phase(nc, "lin") as ph:
        w_sb, b_row = ph.sb("w", [P, 2, D]), ph.sb("b", [P, D])
        p_z = [ph.ps(f"p_z{n}", [P, 512]) for n in range(4)]
        loaded, done, taken = ph.sem("loaded"), ph.sem("done"), ph.sem("taken")
        block = ph.block()

        @block.sync
        def _(sp):
            sp.dma_start(w_sb[:, :, :], w.rearrange("(k p) n -> p k n", p=P)).then_inc(loaded, 16)
            sp.dma_start(b_row[:, :], row(b)).then_inc(loaded, 16)

        @block.tensor
        def _(pe):
            pe.wait_ge(loaded, 32)
            for t in range(T):
                if t >= 4:
                    pe.wait_ge(taken, t - 3)
                for k in range(2):
                    ins = nc.tensor.matmul(p_z[t % 4][:, 0:D], agg[:, t, k, :], w_sb[:, k, :], start=(k == 0), stop=(k == 1))
                ins.then_inc(done, 1)

        @block.vector
        def _(v):
            v.wait_ge(loaded, 32)
            for t in range(T):
                v.wait_ge(done, t + 1)
                nc.vector.scalar_tensor_tensor(z[:, t, :], p_z[t % 4][:, 0:D], g.dinv[:, t:t + 1], b_row[:, :], ALU.mult, ALU.add)\
                    .then_inc(taken, 1)


def softmax_into(nc, g, z, into):
    with Phase(nc, "soft") as ph:
        top, total = ph.sb("top", [P, T]), ph.sb("total", [P, T])
        ready, done = ph.sem("ready"), ph.sem("done")
        block = ph.block()

        @block.vector
        def _(v):
            nc.vector.tensor_reduce(top[:, :], z[:, :, :], AX.X, ALU.max)
            v.drain()
            nc.vector.tensor_scalar(top[:, :], top[:, :], -1.0, None, ALU.mult).then_inc(ready, 1)
            v.wait_ge(done, T)
            nc.vector.reciprocal(total[:, :], total[:, :])
            v.drain()
            for t in range(T):
                nc.vector.scalar_tensor_tensor(into[:, t, :], z[:, t, :], total[:, t:t + 1], into[:, t, :], ALU.mult, ALU.add)

        @block.scalar
        def _(act):
            act.wait_ge(ready, 1)
            for t in range(T):
                nc.scalar.activation(z[:, t, :], z[:, t, :], ACT.Exp, bias=top[:, t:t + 1], accum_out=total[:, t:t + 1]).then_inc(done, 1)


def relu_into(nc, g, z, xn, into):
    with Phase(nc, "relu") as ph:
        block = ph.block()

        @block.vector
        def _(v):
            nc.vector.tensor_tensor(into[:, :, :], into[:, :, :], xn[:, :, :], ALU.add)
            v.drain()
            nc.vector.scalar_tensor_tensor(into[:, :, :], z[:, :, :], 0.0, into[:, :, :], ALU.max, ALU.add)


def gcn_softmax(nc, g, i):
    with Phase(nc, "gcn2") as ph:
        y, z, acc = ph.sb("y", [P, T, D]), ph.sb("z", [P, T, D]), ph.sb("acc", [P, T, 2, P])
        layernorm(nc, g.X, z)
        for n in (1, 2):
            table = g.dram(f"gcn_table{n}", [NP, D])
            scale_rows(nc, g, z, y, table, relu=(n == 2))
            self_terms(nc, g, y, acc)
            gcn_edges(nc, g, table, acc)
            gcn_linear(nc, g, acc, i[f"L2_gnn_W{n}"], i[f"L2_gnn_b{n}"], z)
        softmax_into(nc, g, z, g.X)


def gcn_residual(nc, g, i):
    with Phase(nc, "gcn1") as ph:
        xn, y, z, acc = ph.sb("xn", [P, T, D]), ph.sb("y", [P, T, D]), ph.sb("z", [P, T, D]), ph.sb("acc", [P, T, 2, P])
        table = g.dram("gcn_table3", [NP, D])
        layernorm(nc, g.X, xn)
        scale_rows(nc, g, xn, y, table)
        self_terms(nc, g, y, acc)
        gcn_edges(nc, g, table, acc)
        gcn_linear(nc, g, acc, i["L3_gnn_W"], i["L3_gnn_b"], z)
        relu_into(nc, g, z, xn, g.X)


def relation_tables(nc, g, xt, w, wt, attn_src, attn_dst, h_table, src_table, score_dst):
    S2 = 2 * HD
    with Phase(nc, "rel") as ph:
        w_sb, wt_sb = ph.sb("w", [P, R, 2, D]), ph.sb("wt", [P, R, 2, D])
        heads = ph.sb("heads", [P, 2, S2])
        proj = ph.sb("proj", [P, 2, R, S2])
        rows = ph.sb("rows", [P, 2, R, D])
        scores = ph.sb("scores", [P, T, R, HD])
        p_proj = ph.ps("p_proj", [P, 2, R, S2])
        p_score = [ph.ps(f"p_score{b}", [P, 512]) for b in range(2)]
        p_rows = [ph.ps(f"p_rows{b}", [P, 2, D]) for b in range(4)]
        blanked, heads_in, w_in, wt_in = ph.sem("blanked"), ph.sem("heads_in"), ph.sem("w_in"), ph.sem("wt_in")
        proj_done, proj_ready, score_done, score_taken = (ph.sem(s) for s in ("proj_done", "proj_ready", "score_done", "score_taken"))
        rows_done, rows_taken, scores_written = ph.sem("rows_done"), ph.sem("rows_taken"), ph.sem("scores_written")
        written = [ph.sem(f"written{b}") for b in range(2)]
        block = ph.block()
        per_tile = R // 2

        @block.sync
        def _(sp):
            sp.dma_start(w_sb[:, :, :, :], w.rearrange("r (k p) f -> p (r k) f", p=P)).then_inc(w_in, 16)
            sp.wait_ge(blanked, 1)
            for n, attn in enumerate((attn_src, attn_dst)):
                for h in range(HD):
                    p0 = h * DH % P
                    sp.dma_start(heads[p0:p0 + DH, h * DH // P, n * HD + h:n * HD + h + 1],
                                 attn[h:h + 1, :].rearrange("a d -> d a")).then_inc(heads_in, 16)
            sp.dma_start(wt_sb[:, :, :, :], wt.rearrange("r (k p) o -> p (r k) o", p=P)).then_inc(wt_in, 16)
            h_view = h_table.rearrange("(r t p) f -> t p r f", r=R, p=P)
            for t in range(T):
                sp.wait_ge(rows_taken, per_tile * (t + 1))
                sp.dma_start(h_view[t, :, :, :], rows[:, t % 2, :, :]).then_inc(written[t % 2], 16)
            sp.wait_ge(score_taken, 2 * T)
            for r in range(R):
                sp.dma_start(src_table[r * NP:(r + 1) * NP, :].rearrange("(t p) h -> p t h", p=P), scores[:, :, r, :])\
                    .then_inc(scores_written, 16)
            sp.wait_ge(scores_written, 16 * R)
            for b in range(2):
                sp.wait_ge(written[b], 16 * ((T + 1 - b) // 2))

        @block.tensor
        def _(pe):
            pe.wait_ge(w_in, 16)
            pe.wait_ge(heads_in, 16 * S2)
            for half in range(2):
                for r in range(R):
                    for k in range(2):
                        ins = nc.tensor.matmul(p_proj[:, half, r, :], w_sb[:, r, k, half * P:(half + 1) * P], heads[:, k, :],
                                               start=(k == 0), stop=(k == 1))
            ins.then_inc(proj_done, 1)
            pe.wait_ge(proj_ready, 1)
            for t in range(T):
                if t >= 2:
                    pe.wait_ge(score_taken, 2 * (t - 1))
                for k in range(2):
                    ins = nc.tensor.matmul(p_score[t % 2][:, 0:R * S2], xt[:, t, k, :], proj[:, k, :, :].rearrange("p r s -> p (r s)"),
                                           start=(k == 0), stop=(k == 1))
                ins.then_inc(score_done, 1)
            pe.wait_ge(wt_in, 16)
            for t in range(T):
                for b in range(per_tile):
                    n = t * per_tile + b
                    if n >= 4:
                        pe.wait_ge(rows_taken, n - 3)
                    for r in range(2):
                        for k in range(2):
                            ins = nc.tensor.matmul(p_rows[n % 4][:, r, :], xt[:, t, k, :], wt_sb[:, 2 * b + r, k, :],
                                                   start=(k == 0), stop=(k == 1))
                    ins.then_inc(rows_done, 1)

        def take(n, copy, eng):
            t, b = n // per_tile, n % per_tile
            if t >= 2:
                eng.wait_ge(written[t % 2], 16 * (t // 2))
            eng.wait_ge(rows_done, n + 1)
            if n:
                eng.wait_ge(rows_taken, n)
            copy(rows[:, t % 2, 2 * b:2 * b + 2, :], p_rows[n % 4][:, :, :]).then_inc(rows_taken, 1)

        @block.scalar
        def _(act):
            for n in range(1, T * per_tile, 2):
                take(n, nc.scalar.copy, act)

        @block.vector
        def _(v):
            nc.vector.memset(heads[:, :, :], 0.0).then_inc(blanked, 1)
            v.wait_ge(proj_done, 1)
            nc.vector.tensor_copy(proj[:, :, :, :], p_proj[:, :, :, :]).then_inc(proj_ready, 1)
            for t in range(T):
                v.wait_ge(score_done, t + 1)
                both = p_score[t % 2][:, 0:R * S2].rearrange("p (r s) -> p r s", r=R)
                nc.vector.tensor_copy(scores[:, t, :, :], both[:, :, 0:HD]).then_inc(score_taken, 1)
                nc.vector.tensor_copy(score_dst[:, t, :, :], both[:, :, HD:S2]).then_inc(score_taken, 1)
            for n in range(0, T * per_tile, 2):
                take(n, nc.vector.tensor_copy, v)


def edge_scores(nc, g, src_table, score_dst, scores, amax):
    HH = HD // 2
    with Phase(nc, "score") as ph:
        idx = ph.sb("idx", [P, U], I32)
        got = ph.sb("got", [P, U, HD])
        hot, hot_t = ph.sb("hot", [P, U, P]), ph.sb("hot_t", [P, U, P])
        rel_idx = ph.sb("rel_idx", [P, R])
        rel, picked, s = ph.sb("rel", [P, U, R]), ph.sb("picked", [P, U, R, HD]), ph.sb("s", [P, U, HD])
        diag = ph.sb("diag", [P, 2, HD, P])
        peak = ph.sb("peak", [P, 2, HD])
        p_hot = [ph.ps(f"p_hot{b}", [P, 4, P]) for b in range(2)]
        p_dst = ph.ps("p_dst", [P, U, R, HD])
        p_max = [ph.ps(f"p_max{b}", [P, HD, P]) for b in range(2)]
        idx_ready, turn, hot_ready, turned, copied = (ph.sem(x) for x in ("idx_ready", "turn", "hot_ready", "turned", "copied"))
        dst_done, s_ready, diag_v, diag_a, max_done, peaked = (ph.sem(x) for x in ("dst_done", "s_ready", "diag_v", "diag_a", "max_done", "peaked"))
        iota_made = ph.sem("iota_made")
        gathered = [ph.sem(f"gathered{u}") for u in range(U)]
        block = ph.block()

        @block.sync
        def _(sp):
            sp.sem_inc(max_done, U)
            sp.sem_inc(peaked, U)
            sp.sem_inc(s_ready, 1)
            sp.sem_inc(dst_done, 1)

        @block.gpsimd
        def _(pool):
            nc.gpsimd.iota(rel_idx[:, :], [[1, R]], base=0, channel_multiplier=0,
                           allow_small_or_imprecise_dtypes=True).then_inc(iota_made, 1)
            with pool.Fori(0, EC // U) as i:
                for u in range(U):
                    pool.wait_ge(idx_ready, i * U + (u + 1))
                    pool.sem_inc(turn, 1)
                    pool.indirect_dma_start(got[:, u, :], None, src_table,
                                            bass.IndirectOffsetOnAxis(ap=idx[:, u:u + 1], axis=0)).then_inc(gathered[u], 16)

        @block.tensor
        def _(pe):
            tile = [pe.alloc_register(f"{ph.name}_pe_tile{u}") for u in range(U)]
            with pe.Fori(0, EC // U) as i:
                tiles = tiles_of(pe, g, tile, i)
                for u in range(U):
                    pe.wait_ge(hot_ready, i * U + (u + 1))
                    ins = nc.tensor.transpose(p_hot[u // 4][:, u % 4, :], hot[:, u, :], g.ident[:, :])
                    if u % 4 == 3:
                        ins.then_inc(turned, 1)
                pe.wait_ge(s_ready, i + 1)
                for u in range(U):
                    if u % 4 == 0:
                        pe.wait_ge(copied, i * 2 + (u // 4 + 1))
                    ins = nc.tensor.matmul(p_dst[:, u, :, :].rearrange("p r h -> p (r h)"), hot_t[:, u, :],
                                           score_dst[:, bass.ds(tiles[u], 1), :, :].rearrange("p a r h -> p (a r h)"),
                                           start=True, stop=True)
                ins.then_inc(dst_done, 1)
                for u in range(U):
                    pe.wait_ge(peaked, i * U + (u + 1 + U - 2))
                    for part, ready in ((0, diag_v), (1, diag_a)):
                        pe.wait_ge(ready, i * U + (u + 1))
                        ins = nc.tensor.matmul(p_max[u % 2][:, part * HH:(part + 1) * HH, :].rearrange("p h e -> p (h e)"), hot[:, u, :],
                                               diag[:, u % 2, part * HH:(part + 1) * HH, :].rearrange("p h e -> p (h e)"),
                                               start=True, stop=True)
                    ins.then_inc(max_done, 1)

        @block.scalar
        def _(act):
            with act.Fori(0, EC // U) as i:
                for u in range(U):
                    act.wait_ge(s_ready, i + 1)
                    act.sem_inc(turn, 1)
                    nc.scalar.copy(idx[:, u:u + 1], g.hrow[:, bass.ds(i * U + u, 1)]).then_inc(idx_ready, 1)
                for b in range(2):
                    act.wait_ge(dst_done, i + 1)
                    act.wait_ge(turned, i * 2 + (b + 1))
                    nc.scalar.copy(hot_t[:, 4 * b:4 * b + 4, :], p_hot[b][:, :, :]).then_inc(copied, 1)
                act.wait_ge(s_ready, i + 2)
                act.sem_inc(turn, 1)
                for u in range(U):
                    act.wait_ge(max_done, i * U + (u + 1 + U - 2))
                    for h in range(HH, HD):
                        ins = nc.scalar.activation(diag[:, u % 2, h, :], g.ident[:, :], ACT.Copy, scale=s[:, u, h:h + 1])
                    ins.then_inc(diag_a, 1)

        @block.vector
        def _(v):
            tile = [v.alloc_register(f"{ph.name}_tile{u}") for u in range(U)]
            nc.vector.memset(amax[:, :, :], 0.0)
            v.wait_ge(iota_made, 1)

            def peak_of(i, u, t):
                v.wait_ge(max_done, i * U + (u + 1 + U))
                nc.vector.tensor_reduce(peak[:, u % 2, :], p_max[u % 2][:, :, :], AX.X, ALU.max).then_inc(peaked, 1)
                v.drain()
                a = amax[:, bass.ds(t, 1), :].rearrange("p a h -> p (a h)")
                nc.vector.tensor_tensor(a, a, peak[:, u % 2, :], ALU.max)

            with v.Fori(0, EC // U) as i:
                tiles = tiles_of(v, g, tile, i)
                for u in range(U):
                    v.wait_ge(max_done, i * U + (u + 1))
                    nc.vector.tensor_scalar(hot[:, u, :], g.iota_free[:, :], g.dst[:, bass.ds(i * U + u, 1)], None,
                                            ALU.is_equal).then_inc(hot_ready, 1)
                nc.vector.tensor_tensor(rel[:, :, :], rel_idx[:, :].unsqueeze(1).to_broadcast([P, U, R]),
                                        g.etype[:, bass.ds(i * U, U)].unsqueeze(2).to_broadcast([P, U, R]), ALU.is_equal)
                v.drain()
                v.wait_ge(dst_done, i + 2)
                nc.vector.tensor_tensor(picked[:, :, :, :], p_dst[:, :, :, :],
                                        rel[:, :, :].unsqueeze(3).to_broadcast([P, U, R, HD]), ALU.mult)
                v.drain()
                v.wait_ge(max_done, i * U + U)
                v.sem_inc(turn, 1)
                nc.vector.tensor_reduce(s[:, :, :], picked[:, :, :, :].rearrange("p u r h -> p u h r"), AX.X, ALU.add)
                v.drain()
                for u in range(U):
                    v.wait_ge(gathered[u], i * 16 + 16)
                    v.sem_inc(turn, 1)
                nc.vector.tensor_tensor(s[:, :, :], s[:, :, :], got[:, :, :], ALU.add)
                v.drain()
                nc.vector.scalar_tensor_tensor(s[:, :, :], s[:, :, :], 0.2, s[:, :, :], ALU.mult, ALU.max)
                v.drain()
                nc.vector.tensor_copy(scores[:, bass.ds(i * U, U), :], s[:, :, :]).then_inc(s_ready, 1)
                for u in range(U):
                    v.wait_ge(max_done, i * U + (u + 1 + U - 2))
                    nc.vector.tensor_tensor(diag[:, u % 2, 0:HH, :], g.ident[:, :].unsqueeze(1).to_broadcast([P, HH, P]),
                                            s[:, u, 0:HH].unsqueeze(2).to_broadcast([P, HH, P]), ALU.mult).then_inc(diag_v, 1)
                    if u:
                        peak_of(i, u - 1, tiles[u - 1])
                peak_of(i, U - 1, tiles[U - 1])
                v.drain()


def attend(nc, g, h_table, scores, amax, acc):
    WIDE = D + HD
    with Phase(nc, "attend") as ph:
        idx = ph.sb("idx", [P, U], I32)
        got = ph.sb("got", [P, U, D])
        hot, hot_t = ph.sb("hot", [P, U, P]), ph.sb("hot_t", [P, U, P])
        less = ph.sb("less", [P, U, HD])
        msg = ph.sb("msg", [P, U, WIDE])
        p_hot = [ph.ps(f"p_hot{b}", [P, 4, P]) for b in range(2)]
        p_amax = ph.ps("p_amax", [P, U, HD])
        p_sum = [ph.ps(f"p_sum{b}", [P, 512]) for b in range(4)]
        idx_ready, turn, hot_ready, turned, copied = (ph.sem(x) for x in ("idx_ready", "turn", "hot_ready", "turned", "copied"))
        amax_done, less_ready, exp_done, msg_ready, agg_done, added = (
            ph.sem(x) for x in ("amax_done", "less_ready", "exp_done", "msg_ready", "agg_done", "added"))
        gathered = [ph.sem(f"gathered{u}") for u in range(U)]
        block = ph.block()

        @block.sync
        def _(sp):
            sp.sem_inc(agg_done, U)
            sp.sem_inc(added, U)
            sp.sem_inc(msg_ready, U)
            sp.sem_inc(less_ready, 1)

        @block.gpsimd
        def _(pool):
            with pool.Fori(0, EC // U) as i:
                for u in range(U):
                    pool.wait_ge(msg_ready, i * U + (u + 1))
                    pool.sem_inc(turn, 1)
                    pool.wait_ge(idx_ready, i * U + (u + 1))
                    pool.sem_inc(turn, 1)
                    pool.indirect_dma_start(got[:, u, :], None, h_table,
                                            bass.IndirectOffsetOnAxis(ap=idx[:, u:u + 1], axis=0)).then_inc(gathered[u], 16)

        @block.tensor
        def _(pe):
            tile = [pe.alloc_register(f"{ph.name}_pe_tile{u}") for u in range(U)]
            with pe.Fori(0, EC // U) as i:
                tiles = tiles_of(pe, g, tile, i)
                for u in range(U):
                    pe.wait_ge(hot_ready, i * U + (u + 1))
                    ins = nc.tensor.transpose(p_hot[u // 4][:, u % 4, :], hot[:, u, :], g.ident[:, :])
                    if u % 4 == 3:
                        ins.then_inc(turned, 1)
                pe.wait_ge(less_ready, i + 1)
                for u in range(U):
                    if u % 4 == 0:
                        pe.wait_ge(copied, i * 2 + (u // 4 + 1))
                    ins = nc.tensor.matmul(p_amax[:, u, :], hot_t[:, u, :],
                                           amax[:, bass.ds(tiles[u], 1), :].rearrange("p a h -> p (a h)"), start=True, stop=True)
                ins.then_inc(amax_done, 1)
                for u in range(U):
                    pe.wait_ge(added, i * U + (u + 1 + U - 4))
                    pe.wait_ge(msg_ready, i * U + (u + 1 + U))
                    nc.tensor.matmul(p_sum[u % 4][:, 0:WIDE], hot[:, u, :], msg[:, u, :], start=True, stop=True).then_inc(agg_done, 1)

        @block.scalar
        def _(act):
            with act.Fori(0, EC // U) as i:
                for u in range(U):
                    act.wait_ge(msg_ready, i * U + (u + 1))
                    act.sem_inc(turn, 1)
                    nc.scalar.copy(idx[:, u:u + 1], g.hrow[:, bass.ds(i * U + u, 1)]).then_inc(idx_ready, 1)
                for b in range(2):
                    act.wait_ge(less_ready, i + 1)
                    act.wait_ge(turned, i * 2 + (b + 1))
                    nc.scalar.copy(hot_t[:, 4 * b:4 * b + 4, :], p_hot[b][:, :, :]).then_inc(copied, 1)
                act.wait_ge(agg_done, i * U + U)
                act.wait_ge(less_ready, i + 2)
                nc.scalar.activation(msg[:, :, D:WIDE], less[:, :, :], ACT.Exp).then_inc(exp_done, 1)

        @block.vector
        def _(v):
            tile = [v.alloc_register(f"{ph.name}_tile{u}") for u in range(U)]
            nc.vector.memset(acc[:, :, :], 0.0)

            def add(i, u, t):
                v.drain()
                v.wait_ge(agg_done, i * U + (u + 1 + U))
                a = acc[:, bass.ds(t, 1), :].rearrange("p a f -> p (a f)")
                nc.vector.tensor_tensor(a, a, p_sum[u % 4][:, 0:WIDE], ALU.add).then_inc(added, 1)

            with v.Fori(0, EC // U) as i:
                tiles = tiles_of(v, g, tile, i)
                for u in range(U):
                    v.wait_ge(agg_done, i * U + (u + 1))
                    nc.vector.tensor_scalar(hot[:, u, :], g.iota_free[:, :], g.dst[:, bass.ds(i * U + u, 1)], None,
                                            ALU.is_equal).then_inc(hot_ready, 1)
                v.wait_ge(amax_done, i + 1)
                nc.vector.tensor_tensor(less[:, :, :], scores[:, bass.ds(i * U, U), :], p_amax[:, :, :], ALU.subtract).then_inc(less_ready, 1)
                v.wait_ge(exp_done, i + 1)
                v.sem_inc(turn, 1)
                for u in range(U):
                    v.wait_ge(gathered[u], i * 16 + 16)
                    nc.vector.tensor_tensor(msg[:, u, 0:D].rearrange("p (h d) -> p h d", h=HD),
                                            got[:, u, :].rearrange("p (h d) -> p h d", h=HD),
                                            msg[:, u, D:WIDE].unsqueeze(2).to_broadcast([P, HD, DH]), ALU.mult).then_inc(msg_ready, 1)
                    if u >= 2:
                        add(i, u - 2, tiles[u - 2])
                for u in range(U - 2, U):
                    add(i, u, tiles[u])
                v.drain()


def divide_into(nc, g, acc, into):
    with Phase(nc, "divide") as ph:
        total, share = ph.sb("total", [P, T, HD]), ph.sb("share", [P, T, HD])
        block = ph.block()

        @block.vector
        def _(v):
            nc.vector.tensor_scalar(total[:, :, :], acc[:, :, D:D + HD], 1e-12, None, ALU.add)
            v.drain()
            nc.vector.reciprocal(share[:, :, :], total[:, :, :])
            v.drain()
            for t in range(T):
                a = acc[:, t, 0:D].rearrange("p (h d) -> p h d", h=HD)
                nc.vector.tensor_tensor(a, a, share[:, t, :].unsqueeze(2).to_broadcast([P, HD, DH]), ALU.mult)
            v.drain()
            nc.vector.tensor_tensor(into[:, :, :], into[:, :, :], acc[:, :, 0:D], ALU.add)


def relational_attention(nc, g, i):
    h_table, src_table = g.dram("h_table", [R * NP, D]), g.dram("src_table", [R * NP, HD])
    with Phase(nc, "rgat") as ph:
        score_dst, amax = ph.sb("score_dst", [P, T, R, HD]), ph.sb("amax", [P, T, HD])
        scores, acc = ph.sb("scores", [P, EC, HD]), ph.sb("acc", [P, T, D + HD])
        with Phase(nc, "rgat_in") as inner:
            xn, xt = inner.sb("xn", [P, T, D]), inner.sb("xt", [P, T, 2, P])
            layernorm(nc, g.X, xn)
            self_terms(nc, g, xn, xt)
            relation_tables(nc, g, xt, i["L1_gnn_W"], i["L1_gnn_W_turned"], i["L1_gnn_attn_src"], i["L1_gnn_attn_dst"],
                            h_table, src_table, score_dst)
        edge_scores(nc, g, src_table, score_dst, scores, amax)
        attend(nc, g, h_table, scores, amax, acc)
        divide_into(nc, g, acc, g.X)


STAGES = [capacity_ffn, relational_attention, switch_ffn, gcn_softmax, top2_gelu_ffn, gcn_residual, top2_relu_ffn]
UNUSED = ("L0_ffn_attention_mask",)


def column(a):
    return a.reshape(*a.shape[:-1], -1, P).swapaxes(-1, -2)


LAYOUT = {"L0_gnn_b1": column, "L0_ffn_b1": lambda a: column(a[None]), "L1_ffn_b1": column, "L2_ffn_b1": column,
          "L3_ffn_b1": column, "L2_ffn_ln_g": column, "L2_ffn_ln_b": column, "L3_gnn_W": lambda a: a.T}


LAST_STAGE = 8
FIRST_STAGE = 1


def build(nc, i, out):
    Phase.count, Phase.spent = 0, []
    with ExitStack() as stack:
        g = Shared()

        def sb(name, shape, dt=F32):
            return stack.enter_context(nc.sbuf_tensor(name, shape, dt))

        g.dram = lambda name, shape, dt=F32: nc.dram_tensor(name, shape, dt, kind="Internal").ap()
        g.X = sb("X", [P, T, D])
        g.iota_free, g.iota_part = sb("iota_free", [P, P]), sb("iota_part", [P, 1])
        g.ident, g.upto, g.before, g.ones = (sb(s, [P, P]) for s in ("ident", "upto", "before", "ones"))
        g.zero_row = sb("zero_row", [P, 512])
        g.dinv = sb("dinv", [P, T])
        g.chunk_tile = sb("chunk_tile", [1, EC], I32)
        g.src, g.hrow = sb("src", [P, EC], I32), sb("hrow", [P, EC], I32)
        g.dst, g.weight, g.etype = sb("dst", [P, EC]), sb("weight", [P, EC]), sb("etype", [P, EC])
        constants(nc, g, i["x"])
        sorted_rows = g.dram("sorted_rows", [P * EC, ROW])
        sort_edges(nc, g, i["src"], i["dst"], i["edge_type_8"], i["edge_weight"], i["edge_attr_32"], sorted_rows)
        g.attrs_t = sb("attrs_t", [P, EC // 4, P])
        load_sorted(nc, g, sorted_rows)
        if FIRST_STAGE == 1:
            gine_stack(nc, g, i)
        degrees(nc, g)
        for s, stage in enumerate(STAGES):
            if FIRST_STAGE <= s + 2 <= LAST_STAGE:
                stage(nc, g, i)
        store(nc, g.X, out)


def kernel(**inputs):
    import numpy as np
    import concourse.bacc as bacc
    from concourse.bass_utils import run_bass_kernel_spmd

    nc = bacc.Bacc("TRN2", target_bir_lowering=False, num_devices=1)
    arrays, aps = {}, {}
    for name, given in inputs.items():
        a = np.ascontiguousarray(given)
        if a.ndim == 0 or name in UNUSED:
            continue
        if name == "L1_gnn_W":
            inputs_turned = np.ascontiguousarray(a.transpose(0, 2, 1))
            arrays["in_L1_gnn_W_turned"] = inputs_turned
            aps["L1_gnn_W_turned"] = nc.dram_tensor("in_L1_gnn_W_turned", a.shape, F32, kind="ExternalInput").ap()
        if name in LAYOUT:
            a = np.ascontiguousarray(LAYOUT[name](a))
        arrays[f"in_{name}"] = a
        aps[name] = nc.dram_tensor(f"in_{name}", a.shape, mybir.dt.from_np(a.dtype), kind="ExternalInput").ap()
    out = nc.dram_tensor("out", (N, D), F32, kind="ExternalOutput").ap()
    build(nc, aps, out)
    r = run_bass_kernel_spmd(nc, [arrays], core_ids=[0])
    return r.results[0]["out"]
```

```python
from contextlib import ExitStack

import concourse.bass as bass
from concourse import mybir

F32 = mybir.dt.float32
I32 = mybir.dt.int32
BF16 = mybir.dt.bfloat16
ALU = mybir.AluOpType
ACT = mybir.ActivationFunctionType
AX = mybir.AxisListType

P = 128
N = 1875
D = 256
T = (N + P - 1) // P
NP = T * P
TAIL = N - (T - 1) * P
E = 31875
EP = 125
EJ = E // EP
EC = 264
ED = 32
ROW = 40
C_SRC, C_DST, C_W, C_HROW, C_TYPE = 32, 33, 34, 35, 36
R = 8
HD, DH = 8, 32
U = 12
G = 4
LAG = 4
LN_EPS = 1e-5
assert EP * EJ == E and EC * P >= E + T * (P - 1) and EC % U == 0 and U % G == 0


class Phase:

    count = 0
    spent = []
    branch = False

    def __init__(self, nc, name):
        Phase.count += 1
        self.nc, self.name, self.stack = nc, f"{name}{Phase.count}", ExitStack()

    def __enter__(self):
        return self

    def __exit__(self, *what):
        self.stack.close()
        if len(Phase.spent) > 90 and not Phase.branch:
            self.nc.clear_and_free_semaphores(Phase.spent)
            self.nc.all_engine_barrier(sem_only=True)
            Phase.spent.clear()

    def sb(self, name, shape, dt=F32):
        return self.stack.enter_context(self.nc.sbuf_tensor(f"{self.name}_{name}", shape, dt))

    def ps(self, name, shape, dt=F32):
        return self.stack.enter_context(self.nc.psum_tensor(f"{self.name}_{name}", shape, dt))

    def sem(self, name):
        Phase.spent.append(self.nc.alloc_semaphore(f"{self.name}_{name}"))
        return Phase.spent[-1]

    def block(self):
        return self.stack.enter_context(self.nc.Block())


class Shared:
    pass


def row(ap):
    return ap.partition_broadcast(P)


def constants(nc, g, x):
    with Phase(nc, "const") as ph:
        tail_zeroed, iota_made, loaded = ph.sem("tail_zeroed"), ph.sem("iota_made"), ph.sem("loaded")
        block = ph.block()

        @block.sync
        def _(sp):
            sp.dma_start(g.X[:, 0:T - 1, :], x[0:(T - 1) * P, :].rearrange("(t p) f -> p t f", p=P)).then_inc(loaded, 16)
            sp.wait_ge(tail_zeroed, 1)
            sp.dma_start(g.X[0:TAIL, T - 1, :], x[(T - 1) * P:N, :]).then_inc(loaded, 16)
            sp.wait_ge(loaded, 32)

        @block.gpsimd
        def _(pool):
            nc.gpsimd.iota(g.iota_free[:, :], [[1, P]], base=0, channel_multiplier=0,
                           allow_small_or_imprecise_dtypes=True).then_inc(iota_made, 1)
            nc.gpsimd.iota(g.iota_part[:, :], [[0, 1]], base=0, channel_multiplier=1,
                           allow_small_or_imprecise_dtypes=True).then_inc(iota_made, 1)

        @block.vector
        def _(v):
            nc.vector.memset(g.X[:, T - 1, :], 0.0).then_inc(tail_zeroed, 1)
            nc.vector.memset(g.ones[:, :], 1.0)
            nc.vector.memset(g.zero_row[:, :], 0.0)
            v.wait_ge(iota_made, 2)
            nc.vector.tensor_scalar(g.ident[:, :], g.iota_free[:, :], g.iota_part[:, 0:1], None, ALU.is_equal)
            nc.vector.tensor_scalar(g.ident_b[:, :], g.iota_free[:, :], g.iota_part[:, 0:1], None, ALU.is_equal)
            nc.vector.tensor_scalar(g.upto[:, :], g.iota_free[:, :], g.iota_part[:, 0:1], None, ALU.is_ge)
            nc.vector.tensor_scalar(g.before[:, :], g.iota_free[:, :], g.iota_part[:, 0:1], None, ALU.is_gt)


def sort_edges(nc, g, src, dst, etype, weight, attr, sorted_rows):
    with Phase(nc, "sort") as ph:
        src_i, dst_i, typ_i = (ph.sb(n, [EP, EJ], I32) for n in ("src_i", "dst_i", "typ_i"))
        wgt = ph.sb("wgt", [EP, EJ])
        stage = ph.sb("stage", [EP, EJ, ROW])
        blank = ph.sb("blank", [P, EC, ROW])
        tile_i, local_i = ph.sb("tile_i", [EP, EJ], I32), ph.sb("local_i", [EP, EJ], I32)
        tile_f = ph.sb("tile_f", [EP, EJ])
        member, rank = ph.sb("member", [EP, T, EJ]), ph.sb("rank", [EP, T, EJ])
        zeros = ph.sb("zeros", [EP, EJ])
        below = ph.sb("below", [EP, T])
        padded_i, padded = ph.sb("padded_i", [P, T], I32), ph.sb("padded", [P, T])
        end, base = ph.sb("end", [P, T]), ph.sb("base", [P, T])
        pos, pos_i = ph.sb("pos", [EP, EJ]), ph.sb("pos_i", [EP, EJ], I32)
        lane_i, chunk_i = ph.sb("lane_i", [EP, EJ], I32), ph.sb("chunk_i", [EP, EJ], I32)
        lane, slot_i = ph.sb("lane", [EP, EJ]), ph.sb("slot_i", [EP, EJ], I32)
        chunk0 = ph.sb("chunk0", [1, EC])
        passed, tile_of = ph.sb("passed", [1, EC, T]), ph.sb("tile_of", [1, EC])
        NB = 5
        out_row, out_slot = ph.sb("out_row", [EP, NB, ROW]), ph.sb("out_slot", [EP, NB], I32)
        p_below, p_total = ph.ps("p_below", [P, T]), ph.ps("p_total", [P, T])
        loaded, blanked, prefilled = ph.sem("loaded"), ph.sem("blanked"), ph.sem("prefilled")
        ranked, counted, placed = ph.sem("ranked"), ph.sem("counted"), ph.sem("placed")
        iota_made, turn = ph.sem("iota_made"), ph.sem("turn")
        row_ready, scattered = ph.sem("row_ready"), [ph.sem(f"scattered{u}") for u in range(NB)]
        block = ph.block()
        edges = "(p j) -> p j"

        @block.sync
        def _(sp):
            for tile, ap in ((dst_i, dst), (src_i, src), (typ_i, etype), (wgt, weight)):
                sp.dma_start(tile[:, :], ap.rearrange(edges, p=EP)).then_inc(loaded, 16)
            sp.dma_start(stage[:, :, 0:ED], attr.rearrange("(p j) c -> p j c", p=EP)).then_inc(loaded, 16)
            sp.wait_ge(blanked, 2)
            sp.dma_start(sorted_rows.rearrange("(p c) w -> p c w", p=P), blank[:, :, :]).then_inc(prefilled, 16)
            sp.wait_ge(prefilled, 16)

        @block.tensor
        def _(pe):
            pe.wait_ge(ranked, 1)
            nc.tensor.matmul(p_below[:, :], g.before[0:EP, :], rank[:, :, EJ - 1], start=True, stop=True)
            nc.tensor.matmul(p_total[:, :], g.ones[0:EP, :], rank[:, :, EJ - 1], start=True, stop=True).then_inc(counted, 1)

        @block.gpsimd
        def _(pool):
            nc.gpsimd.iota(chunk0[:, :], [[P, EC]], base=0, channel_multiplier=0,
                           allow_small_or_imprecise_dtypes=True).then_inc(iota_made, 1)
            nc.gpsimd.memset(blank[:, :, :], 0.0).then_inc(blanked, 1)
            pool.wait_ge(blanked, 1)
            nc.gpsimd.memset(blank[:, :, C_DST:C_DST + 1], -1.0).then_inc(blanked, 1)
            pool.wait_ge(prefilled, 16)
            with pool.Fori(0, EJ // NB) as i:
                for u in range(NB):
                    pool.wait_ge(row_ready, i * NB + u + 1)
                    pool.sem_inc(turn, 1)
                    pool.indirect_dma_start(sorted_rows, bass.IndirectOffsetOnAxis(ap=out_slot[:, u:u + 1], axis=0),
                                            out_row[:, u, :], None).then_inc(scattered[u], 16)
            for u in range(NB):
                pool.wait_ge(scattered[u], 16 * (EJ // NB))

        @block.vector
        def _(v):
            nc.vector.memset(zeros[:, :], 0.0)
            v.wait_ge(loaded, 80)
            nc.vector.tensor_scalar(tile_i[:, :], dst_i[:, :], 7, None, ALU.arith_shift_right)
            nc.vector.tensor_scalar(local_i[:, :], dst_i[:, :], P - 1, None, ALU.bitwise_and)
            v.drain()
            nc.vector.tensor_copy(tile_f[:, :], tile_i[:, :])
            nc.vector.tensor_copy(stage[:, :, C_DST], local_i[:, :])
            nc.vector.tensor_copy(stage[:, :, C_TYPE], typ_i[:, :])
            nc.vector.tensor_copy(stage[:, :, C_W], wgt[:, :])
            nc.vector.tensor_copy(stage[:, :, C_SRC].bitcast(I32), src_i[:, :])
            v.drain()
            nc.vector.scalar_tensor_tensor(stage[:, :, C_HROW].bitcast(I32), stage[:, :, C_TYPE], float(NP), src_i[:, :],
                                           ALU.mult, ALU.add)
            nc.vector.memset(stage[:, :, C_TYPE + 1:ROW], 0.0)
            for t in range(T):
                nc.vector.tensor_scalar(member[:, t, :], tile_f[:, :], float(t), None, ALU.is_equal)
            v.drain()
            for t in range(T):
                nc.vector.tensor_tensor_scan(rank[:, t, :], member[:, t, :], zeros[:, :], 0.0, ALU.add, ALU.add)
            v.drain()
            v.sem_inc(ranked, 1)
            v.wait_ge(counted, 1)
            nc.vector.tensor_scalar(padded_i[:, :], p_total[:, :], float(P - 1), None, ALU.add)
            v.drain()
            nc.vector.tensor_scalar(padded_i[:, :], padded_i[:, :], 7, 7, ALU.arith_shift_right, ALU.arith_shift_left)
            v.drain()
            nc.vector.tensor_copy(padded[:, :], padded_i[:, :])
            v.drain()
            nc.vector.tensor_tensor_scan(end[:, :], padded[:, :], g.zero_row[:, 0:T], 0.0, ALU.add, ALU.add)
            v.drain()
            nc.vector.tensor_tensor(base[:, :], end[:, :], padded[:, :], ALU.subtract)
            v.drain()
            nc.vector.scalar_tensor_tensor(below[:, :], p_below[0:EP, :], -1.0, base[0:EP, :], ALU.add, ALU.add)
            v.drain()
            for t in range(T):
                nc.vector.scalar_tensor_tensor(member[:, t, :], rank[:, t, :], below[:, t:t + 1], member[:, t, :],
                                               ALU.add, ALU.mult)
            v.drain()
            nc.vector.tensor_reduce(pos[:, :], member[:, :, :].rearrange("p t j -> p j t"), AX.X, ALU.add)
            v.drain()
            nc.vector.tensor_copy(pos_i[:, :], pos[:, :])
            v.drain()
            nc.vector.tensor_scalar(chunk_i[:, :], pos_i[:, :], 7, None, ALU.arith_shift_right)
            nc.vector.tensor_scalar(lane_i[:, :], pos_i[:, :], P - 1, None, ALU.bitwise_and)
            v.drain()
            nc.vector.tensor_copy(lane[:, :], lane_i[:, :])
            v.drain()
            nc.vector.scalar_tensor_tensor(slot_i[:, :], lane[:, :], float(EC), chunk_i[:, :], ALU.mult, ALU.add)
            v.wait_ge(iota_made, 1)
            nc.vector.tensor_tensor(passed[:, :, :], chunk0[:, :].unsqueeze(2).to_broadcast([1, EC, T]),
                                    end[0:1, :].unsqueeze(1).to_broadcast([1, EC, T]), ALU.is_ge)
            v.drain()
            nc.vector.tensor_reduce(tile_of[:, :], passed[:, :, :], AX.X, ALU.add)
            v.drain()
            nc.vector.tensor_scalar(g.chunk_tile[:, :], tile_of[:, :], float(T - 1), None, ALU.min)
            def fill(i):
                for u in range(NB):
                    if not isinstance(i, int):
                        v.wait_ge(scattered[u], i * 16)
                    nc.vector.tensor_copy(out_row[:, u, :], stage[:, bass.ds(i * NB + u, 1), :].rearrange("p a w -> p (a w)"))
                    nc.vector.tensor_copy(out_slot[:, u:u + 1], slot_i[:, bass.ds(i * NB + u, 1)])
                    v.drain()
                    v.sem_inc(row_ready, 1)

            v.drain()
            fill(0)
            with v.Fori(1, EJ // NB) as i:
                fill(i)


def split3(nc, eng, x, parts, left):
    nc.vector.tensor_copy(parts[0], x)
    eng.drain()
    nc.vector.tensor_tensor(left, x, parts[0], ALU.subtract)
    eng.drain()
    nc.vector.tensor_copy(parts[1], left)
    eng.drain()
    nc.vector.tensor_tensor(parts[2], left, parts[1], ALU.subtract)


def load_sorted(nc, g, sorted_rows):
    with Phase(nc, "unpack") as ph:
        B = EC // 2
        rows = ph.sb("rows", [P, B, ROW])
        left = ph.sb("left", [P, B, ED])
        parts = ph.sb("parts", [P, B, 4, ED], BF16)
        p_turned = [ph.ps(f"p_turned{b}", [P, 4, P], BF16) for b in range(8)]
        loaded, packed, turned = ph.sem("loaded"), ph.sem("packed"), ph.sem("turned")
        stored = [ph.sem("stored_a"), ph.sem("stored_v")]
        block = ph.block()
        batches = [(h, q) for h in range(2) for q in range(B // 4)]

        @block.sync
        def _(sp):
            view = sorted_rows.rearrange("(p c) w -> p c w", p=P)
            sp.dma_start(rows[:, :, :], view[:, 0:B, :]).then_inc(loaded, 16)
            sp.wait_ge(packed, 1)
            sp.dma_start(rows[:, :, :], view[:, B:EC, :]).then_inc(loaded, 16)

        def store(eng, copy, who, some):
            for n in some:
                if n % 2 != who:
                    continue
                h, q = batches[n]
                eng.wait_ge(turned, n + 1)
                c = h * B + 4 * q
                copy(g.attrs_t[:, c:c + 4, :], p_turned[n % 8][:, :, :]).then_inc(stored[who], 1)

        @block.vector
        def _(v):
            for h in range(2):
                v.wait_ge(loaded, 16 * (h + 1))
                if h:
                    v.wait_ge(turned, len(batches) // 2)
                a = rows[:, :, 0:ED]
                split3(nc, v, a, [parts[:, :, k, :] for k in range(3)], left[:, :, :])
                nc.vector.tensor_copy(parts[:, :, 3, :], a)
                half = slice(h * B, (h + 1) * B)
                nc.vector.tensor_copy(g.src[:, half], rows[:, :, C_SRC].bitcast(I32))
                nc.vector.tensor_copy(g.hrow[:, half], rows[:, :, C_HROW].bitcast(I32))
                nc.vector.tensor_copy(g.dst[:, half], rows[:, :, C_DST])
                nc.vector.tensor_copy(g.weight[:, half], rows[:, :, C_W])
                nc.vector.tensor_copy(g.etype[:, half], rows[:, :, C_TYPE])
                v.drain()
                v.sem_inc(packed, 1)
                store(v, nc.vector.tensor_copy, 1, range(h * B // 4, (h + 1) * B // 4))

        @block.tensor
        def _(pe):
            for n, (h, q) in enumerate(batches):
                pe.wait_ge(packed, h + 1)
                if n >= 8:
                    pe.wait_ge(stored[n % 2], (n - 8) // 2 + 1)
                for k in range(4):
                    ins = nc.tensor.transpose(p_turned[n % 8][:, k, :], parts[:, 4 * q + k, :, :].rearrange("p a w -> p (a w)"),
                                              g.ident_b[:, :])
                ins.then_inc(turned, 1)

        @block.scalar
        def _(act):
            store(act, nc.scalar.copy, 0, range(len(batches)))


def layernorm(nc, h, y, gamma=None, beta=None, relu=False, add=None, table=None, addrow=None):
    with Phase(nc, "ln") as ph:
        stats, mv = ph.sb("stats", [P, T, 6]), ph.sb("mv", [P, T, 2])
        var, std, rstd = ph.sb("var", [P, T]), ph.sb("std", [P, T]), ph.sb("rstd", [P, T])
        vec = ph.sb("vec", [P, 3, D])
        rows = ph.sb("rows", [P, T, D]) if addrow is not None else y
        loaded, var_ready, std_ready = ph.sem("loaded"), ph.sem("var_ready"), ph.sem("std_ready")
        rows_ready, written = ph.sem("rows_ready"), ph.sem("written")
        block = ph.block()
        wide = [P, T, D]
        given = [(i, a) for i, a in enumerate((gamma, beta, addrow)) if a is not None]

        @block.sync
        def _(sp):
            for i, a in given:
                sp.dma_start(vec[:, i, :], row(a)).then_inc(loaded, 16)
            if table is not None:
                sp.wait_ge(rows_ready, 1)
                sp.dma_start(table.rearrange("(t p) f -> p t f", p=P), rows[:, :, :]).then_inc(written, 16)
                sp.wait_ge(written, 16)

        @block.scalar
        def _(act):
            act.wait_ge(var_ready, 1)
            nc.scalar.activation(std[:, :], var[:, :], ACT.Sqrt).then_inc(std_ready, 1)

        @block.vector
        def _(v):
            for t in range(T):
                nc.vector.bn_stats(stats[:, t, :], h[:, t, :])
            v.drain()
            for t in range(T):
                nc.vector.bn_aggr(mv[:, t, :], stats[:, t, :])
            v.drain()
            nc.vector.tensor_scalar(var[:, :], mv[:, :, 1], LN_EPS, None, ALU.add).then_inc(var_ready, 1)
            v.wait_ge(std_ready, 1)
            nc.vector.reciprocal(rstd[:, :], std[:, :])
            v.drain()
            for t in range(T):
                nc.vector.tensor_scalar(y[:, t, :], h[:, t, :], mv[:, t, 0:1], rstd[:, t:t + 1], ALU.subtract, ALU.mult)
            if given:
                v.wait_ge(loaded, 16 * len(given))
            if gamma is not None:
                v.drain()
                nc.vector.tensor_tensor(y[:, :, :], y[:, :, :], vec[:, 0, :].unsqueeze(1).to_broadcast(wide), ALU.mult)
                v.drain()
                nc.vector.tensor_tensor(y[:, :, :], y[:, :, :], vec[:, 1, :].unsqueeze(1).to_broadcast(wide), ALU.add)
            if relu:
                v.drain()
                nc.vector.tensor_scalar(y[:, :, :], y[:, :, :], 0.0, None, ALU.max)
            v.drain()
            if addrow is not None:
                nc.vector.tensor_tensor(rows[:, :, :], y[:, :, :], vec[:, 2, :].unsqueeze(1).to_broadcast(wide), ALU.add)
                v.drain()
            v.sem_inc(rows_ready, 1)
            if add is not None:
                nc.vector.tensor_tensor(add[:, :, :], add[:, :, :], y[:, :, :], ALU.add)


def self_terms(nc, g, y, acc, eps=None):
    with Phase(nc, "self") as ph:
        scale, scaled = ph.sb("scale", [P, 1]), ph.sb("scaled", [P, P])
        banks = (T + 1) // 2
        p_turned = ph.ps("p_turned", [P, banks, 2, 2, P])
        loaded, scaled_ready, turned = ph.sem("loaded"), ph.sem("scaled_ready"), ph.sem("turned")
        block = ph.block()

        @block.sync
        def _(sp):
            if eps is not None:
                sp.dma_start(scale[:, :], row(eps)).then_inc(loaded, 16)

        @block.vector
        def _(v):
            if eps is not None:
                v.wait_ge(loaded, 16)
                nc.vector.tensor_scalar(scale[:, :], scale[:, :], 1.0, None, ALU.add)
                v.drain()
                nc.vector.tensor_scalar(scaled[:, :], g.ident[:, :], scale[:, 0:1], None, ALU.mult).then_inc(scaled_ready, 1)
            for b in range(1, banks, 2):
                v.wait_ge(turned, b + 1)
                n = min(2, T - 2 * b)
                nc.vector.tensor_copy(acc[:, 2 * b:2 * b + n, :, :], p_turned[:, b, 0:n, :, :])

        @block.scalar
        def _(act):
            for b in range(0, banks, 2):
                act.wait_ge(turned, b + 1)
                n = min(2, T - 2 * b)
                nc.scalar.copy(acc[:, 2 * b:2 * b + n, :, :], p_turned[:, b, 0:n, :, :])

        @block.tensor
        def _(pe):
            if eps is not None:
                pe.wait_ge(scaled_ready, 1)
            diag = g.ident if eps is None else scaled
            for t in range(T):
                for half in range(2):
                    ins = nc.tensor.matmul(p_turned[:, t // 2, t % 2, half, :], y[:, t, half * P:(half + 1) * P], diag[:, :],
                                           start=True, stop=True)
                if t % 2 or t == T - 1:
                    ins.then_inc(turned, 1)


def tiles_of(eng, g, registers, i):
    eng.load(registers, g.chunk_tile[0:1, bass.ds(i * U, U)])
    return [eng.snap(r, min_val=0, max_val=T - 1) for r in registers]


def gather_loop(nc, pool, ph, rows, table, got, idx, gathered, freed, idx_set, turn):
    with pool.Fori(0, EC // U) as i:
        for b in range(U // G):
            pool.wait_ge(freed, i * U + G * (b + 1))
            pool.sem_inc(turn, 1)
            nc.gpsimd.tensor_copy(idx[:, b * G:(b + 1) * G], rows[:, bass.ds(i * U + b * G, G)]).then_inc(idx_set, 1)
            pool.wait_ge(idx_set, i * (U // G) + (b + 1))
            pool.sem_inc(turn, 1)
            for u in range(b * G, (b + 1) * G):
                pool.indirect_dma_start(got[:, u, :], None, table,
                                        bass.IndirectOffsetOnAxis(ap=idx[:, u:u + 1], axis=0)).then_inc(gathered[u], 16)


def add_loop(nc, v, g, ph, each, add):
    registers = [v.alloc_register(f"{ph.name}_tile{u}") for u in range(U)]

    def tail(i):
        last = [v.snap(r, min_val=0, max_val=T - 1) for r in registers[U - LAG:]]
        return lambda n: add(i, n - LAG, last[n])

    def one_pass(i):
        left = tail(i) if not isinstance(i, int) else None
        for u in range(U):
            each(i, u)
            if u < LAG and left:
                left(u)
            if u == LAG - 1:
                tiles = tiles_of(v, g, registers, i)
            if u >= LAG:
                add(i, u - LAG, tiles[u - LAG])

    one_pass(0)
    with v.Fori(1, EC // U) as i:
        one_pass(i)
    left = tail(EC // U)
    for n in range(LAG):
        left(n)
    v.drain()


def lagged(eng, ahead, behind, lag):
    def one_pass(i):
        for u in range(U):
            ahead(i, u)
            if u >= lag or not isinstance(i, int):
                behind(i, u - lag)

    one_pass(0)
    with eng.Fori(1, EC // U) as i:
        one_pass(i)
    for u in range(lag):
        behind(EC // U, u - lag)


def gine_edges(nc, g, table, edge_w, acc):
    with Phase(nc, "gine") as ph:
        ew, left = ph.sb("ew", [P, D]), ph.sb("left", [P, D])
        parts = ph.sb("parts", [P, 3, D], BF16)
        w_a, w_b = ph.sb("w_a", [P, D], BF16), ph.sb("w_b", [P, D], BF16)
        idx = ph.sb("idx", [P, U], I32)
        got = ph.sb("got", [P, U, D])
        hot = ph.sb("hot", [P, U, P])
        msg = ph.sb("msg", [P, U, D])
        p_edge = [ph.ps(f"p_edge{b}", [P, 512]) for b in range(4)]
        p_sum = [ph.ps(f"p_sum{b}", [P, 512]) for b in range(4)]
        loaded, split, idx_set, turn = ph.sem("loaded"), ph.sem("split"), ph.sem("idx_set"), ph.sem("turn")
        gathered = [ph.sem(f"gathered{u}") for u in range(U)]
        edge_done, summed, msg_ready, hot_ready = ph.sem("edge_done"), ph.sem("summed"), ph.sem("msg_ready"), ph.sem("hot_ready")
        agg_done, added = ph.sem("agg_done"), ph.sem("added")
        block = ph.block()

        @block.sync
        def _(sp):
            for q in range(4):
                sp.dma_start(ew[q * ED:(q + 1) * ED, :], edge_w).then_inc(loaded, 16)
            for s in (summed, agg_done, added, msg_ready):
                sp.sem_inc(s, U)

        @block.gpsimd
        def _(pool):
            gather_loop(nc, pool, ph, g.src, table, got, idx, gathered, msg_ready, idx_set, turn)

        @block.tensor
        def _(pe):
            pe.wait_ge(split, 1)

            def edge(i, u):
                pe.wait_ge(summed, i * U + (u - 4 + 1 + U))
                a = g.attrs_t[:, bass.ds(i * U + u, 1), :].rearrange("p a e -> p (a e)")
                nc.tensor.matmul(p_edge[u % 4][:, 0:D], a, w_a[:, :], start=True, stop=False)
                nc.tensor.matmul(p_edge[u % 4][:, 0:D], a, w_b[:, :], start=False, stop=True).then_inc(edge_done, 1)

            def aggregate(i, u):
                pe.wait_ge(hot_ready, i * U + (u + 1))
                pe.wait_ge(added, i * U + (u - 4 + 1 + U))
                pe.wait_ge(msg_ready, i * U + (u + 1 + U))
                for half in range(2):
                    ins = nc.tensor.matmul(p_sum[u % 4][:, half * P:(half + 1) * P], msg[:, u % U, half * P:(half + 1) * P],
                                           hot[:, u % U, :], start=True, stop=True)
                ins.then_inc(agg_done, 1)

            lagged(pe, edge, aggregate, 3)

        @block.scalar
        def _(act):
            with act.Fori(0, EC // U) as i:
                for u in range(U):
                    act.wait_ge(agg_done, i * U + (u + 1))
                    act.wait_ge(summed, i * U + (u + 1 + U))
                    nc.scalar.activation(msg[:, u, :], got[:, u, :], ACT.Relu).then_inc(msg_ready, 1)

        @block.vector
        def _(v):
            v.wait_ge(loaded, 64)
            split3(nc, v, ew[:, :], [parts[:, k, :] for k in range(3)], left[:, :])
            nc.vector.memset(w_b[:, :], 0.0)
            v.drain()
            for q, part in enumerate((0, 0, 0, 1)):
                nc.vector.tensor_copy(w_a[q * ED:(q + 1) * ED, :], parts[q * ED:(q + 1) * ED, part, :])
            for q, part in enumerate((2, 1)):
                nc.vector.tensor_copy(w_b[q * ED:(q + 1) * ED, :], parts[q * ED:(q + 1) * ED, part, :])
            v.drain()
            v.sem_inc(split, 1)

            def each(i, u):
                v.wait_ge(agg_done, i * U + (u + 1))
                nc.vector.tensor_scalar(hot[:, u, :], g.iota_free[:, :], g.dst[:, bass.ds(i * U + u, 1)], None,
                                        ALU.is_equal).then_inc(hot_ready, 1)
                v.wait_ge(edge_done, i * U + (u + 1))
                v.wait_ge(gathered[u], i * 16 + 16)
                nc.vector.tensor_tensor(got[:, u, :], got[:, u, :], p_edge[u % 4][:, 0:D], ALU.add).then_inc(summed, 1)

            def add(i, u, tile):
                v.wait_ge(added, i * U + (u + U))
                v.wait_ge(agg_done, i * U + (u + 1 + U))
                a = acc[:, bass.ds(tile, 1), :, :].rearrange("p a h n -> p (a h n)")
                nc.vector.tensor_tensor(a, a, p_sum[u % 4][:, 0:D], ALU.add).then_inc(added, 1)

            add_loop(nc, v, g, ph, each, add)


def gine_mlp(nc, g, agg, h, w1, b1, w2, b2, first):
    with Phase(nc, "mlp") as ph:
        w1_sb, w2_sb = ph.sb("w1", [P, 2, D]), ph.sb("w2", [P, 2, D])
        b1_sb, b2_row = ph.sb("b1", [P, 2]), ph.sb("b2", [P, D])
        z = ph.sb("z", [P, 2, T, P])
        p_z = [ph.ps(f"p_z{b}", [P, 4, P]) for b in range(4)]
        p_h = [ph.ps(f"p_h{b}", [P, 512]) for b in range(4)]
        loaded, z_done, z_ready, h_done, h_added = (ph.sem(s) for s in ("loaded", "z_done", "z_ready", "h_done", "h_added"))
        block = ph.block()
        groups = [(t, min(4, T - t)) for t in range(0, T, 4)]
        steps = [(t, k, m) for t, k in groups for m in range(2)]

        @block.sync
        def _(sp):
            sp.dma_start(w1_sb[:, :, :], w1.rearrange("(k p) n -> p k n", p=P)).then_inc(loaded, 16)
            sp.dma_start(w2_sb[:, :, :], w2.rearrange("(k p) n -> p k n", p=P)).then_inc(loaded, 16)
            sp.dma_start(b1_sb[:, :], b1).then_inc(loaded, 16)
            sp.dma_start(b2_row[:, :], row(b2)).then_inc(loaded, 16)

        @block.tensor
        def _(pe):
            pe.wait_ge(loaded, 64)
            for s, (t, n, m) in enumerate(steps):
                if s >= 4:
                    pe.wait_ge(z_ready, s - 3)
                for k in range(2):
                    ins = nc.tensor.matmul(p_z[s % 4][:, 0:n, :], w1_sb[:, k, m * P:(m + 1) * P], agg[:, t:t + n, k, :],
                                           start=(k == 0), stop=(k == 1))
                ins.then_inc(z_done, 1)
            for t in range(T):
                pe.wait_ge(z_ready, 2 * (t // 4 + 1))
                if t >= 4:
                    pe.wait_ge(h_added, t - 3)
                for k in range(2):
                    ins = nc.tensor.matmul(p_h[t % 4][:, 0:D], z[:, k, t, :], w2_sb[:, k, :], start=(k == 0), stop=(k == 1))
                ins.then_inc(h_done, 1)

        @block.scalar
        def _(act):
            act.wait_ge(loaded, 64)
            for s, (t, n, m) in enumerate(steps):
                act.wait_ge(z_done, s + 1)
                nc.scalar.activation(z[:, m, t:t + n, :], p_z[s % 4][:, 0:n, :], ACT.Relu, bias=b1_sb[:, m:m + 1]).then_inc(z_ready, 1)

        @block.vector
        def _(v):
            v.wait_ge(loaded, 64)
            if not first:
                nc.vector.tensor_tensor(h[:, :, :], h[:, :, :], b2_row[:, :].unsqueeze(1).to_broadcast([P, T, D]), ALU.add)
                v.drain()
            for t in range(T):
                v.wait_ge(h_done, t + 1)
                nc.vector.tensor_tensor(h[:, t, :], p_h[t % 4][:, 0:D], b2_row[:, :] if first else h[:, t, :],
                                        ALU.add).then_inc(h_added, 1)


def store(nc, x, out):
    with Phase(nc, "store") as ph:
        written = ph.sem("written")
        block = ph.block()

        @block.sync
        def _(sp):
            sp.dma_start(out[0:(T - 1) * P, :].rearrange("(t p) f -> p t f", p=P), x[:, 0:T - 1, :]).then_inc(written, 16)
            sp.dma_start(out[(T - 1) * P:N, :], x[0:TAIL, T - 1, :]).then_inc(written, 16)
            sp.wait_ge(written, 32)


def gine_stack(nc, g, i):
    with Phase(nc, "stack") as ph:
        h, y, acc = ph.sb("h", [P, T, D]), ph.sb("y", [P, T, D]), ph.sb("acc", [P, T, 2, P])
        L = i["L0_gnn_W1"].shape[0]
        for k in range(L):
            table = g.dram(f"gine_table{k}", [NP, D])
            if k == 0:
                layernorm(nc, g.X, y, table=table, addrow=i["L0_gnn_eb"][k, :])
            else:
                layernorm(nc, h, y, gamma=i["L0_gnn_gamma"][k, :], beta=i["L0_gnn_beta"][k, :], relu=True,
                          table=table, addrow=i["L0_gnn_eb"][k, :])
            self_terms(nc, g, y, acc, eps=i["L0_gnn_eps"][k:k + 1])
            gine_edges(nc, g, table, i["L0_gnn_eW"][k, :, :], acc)
            gine_mlp(nc, g, acc, h, i["L0_gnn_W1"][k, :, :], i["L0_gnn_b1"][k, :, :], i["L0_gnn_W2"][k, :, :],
                     i["L0_gnn_b2"][k, :], first=(k == 0))
        layernorm(nc, h, y, gamma=i["L0_gnn_gamma"][0, :], beta=i["L0_gnn_beta"][0, :], relu=True, add=g.X)


class Routes:

    def __init__(self, ph, k, blocks):
        self.slot, self.gate = ph.sb("slot", [P, k, T], I32), ph.sb("gate", [P, k, T])
        self.expert = ph.sb("expert", [1, blocks], I32)
        self.blocks, self.choices = blocks, k


def rank_tokens(nc, g, xn, wr, br, chosen, r):
    weights = g.dram("router_weights", [NP])
    last = r.blocks * P - 1
    with Phase(nc, "rank") as ph:
        prod, wr_row, br_col = ph.sb("prod", [P, T, D]), ph.sb("wr", [P, D]), ph.sb("br", [P, 1])
        w, turned, every = ph.sb("w", [P, T]), ph.sb("turned", [P, P]), ph.sb("every", [P, NP])
        junk, valid, gone = ph.sb("junk", [P, NP]), ph.sb("valid", [P, 1]), ph.sb("gone", [P, 1])
        lower, over, above, ties = ph.sb("lower", [P, P]), ph.sb("over", [P, T]), ph.sb("above", [P, T]), ph.sb("ties", [P, T])
        rank = ph.sb("rank", [P, T])
        p_turned = ph.ps("p_turned", [T, P])
        loaded, w_ready, w_turned, w_copied = (ph.sem(s) for s in ("loaded", "w_ready", "w_turned", "w_copied"))
        w_written, w_spread = ph.sem("w_written"), ph.sem("w_spread")
        block = ph.block()

        @block.sync
        def _(sp):
            sp.dma_start(wr_row[:, :], row(wr)).then_inc(loaded, 16)
            sp.dma_start(br_col[:, :], row(br)).then_inc(loaded, 16)
            sp.wait_ge(w_copied, 1)
            sp.dma_start(weights.rearrange("(t p) -> t p", p=P), turned[0:T, :]).then_inc(w_written, 16)
            sp.wait_ge(w_written, 16)
            sp.dma_start(every[:, :], row(weights)).then_inc(w_spread, 16)

        @block.tensor
        def _(pe):
            pe.wait_ge(w_ready, 1)
            nc.tensor.transpose(p_turned[:, :], w[:, :], g.ident[:, :]).then_inc(w_turned, 1)

        @block.vector
        def _(v):
            nc.vector.tensor_scalar(lower[:, :], g.iota_free[:, :], g.iota_part[:, 0:1], None, ALU.is_lt)
            nc.vector.tensor_scalar(valid[:, :], g.iota_part[:, :], float(TAIL), None, ALU.is_lt)
            nc.vector.tensor_scalar(gone[:, :], g.iota_part[:, :], float(TAIL), -3e38, ALU.is_ge, ALU.mult)
            v.wait_ge(loaded, 32)
            nc.vector.tensor_tensor(prod[:, :, :], xn[:, :, :], wr_row[:, :].unsqueeze(1).to_broadcast([P, T, D]), ALU.mult)
            v.drain()
            nc.vector.tensor_reduce(w[:, :], prod[:, :, :], AX.X, ALU.add)
            v.drain()
            nc.vector.tensor_scalar(w[:, :], w[:, :], br_col[:, 0:1], None, ALU.add)
            v.drain()
            nc.vector.tensor_scalar(w[:, T - 1:T], w[:, T - 1:T], valid[:, 0:1], gone[:, 0:1], ALU.mult, ALU.add).then_inc(w_ready, 1)
            v.wait_ge(w_turned, 1)
            nc.vector.tensor_copy(turned[0:T, :], p_turned[:, :]).then_inc(w_copied, 1)
            v.wait_ge(w_spread, 16)
            nc.vector.memset(over[:, 0:1], 0.0)
            for t in range(T):
                if t:
                    nc.vector.tensor_scalar(junk[:, 0:t * P], every[:, 0:t * P], w[:, t:t + 1], 0.0, ALU.is_ge, ALU.add,
                                            accum_out=over[:, t:t + 1])
                nc.vector.tensor_scalar(junk[:, t * P:NP], every[:, t * P:NP], w[:, t:t + 1], 0.0, ALU.is_gt, ALU.add,
                                        accum_out=above[:, t:t + 1])
                v.drain()
                nc.vector.scalar_tensor_tensor(junk[:, 0:P], every[:, t * P:(t + 1) * P], w[:, t:t + 1], lower[:, :],
                                               ALU.is_equal, ALU.mult, accum_out=ties[:, t:t + 1])
                v.drain()
            nc.vector.tensor_tensor(rank[:, :], over[:, :], above[:, :], ALU.add)
            v.drain()
            nc.vector.tensor_tensor(rank[:, :], rank[:, :], ties[:, :], ALU.add)
            v.drain()
            nc.vector.tensor_copy(r.slot[:, 0, :], rank[:, :])
            nc.vector.tensor_scalar(r.source[:, :], rank[:, :], float(last), None, ALU.min)
            nc.vector.scalar_tensor_tensor(r.gate[:, 0, :], rank[:, :], float(chosen), w[:, :], ALU.is_lt, ALU.mult)


def choose_experts(nc, g, xt, gate_w, gate_b, r, capacity=None):
    ne, k_all, nb = gate_w.shape[1], r.choices, r.blocks
    with Phase(nc, "route") as ph:
        gw, gb = ph.sb("gw", [P, 2, ne]), ph.sb("gb", [P, ne])
        lg, eq, e_idx = ph.sb("lg", [P, T, ne]), ph.sb("eq", [P, T, ne]), ph.sb("e_idx", [P, ne])
        top, first = ph.sb("top", [P, k_all, T]), ph.sb("first", [P, T])
        hot = ph.sb("hot", [P, k_all, T, ne])
        ex, total = ph.sb("ex", [P, T, ne]), ph.sb("total", [P, T])
        count = [ph.sb(f"count{b}", [P, k_all * T, ne]) for b in range(2)]
        before, place = ph.sb("before", [P, k_all * T, ne]), ph.sb("place", [P, k_all * T, ne])
        padded_i, padded, end, base = ph.sb("padded_i", [P, ne], I32), ph.sb("padded", [P, ne]), ph.sb("end", [P, ne]), ph.sb("base", [P, ne])
        slot, pos = ph.sb("slot_f", [P, k_all * T]), ph.sb("pos", [P, k_all * T])
        block0, passed, owner = ph.sb("block0", [1, nb]), ph.sb("passed", [1, nb, ne]), ph.sb("owner", [1, nb])
        p_lg = ph.ps("p_lg", [P, T, ne])
        p_in, p_all = ph.ps("p_in", [P, k_all * T, ne]), ph.ps("p_all", [P, k_all * T, ne])
        loaded, iota_made, lg_done, ex_in, ex_done = (ph.sem(s) for s in ("loaded", "iota_made", "lg_done", "ex_in", "ex_done"))
        hot_ready, counted = ph.sem("hot_ready"), ph.sem("counted")
        block = ph.block()
        big = 1000.0
        wide = [P, T, ne]

        @block.sync
        def _(sp):
            sp.dma_start(gw[:, :, :], gate_w.rearrange("(k p) e -> p k e", p=P)).then_inc(loaded, 16)
            sp.dma_start(gb[:, :], row(gate_b)).then_inc(loaded, 16)

        @block.gpsimd
        def _(pool):
            nc.gpsimd.iota(e_idx[:, :], [[1, ne]], base=0, channel_multiplier=0,
                           allow_small_or_imprecise_dtypes=True).then_inc(iota_made, 1)
            nc.gpsimd.iota(block0[:, :], [[P, nb]], base=0, channel_multiplier=0,
                           allow_small_or_imprecise_dtypes=True).then_inc(iota_made, 1)

        @block.tensor
        def _(pe):
            pe.wait_ge(loaded, 32)
            for t in range(T):
                for k in range(2):
                    ins = nc.tensor.matmul(p_lg[:, t, :], xt[:, t, k, :], gw[:, k, :], start=(k == 0), stop=(k == 1))
            ins.then_inc(lg_done, 1)
            pe.wait_ge(hot_ready, 1)
            flat = hot[:, :, :, :].rearrange("p k t e -> p (k t e)")
            nc.tensor.matmul(p_in[:, :, :].rearrange("p a e -> p (a e)"), g.upto[:, :], flat, start=True, stop=True)
            nc.tensor.matmul(p_all[:, :, :].rearrange("p a e -> p (a e)"), g.ones[:, :], flat, start=True, stop=True).then_inc(counted, 1)

        @block.scalar
        def _(act):
            act.wait_ge(ex_in, 1)
            if k_all == 1:
                nc.scalar.activation(ex[:, :, :], ex[:, :, :], ACT.Exp).then_inc(ex_done, 1)
            else:
                nc.scalar.activation(total[:, :], total[:, :], ACT.Exp).then_inc(ex_done, 1)

        @block.vector
        def _(v):
            v.wait_ge(loaded, 32)
            v.wait_ge(lg_done, 1)
            nc.vector.tensor_tensor(lg[:, :, :], p_lg[:, :, :], gb[:, :].unsqueeze(1).to_broadcast(wide), ALU.add)
            v.wait_ge(iota_made, 2)
            nc.vector.tensor_scalar(e_idx[:, :], e_idx[:, :], -big, None, ALU.add)
            v.drain()
            for k in range(k_all):
                nc.vector.tensor_reduce(top[:, k, :], lg[:, :, :], AX.X, ALU.max)
                v.drain()
                if k_all == 1:
                    nc.vector.tensor_tensor(ex[:, :, :], lg[:, :, :], top[:, k, :].unsqueeze(2).to_broadcast(wide),
                                            ALU.subtract)
                nc.vector.tensor_tensor(eq[:, :, :], lg[:, :, :], top[:, k, :].unsqueeze(2).to_broadcast(wide), ALU.not_equal)
                v.drain()
                nc.vector.scalar_tensor_tensor(eq[:, :, :], eq[:, :, :], big, e_idx[:, :].unsqueeze(1).to_broadcast(wide),
                                               ALU.mult, ALU.add)
                v.drain()
                nc.vector.tensor_reduce(first[:, :], eq[:, :, :], AX.X, ALU.min)
                v.drain()
                nc.vector.tensor_tensor(hot[:, k, :, :], e_idx[:, :].unsqueeze(1).to_broadcast(wide),
                                        first[:, :].unsqueeze(2).to_broadcast(wide), ALU.is_equal)
                v.drain()
                if k + 1 < k_all:
                    nc.vector.scalar_tensor_tensor(lg[:, :, :], hot[:, k, :, :], -1e30, lg[:, :, :], ALU.mult, ALU.add)
                    v.drain()
            if k_all == 2:
                nc.vector.tensor_tensor(total[:, :], top[:, 1, :], top[:, 0, :], ALU.subtract)
                v.drain()
            v.sem_inc(ex_in, 1)
            v.sem_inc(hot_ready, 1)
            v.wait_ge(ex_done, 1)
            if k_all == 1:
                nc.vector.tensor_reduce(total[:, :], ex[:, :, :], AX.X, ALU.add)
                v.drain()
                nc.vector.reciprocal(r.gate[:, 0, :], total[:, :])
            else:
                nc.vector.tensor_scalar(first[:, :], total[:, :], 1.0, None, ALU.add)
                v.drain()
                nc.vector.reciprocal(r.gate[:, 0, :], first[:, :])
                v.drain()
                nc.vector.tensor_tensor(r.gate[:, 1, :], total[:, :], r.gate[:, 0, :], ALU.mult)
            v.wait_ge(counted, 1)
            kt = k_all * T
            nc.vector.tensor_copy(count[0][:, :, :], p_all[:, :, :])
            v.drain()
            s, a = 1, 0
            while s < kt:
                nc.vector.tensor_tensor(count[1 - a][:, s:kt, :], count[a][:, s:kt, :], count[a][:, 0:kt - s, :], ALU.add)
                nc.vector.tensor_copy(count[1 - a][:, 0:s, :], count[a][:, 0:s, :])
                v.drain()
                s, a = 2 * s, 1 - a
            nc.vector.tensor_tensor(before[:, :, :], count[a][:, :, :], p_all[:, :, :], ALU.subtract)
            nc.vector.tensor_scalar(padded_i[:, :], count[a][:, kt - 1, :], float(P - 1), None, ALU.add)
            v.drain()
            nc.vector.tensor_scalar(padded_i[:, :], padded_i[:, :], 7, 7, ALU.arith_shift_right, ALU.arith_shift_left)
            v.drain()
            nc.vector.tensor_copy(padded[:, :], padded_i[:, :])
            v.drain()
            nc.vector.tensor_tensor_scan(end[:, :], padded[:, :], g.zero_row[:, 0:ne], 0.0, ALU.add, ALU.add)
            nc.vector.scalar_tensor_tensor(place[:, :, :], p_in[:, :, :], -1.0, before[:, :, :], ALU.add, ALU.add)
            v.drain()
            nc.vector.tensor_tensor(base[:, :], end[:, :], padded[:, :], ALU.subtract)
            if capacity is not None:
                nc.vector.tensor_tensor(eq[:, :, :], place[:, :, :], hot[:, 0, :, :], ALU.mult)
                v.drain()
                nc.vector.tensor_reduce(pos[:, :], eq[:, :, :], AX.X, ALU.add)
                v.drain()
                nc.vector.scalar_tensor_tensor(r.gate[:, 0, :], pos[:, :], float(capacity), r.gate[:, 0, :], ALU.is_lt, ALU.mult)
            v.drain()
            nc.vector.tensor_tensor(place[:, :, :], place[:, :, :], base[:, :].unsqueeze(1).to_broadcast([P, kt, ne]), ALU.add)
            v.drain()
            nc.vector.tensor_tensor(place[:, :, :], place[:, :, :], hot[:, :, :, :].rearrange("p k t e -> p (k t) e"), ALU.mult)
            v.drain()
            nc.vector.tensor_reduce(slot[:, :], place[:, :, :], AX.X, ALU.add)
            v.drain()
            nc.vector.tensor_copy(r.slot[:, :, :].rearrange("p k t -> p (k t)"), slot[:, :])
            nc.vector.tensor_tensor(passed[:, :, :], block0[:, :].unsqueeze(2).to_broadcast([1, nb, ne]),
                                    end[0:1, :].unsqueeze(1).to_broadcast([1, nb, ne]), ALU.is_ge)
            v.drain()
            nc.vector.tensor_reduce(owner[:, :], passed[:, :, :], AX.X, ALU.add)
            v.drain()
            nc.vector.tensor_scalar(r.expert[:, :], owner[:, :], float(ne - 1), None, ALU.min)


def scatter_tokens(nc, g, rows, r, slots, fill):
    with Phase(nc, "spread") as ph:
        blank = ph.sb("blank", [P, D])
        blanked, filled, sent = ph.sem("blanked"), ph.sem("filled"), ph.sem("sent")
        block = ph.block()
        nb = slots.shape[0] // P

        @block.sync
        def _(sp):
            if fill:
                sp.wait_ge(blanked, 1)
                sp.dma_start(slots.rearrange("(b p) f -> p b f", p=P), blank[:, :].unsqueeze(1).to_broadcast([P, nb, D])).then_inc(filled, 16)

        @block.vector
        def _(v):
            nc.vector.memset(blank[:, :], 0.0).then_inc(blanked, 1)

        @block.gpsimd
        def _(pool):
            if fill:
                pool.wait_ge(filled, 16)
            for k in range(r.choices):
                for t in range(T):
                    pool.indirect_dma_start(slots, bass.IndirectOffsetOnAxis(ap=r.slot[:, k, t:t + 1], axis=0),
                                            rows[:, t, :], None).then_inc(sent, 16)
            pool.wait_ge(sent, 16 * r.choices * T)


def expert_blocks(nc, g, slots, results, r, w1, b1, w2, b2, func, affine=None):
    ne, _, fm = w1.shape
    m_all = fm // P
    banks = m_all // 4
    nb = r.blocks
    assert nb % 2 == 0
    with Phase(nc, "ffn") as ph:
        x = ph.sb("x", [P, 2, D])
        w1_sb, w2_sb = ph.sb("w1", [P, 2, 2, fm]), ph.sb("w2", [P, 2, m_all, D])
        b1_sb, b2_sb, aff = ph.sb("b1", [P, 2, m_all]), ph.sb("b2", [P, 2, D]), ph.sb("aff", [P, 2, 4])
        xt = ph.sb("xt", [P, 2, 2, P])
        ht = ph.sb("ht", [P, 2, m_all, P])
        y = ph.sb("y", [P, 2, D])
        p_x = [ph.ps(f"p_x{u}", [P, 2, 2, P]) for u in range(2)]
        p_h = [[ph.ps(f"p_h{u}{b}", [P, 4, P]) for b in range(2)] for u in range(2)]
        p_y = [ph.ps(f"p_y{u}", [P, 512]) for u in range(2)]
        x_in, w1_in, w2_in = ([ph.sem(f"{s}{u}") for u in range(2)] for s in ("x_in", "w1_in", "w2_in"))
        turned, xt_ready, h_done, h_ready, y_done, y_ready = (ph.sem(s) for s in ("turned", "xt_ready", "h_done", "h_ready", "y_done", "y_ready"))
        stored = [ph.sem(f"stored{u}") for u in range(2)]
        turn, y_free = ph.sem("turn"), ph.sem("y_free")
        block = ph.block()
        n_w1 = 2 if affine is None else 4

        @block.sync
        def _(sp):
            sp.sem_inc(h_ready, 2 * banks)
            sp.sem_inc(y_done, 2)
            sp.sem_inc(y_ready, 2)
            sp.sem_inc(y_free, 2)
            registers = [sp.alloc_register(f"{ph.name}_expert{u}") for u in range(2)]
            with sp.Fori(0, nb // 2) as i:
                if ne > 1:
                    sp.load(registers, r.expert[0:1, bass.ds(i * 2, 2)])
                    experts = [sp.snap(e, min_val=0, max_val=ne - 1) for e in registers]
                else:
                    experts = [0, 0]
                for u in range(2):
                    one = bass.ds(experts[u], 1)
                    sp.wait_ge(h_ready, i * (2 * banks) + (u + 1) * banks)
                    sp.sem_inc(turn, 1)
                    sp.dma_start(x[:, u, :], slots[bass.ds((i * 2 + u) * P, P), :]).then_inc(x_in[u], 16)
                    sp.dma_start(w1_sb[:, u, :, :], w1[one, :, :].rearrange("a (k p) n -> p (a k) n", p=P)).then_inc(w1_in[u], 16)
                    sp.dma_start(b1_sb[:, u, :], b1[one, :, :].rearrange("a p m -> p (a m)")).then_inc(w1_in[u], 16)
                    if affine is not None:
                        for n in range(2):
                            sp.dma_start(aff[:, u, 2 * n:2 * n + 2], affine[n][one, :, :].rearrange("a p m -> p (a m)")).then_inc(w1_in[u], 16)
                for u in range(2):
                    one = bass.ds(experts[u], 1)
                    sp.wait_ge(y_ready, i * 2 + (u + 1))
                    sp.sem_inc(turn, 1)
                    sp.dma_start(w2_sb[:, u, :, :], w2[one, :, :].rearrange("a (k p) n -> p (a k) n", p=P)).then_inc(w2_in[u], 16)
                    sp.dma_start(b2_sb[:, u, :], b2[one, :].rearrange("a n -> (a n)").partition_broadcast(P)).then_inc(w2_in[u], 16)

        @block.gpsimd
        def _(pool):
            with pool.Fori(0, nb // 2) as i:
                for u in range(2):
                    pool.wait_ge(y_ready, i * 2 + (u + 3))
                    pool.sem_inc(turn, 1)
                    pool.dma_start(results[bass.ds((i * 2 + u) * P, P), :], y[:, u, :]).then_inc(stored[u], 16)
                    pool.wait_ge(stored[u], i * 16 + 16)
                    pool.sem_inc(y_free, 1)

        @block.tensor
        def _(pe):
            with pe.Fori(0, nb // 2) as i:
                for u in range(2):
                    pe.wait_ge(x_in[u], i * 16 + 16)
                    for k in range(2):
                        ins = nc.tensor.transpose(p_x[u][:, 0, k, :], x[:, u, k * P:(k + 1) * P], g.ident[:, :])
                    ins.then_inc(turned, 1)
                for u in range(2):
                    pe.wait_ge(w1_in[u], i * (16 * n_w1) + 16 * n_w1)
                    pe.wait_ge(xt_ready, i * 2 + (u + 1))
                    for m in range(m_all):
                        for k in range(2):
                            ins = nc.tensor.matmul(p_h[u][m // 4][:, m % 4, :], w1_sb[:, u, k, m * P:(m + 1) * P], xt[:, u, k, :],
                                                   start=(k == 0), stop=(k == 1))
                        if m % 4 == 3:
                            ins.then_inc(h_done, 1)
                for u in range(2):
                    pe.wait_ge(w2_in[u], i * 32 + 32)
                    for m in range(m_all):
                        if m % 4 == 0:
                            pe.wait_ge(h_ready, i * (2 * banks) + (2 * banks + u * banks + m // 4 + 1))
                        ins = nc.tensor.matmul(p_y[u][:, 0:D], ht[:, u, m, :], w2_sb[:, u, m, :], start=(m == 0), stop=(m == m_all - 1))
                    ins.then_inc(y_done, 1)

        @block.scalar
        def _(act):
            with act.Fori(0, nb // 2) as i:
                for u in range(2):
                    act.wait_ge(y_done, i * 2 + (u + 1))
                    for b in range(banks):
                        act.wait_ge(h_done, i * (2 * banks) + (u * banks + b + 1))
                        for m in range(4 * b, 4 * b + 4):
                            ins = nc.scalar.activation(ht[:, u, m, :], p_h[u][b][:, m % 4, :], func, bias=b1_sb[:, u, m:m + 1])
                        ins.then_inc(h_ready, 1)

        @block.vector
        def _(v):
            with v.Fori(0, nb // 2) as i:
                for u in range(2):
                    v.wait_ge(turned, i * 2 + (u + 1))
                    if affine is None:
                        nc.vector.tensor_copy(xt[:, u, :, :], p_x[u][:, 0, :, :]).then_inc(xt_ready, 1)
                    else:
                        v.wait_ge(w1_in[u], i * (16 * n_w1) + 16 * n_w1)
                        for k in range(2):
                            ins = nc.vector.tensor_scalar(xt[:, u, k, :], p_x[u][:, 0, k, :], aff[:, u, k:k + 1], aff[:, u, 2 + k:3 + k],
                                                          ALU.mult, ALU.add)
                        ins.then_inc(xt_ready, 1)
                for u in range(2):
                    v.wait_ge(y_free, i * 2 + (u + 1))
                    v.wait_ge(y_done, i * 2 + (u + 3))
                    nc.vector.tensor_tensor(y[:, u, :], p_y[u][:, 0:D], b2_sb[:, u, :], ALU.add).then_inc(y_ready, 1)


def combine(nc, g, results, source, r, into, xn=None, guard=False):
    with Phase(nc, "gather") as ph:
        got = ph.sb("got", [P, r.choices, T, D])
        ok, high, low = (ph.sb(s, [P, D], I32) for s in ("ok", "high", "low"))
        clean, top, bottom = ph.sb("clean", [P, T, D]), ph.sb("top", [P, D]), ph.sb("bottom", [P, D])
        arrived = [ph.sem(f"arrived{n}") for n in range(r.choices * T)]
        block = ph.block()

        @block.gpsimd
        def _(pool):
            for k in range(r.choices):
                for t in range(T):
                    pool.indirect_dma_start(got[:, k, t, :], None, results,
                                            bass.IndirectOffsetOnAxis(ap=source[:, k, t:t + 1], axis=0)).then_inc(arrived[k * T + t], 16)

        @block.vector
        def _(v):
            if guard:
                nc.vector.memset(clean[:, :, :], 0.0)
                nc.vector.memset(top[:, :], 1e4)
                nc.vector.memset(bottom[:, :], -1e4)
                v.drain()
            if xn is not None:
                nc.vector.tensor_tensor(into[:, :, :], into[:, :, :], xn[:, :, :], ALU.add)
            for k in range(r.choices):
                v.drain()
                for t in range(T):
                    v.wait_ge(arrived[k * T + t], 16)
                    if not guard:
                        nc.vector.scalar_tensor_tensor(into[:, t, :], got[:, k, t, :], r.gate[:, k, t:t + 1], into[:, t, :], ALU.mult, ALU.add)
                        continue
                    y = got[:, k, t, :]
                    nc.vector.tensor_scalar(y, y, r.gate[:, k, t:t + 1], None, ALU.mult)
                    v.drain()
                    nc.vector.tensor_tensor(ok[:, :], y, y, ALU.is_equal)
                    nc.vector.tensor_scalar(high[:, :], y, 3.4028234e38, None, ALU.is_gt)
                    nc.vector.tensor_scalar(low[:, :], y, -3.4028234e38, None, ALU.is_lt)
                    v.drain()
                    nc.vector.copy_predicated(clean[:, t, :], ok[:, :], y)
                    v.drain()
                    nc.vector.copy_predicated(clean[:, t, :], high[:, :], top[:, :])
                    v.drain()
                    nc.vector.copy_predicated(clean[:, t, :], low[:, :], bottom[:, :])
                    v.drain()
                    nc.vector.tensor_tensor(into[:, t, :], into[:, t, :], clean[:, t, :], ALU.add)


def capacity_ffn(nc, g, i):
    chosen = max(max(1, int(0.5 * N)) - 1, 1)
    with Phase(nc, "cap") as ph:
        xn = ph.sb("xn", [P, T, D])
        r = Routes(ph, 1, (chosen + P - 1) // P)
        source = ph.sb("source_i", [P, 1, T], I32)
        r.source = source[:, 0, :]
        slots, results = g.dram("cap_slots", [NP, D]), g.dram("cap_results", [r.blocks * P, D])
        layernorm(nc, g.X, xn)
        rank_tokens(nc, g, xn, i["L0_ffn_wr"].rearrange("d o -> (d o)"), i["L0_ffn_br"], chosen, r)
        scatter_tokens(nc, g, xn, r, slots, fill=False)
        expert_blocks(nc, g, slots, results, r, i["L0_ffn_w1"].rearrange("(a d) f -> a d f", a=1), i["L0_ffn_b1"],
                      i["L0_ffn_w2"].rearrange("(a d) f -> a d f", a=1), i["L0_ffn_b2"].rearrange("(a d) -> a d", a=1),
                      ACT.Gelu_apprx_tanh)
        combine(nc, g, results, source, r, g.X, xn=xn)


def blocks_for(choices, experts):
    need = (NP * choices + experts * (P - 1)) // P
    return need + need % 2


def switch_ffn(nc, g, i):
    ne = i["L1_ffn_gate_w"].shape[1]
    capacity = -(-5 * N // (4 * ne))
    with Phase(nc, "switch") as ph:
        xn, xt = ph.sb("xn", [P, T, D]), ph.sb("xt", [P, T, 2, P])
        r = Routes(ph, 1, blocks_for(1, ne))
        slots, results = g.dram("switch_slots", [r.blocks * P, D]), g.dram("switch_results", [r.blocks * P, D])
        layernorm(nc, g.X, xn)
        self_terms(nc, g, xn, xt)
        choose_experts(nc, g, xt, i["L1_ffn_gate_w"], i["L1_ffn_gate_b"], r, capacity=capacity)
        scatter_tokens(nc, g, xn, r, slots, fill=True)
        expert_blocks(nc, g, slots, results, r, i["L1_ffn_w1"], i["L1_ffn_b1"], i["L1_ffn_w2"], i["L1_ffn_b2"], ACT.Relu)
        combine(nc, g, results, r.slot, r, g.X, guard=True)


def top2_gelu_ffn(nc, g, i):
    ne = i["L2_ffn_Wr"].shape[1]
    with Phase(nc, "top2") as ph:
        xn, xt = ph.sb("xn", [P, T, D]), ph.sb("xt", [P, T, 2, P])
        r = Routes(ph, 2, blocks_for(2, ne))
        slots, results = g.dram("gelu_slots", [r.blocks * P, D]), g.dram("gelu_results", [r.blocks * P, D])
        layernorm(nc, g.X, xn)
        self_terms(nc, g, xn, xt)
        choose_experts(nc, g, xt, i["L2_ffn_Wr"], i["L2_ffn_br"], r)
        layernorm(nc, xn, xn)
        scatter_tokens(nc, g, xn, r, slots, fill=True)
        expert_blocks(nc, g, slots, results, r, i["L2_ffn_W1"], i["L2_ffn_b1"], i["L2_ffn_W2"], i["L2_ffn_b2"], ACT.Gelu,
                      affine=(i["L2_ffn_ln_g"], i["L2_ffn_ln_b"]))
        combine(nc, g, results, r.slot, r, g.X)


def top2_relu_ffn(nc, g, i):
    ne = i["L3_ffn_gate_w"].shape[1]
    with Phase(nc, "moe") as ph:
        xn, xt = ph.sb("xn", [P, T, D]), ph.sb("xt", [P, T, 2, P])
        r = Routes(ph, 2, blocks_for(2, ne))
        slots, results = g.dram("relu_slots", [r.blocks * P, D]), g.dram("relu_results", [r.blocks * P, D])
        layernorm(nc, g.X, xn)
        self_terms(nc, g, xn, xt)
        choose_experts(nc, g, xt, i["L3_ffn_gate_w"], i["L3_ffn_gate_b"], r)
        scatter_tokens(nc, g, xn, r, slots, fill=True)
        expert_blocks(nc, g, slots, results, r, i["L3_ffn_w1"], i["L3_ffn_b1"], i["L3_ffn_w2"], i["L3_ffn_b2"], ACT.Relu)
        combine(nc, g, results, r.slot, r, xn)
        layernorm(nc, xn, xn, gamma=i["L3_ffn_gamma"], beta=i["L3_ffn_beta"], add=g.X)


BANKS = 6
WIDE = D + HD + 1
assert U % BANKS == 0


def scale_rows(nc, g, x, y, table, relu=False):
    with Phase(nc, "scale") as ph:
        ready, written = ph.sem("ready"), ph.sem("written")
        block = ph.block()

        @block.vector
        def _(v):
            for t in range(T):
                if relu:
                    ins = nc.vector.tensor_scalar(y[:, t, :], x[:, t, :], 0.0, g.dinv[:, t:t + 1], ALU.max, ALU.mult)
                else:
                    ins = nc.vector.tensor_scalar(y[:, t, :], x[:, t, :], g.dinv[:, t:t + 1], None, ALU.mult)
            ins.then_inc(ready, 1)

        @block.sync
        def _(sp):
            sp.wait_ge(ready, 1)
            sp.dma_start(table.rearrange("(t p) f -> p t f", p=P), y[:, :, :]).then_inc(written, 16)
            sp.wait_ge(written, 16)


def gcn_edges(nc, g, table, acc):
    with Phase(nc, "gcn") as ph:
        idx = ph.sb("idx", [P, U], I32)
        got = ph.sb("got", [P, U, D])
        hot = ph.sb("hot", [P, U, P])
        p_sum = [ph.ps(f"p_sum{b}", [P, 512]) for b in range(BANKS)]
        idx_set, turn, hot_ready, agg_done, added = (ph.sem(s) for s in ("idx_set", "turn", "hot_ready", "agg_done", "added"))
        gathered = [ph.sem(f"gathered{u}") for u in range(U)]
        block = ph.block()

        @block.sync
        def _(sp):
            sp.sem_inc(agg_done, U)
            sp.sem_inc(added, U)

        @block.gpsimd
        def _(pool):
            gather_loop(nc, pool, ph, g.src, table, got, idx, gathered, agg_done, idx_set, turn)

        @block.tensor
        def _(pe):
            with pe.Fori(0, EC // U) as i:
                for u in range(U):
                    pe.wait_ge(added, i * U + (u - BANKS + 1 + U))
                    pe.wait_ge(hot_ready, i * U + (u + 1))
                    pe.wait_ge(gathered[u], i * 16 + 16)
                    for half in range(2):
                        ins = nc.tensor.matmul(p_sum[u % BANKS][:, half * P:(half + 1) * P], got[:, u, half * P:(half + 1) * P],
                                               hot[:, u, :], start=True, stop=True)
                    ins.then_inc(agg_done, 1)

        @block.vector
        def _(v):
            def each(i, u):
                v.wait_ge(agg_done, i * U + (u + 1))
                c = bass.ds(i * U + u, 1)
                nc.vector.tensor_scalar(hot[:, u, :], g.iota_free[:, :], g.dst[:, c], g.weight[:, c], ALU.is_equal, ALU.mult)\
                    .then_inc(hot_ready, 1)

            def add(i, u, tile):
                v.wait_ge(added, i * U + (u + U))
                v.wait_ge(agg_done, i * U + (u + 1 + U))
                a = acc[:, bass.ds(tile, 1), :, :].rearrange("p a h n -> p (a h n)")
                nc.vector.tensor_tensor(a, a, p_sum[u % BANKS][:, 0:D], ALU.add).then_inc(added, 1)

            add_loop(nc, v, g, ph, each, add)


def gcn_linear(nc, g, agg, w, b, z):
    with Phase(nc, "lin") as ph:
        w_sb, b_row = ph.sb("w", [P, 2, D]), ph.sb("b", [P, D])
        p_z = [ph.ps(f"p_z{n}", [P, 512]) for n in range(4)]
        loaded, done, taken = ph.sem("loaded"), ph.sem("done"), ph.sem("taken")
        block = ph.block()

        @block.sync
        def _(sp):
            sp.dma_start(w_sb[:, :, :], w.rearrange("(k p) n -> p k n", p=P)).then_inc(loaded, 16)
            sp.dma_start(b_row[:, :], row(b)).then_inc(loaded, 16)

        @block.tensor
        def _(pe):
            pe.wait_ge(loaded, 32)
            for t in range(T):
                if t >= 4:
                    pe.wait_ge(taken, t - 3)
                for k in range(2):
                    ins = nc.tensor.matmul(p_z[t % 4][:, 0:D], agg[:, t, k, :], w_sb[:, k, :], start=(k == 0), stop=(k == 1))
                ins.then_inc(done, 1)

        @block.vector
        def _(v):
            v.wait_ge(loaded, 32)
            for t in range(T):
                v.wait_ge(done, t + 1)
                nc.vector.scalar_tensor_tensor(z[:, t, :], p_z[t % 4][:, 0:D], g.dinv[:, t:t + 1], b_row[:, :], ALU.mult, ALU.add)\
                    .then_inc(taken, 1)


def softmax_into(nc, g, z, into):
    with Phase(nc, "soft") as ph:
        top, total = ph.sb("top", [P, T]), ph.sb("total", [P, T])
        ready, done = ph.sem("ready"), ph.sem("done")
        block = ph.block()

        @block.vector
        def _(v):
            nc.vector.tensor_reduce(top[:, :], z[:, :, :], AX.X, ALU.max)
            v.drain()
            nc.vector.tensor_scalar(top[:, :], top[:, :], -1.0, None, ALU.mult).then_inc(ready, 1)
            v.wait_ge(done, T)
            nc.vector.reciprocal(total[:, :], total[:, :])
            v.drain()
            for t in range(T):
                nc.vector.scalar_tensor_tensor(into[:, t, :], z[:, t, :], total[:, t:t + 1], into[:, t, :], ALU.mult, ALU.add)

        @block.scalar
        def _(act):
            act.wait_ge(ready, 1)
            for t in range(T):
                nc.scalar.activation(z[:, t, :], z[:, t, :], ACT.Exp, bias=top[:, t:t + 1], accum_out=total[:, t:t + 1]).then_inc(done, 1)


def relu_into(nc, g, z, xn, into):
    with Phase(nc, "relu") as ph:
        block = ph.block()

        @block.vector
        def _(v):
            nc.vector.tensor_tensor(into[:, :, :], into[:, :, :], xn[:, :, :], ALU.add)
            v.drain()
            nc.vector.scalar_tensor_tensor(into[:, :, :], z[:, :, :], 0.0, into[:, :, :], ALU.max, ALU.add)


def gcn_softmax(nc, g, i):
    with Phase(nc, "gcn2") as ph:
        y, z, acc = ph.sb("y", [P, T, D]), ph.sb("z", [P, T, D]), ph.sb("acc", [P, T, 2, P])
        layernorm(nc, g.X, z)
        for n in (1, 2):
            table = g.dram(f"gcn_table{n}", [NP, D])
            scale_rows(nc, g, z, y, table, relu=(n == 2))
            self_terms(nc, g, y, acc)
            gcn_edges(nc, g, table, acc)
            gcn_linear(nc, g, acc, i[f"L2_gnn_W{n}"], i[f"L2_gnn_b{n}"], z)
        softmax_into(nc, g, z, g.X)


def gcn_residual(nc, g, i):
    with Phase(nc, "gcn1") as ph:
        xn, y, z, acc = ph.sb("xn", [P, T, D]), ph.sb("y", [P, T, D]), ph.sb("z", [P, T, D]), ph.sb("acc", [P, T, 2, P])
        table = g.dram("gcn_table3", [NP, D])
        layernorm(nc, g.X, xn)
        scale_rows(nc, g, xn, y, table)
        self_terms(nc, g, y, acc)
        gcn_edges(nc, g, table, acc)
        gcn_linear(nc, g, acc, i["L3_gnn_W"], i["L3_gnn_b"], z)
        relu_into(nc, g, z, xn, g.X)


def relation_tables(nc, g, xt, w, wt, attn_src, attn_dst, h_table, src_table, score_dst):
    S2 = 2 * HD
    with Phase(nc, "rel") as ph:
        w_sb, wt_sb = ph.sb("w", [P, R, 2, D]), ph.sb("wt", [P, R, 2, D])
        heads = ph.sb("heads", [P, 2, S2])
        proj = ph.sb("proj", [P, 2, R, S2])
        rows = ph.sb("rows", [P, 2, R, D])
        scores = ph.sb("scores", [P, T, R, HD])
        p_proj = ph.ps("p_proj", [P, 2, R, S2])
        p_score = [ph.ps(f"p_score{b}", [P, 512]) for b in range(2)]
        p_rows = [ph.ps(f"p_rows{b}", [P, 2, D]) for b in range(4)]
        blanked, heads_in, w_in, wt_in = ph.sem("blanked"), ph.sem("heads_in"), ph.sem("w_in"), ph.sem("wt_in")
        proj_done, proj_ready, score_done, score_taken = (ph.sem(s) for s in ("proj_done", "proj_ready", "score_done", "score_taken"))
        rows_done, rows_taken, scores_written = ph.sem("rows_done"), ph.sem("rows_taken"), ph.sem("scores_written")
        written = [ph.sem(f"written{b}") for b in range(2)]
        block = ph.block()
        per_tile = R // 2

        @block.sync
        def _(sp):
            sp.dma_start(w_sb[:, :, :, :], w.rearrange("r (k p) f -> p (r k) f", p=P)).then_inc(w_in, 16)
            sp.wait_ge(blanked, 1)
            for n, attn in enumerate((attn_src, attn_dst)):
                for h in range(HD):
                    p0 = h * DH % P
                    sp.dma_start(heads[p0:p0 + DH, h * DH // P, n * HD + h:n * HD + h + 1],
                                 attn[h:h + 1, :].rearrange("a d -> d a")).then_inc(heads_in, 16)
            sp.dma_start(wt_sb[:, :, :, :], wt.rearrange("r (k p) o -> p (r k) o", p=P)).then_inc(wt_in, 16)
            h_view = h_table.rearrange("(r t p) f -> t p r f", r=R, p=P)
            for t in range(T):
                sp.wait_ge(rows_taken, per_tile * (t + 1))
                sp.dma_start(h_view[t, :, :, :], rows[:, t % 2, :, :]).then_inc(written[t % 2], 16)
            sp.wait_ge(score_taken, 2 * T)
            for r in range(R):
                sp.dma_start(src_table[r * NP:(r + 1) * NP, :].rearrange("(t p) h -> p t h", p=P), scores[:, :, r, :])\
                    .then_inc(scores_written, 16)
            sp.wait_ge(scores_written, 16 * R)
            for b in range(2):
                sp.wait_ge(written[b], 16 * ((T + 1 - b) // 2))

        @block.tensor
        def _(pe):
            pe.wait_ge(w_in, 16)
            pe.wait_ge(heads_in, 16 * S2)
            for half in range(2):
                for r in range(R):
                    for k in range(2):
                        ins = nc.tensor.matmul(p_proj[:, half, r, :], w_sb[:, r, k, half * P:(half + 1) * P], heads[:, k, :],
                                               start=(k == 0), stop=(k == 1))
            ins.then_inc(proj_done, 1)
            pe.wait_ge(proj_ready, 1)
            for t in range(T):
                if t >= 2:
                    pe.wait_ge(score_taken, 2 * (t - 1))
                for k in range(2):
                    ins = nc.tensor.matmul(p_score[t % 2][:, 0:R * S2], xt[:, t, k, :], proj[:, k, :, :].rearrange("p r s -> p (r s)"),
                                           start=(k == 0), stop=(k == 1))
                ins.then_inc(score_done, 1)
            pe.wait_ge(wt_in, 16)
            for t in range(T):
                for b in range(per_tile):
                    n = t * per_tile + b
                    if n >= 4:
                        pe.wait_ge(rows_taken, n - 3)
                    for r in range(2):
                        for k in range(2):
                            ins = nc.tensor.matmul(p_rows[n % 4][:, r, :], xt[:, t, k, :], wt_sb[:, 2 * b + r, k, :],
                                                   start=(k == 0), stop=(k == 1))
                    ins.then_inc(rows_done, 1)

        def take(n, copy, eng):
            t, b = n // per_tile, n % per_tile
            if t >= 2:
                eng.wait_ge(written[t % 2], 16 * (t // 2))
            eng.wait_ge(rows_done, n + 1)
            if n:
                eng.wait_ge(rows_taken, n)
            copy(rows[:, t % 2, 2 * b:2 * b + 2, :], p_rows[n % 4][:, :, :]).then_inc(rows_taken, 1)

        @block.scalar
        def _(act):
            for n in range(1, T * per_tile, 2):
                take(n, nc.scalar.copy, act)

        @block.vector
        def _(v):
            nc.vector.memset(heads[:, :, :], 0.0).then_inc(blanked, 1)
            v.wait_ge(proj_done, 1)
            nc.vector.tensor_copy(proj[:, :, :, :], p_proj[:, :, :, :]).then_inc(proj_ready, 1)
            for t in range(T):
                v.wait_ge(score_done, t + 1)
                both = p_score[t % 2][:, 0:R * S2].rearrange("p (r s) -> p r s", r=R)
                nc.vector.tensor_copy(scores[:, t, :, :], both[:, :, 0:HD]).then_inc(score_taken, 1)
                nc.vector.tensor_copy(score_dst[:, t, :].rearrange("p (r h) -> p r h", r=R), both[:, :, HD:S2]).then_inc(score_taken, 1)
            for n in range(0, T * per_tile, 2):
                take(n, nc.vector.tensor_copy, v)


def edge_scores(nc, g, src_table, score_dst, scores):
    S = R * HD
    with Phase(nc, "score") as ph:
        idx = ph.sb("idx", [P, U], I32)
        got = ph.sb("got", [P, U, HD])
        hot = ph.sb("hot", [P, U, P], BF16)
        parts, left = ph.sb("parts", [P, T, 3, S], BF16), ph.sb("left", [P, T, S])
        rel_idx = ph.sb("rel_idx", [P, R])
        rel, picked, s = ph.sb("rel", [P, EC, R]), ph.sb("picked", [P, U, R, HD]), ph.sb("s", [P, U, HD])
        groups = U // G
        p_hot = [ph.ps(f"p_hot{b}", [P, G, P], BF16) for b in range(groups)]
        p_dst = [ph.ps(f"p_dst{b}", [P, G, 2 * S]) for b in range(groups)]
        idx_set, turn, hot_ready, turned, copied = (ph.sem(x) for x in ("idx_set", "turn", "hot_ready", "turned", "copied"))
        split, dst_done, picked_done, got_used, iota_made = (
            ph.sem(x) for x in ("split", "dst_done", "picked_done", "got_used", "iota_made"))
        gathered = [ph.sem(f"gathered{u}") for u in range(U)]
        block = ph.block()

        @block.sync
        def _(sp):
            sp.sem_inc(got_used, U)
            sp.sem_inc(turned, groups)
            sp.sem_inc(copied, groups)
            sp.sem_inc(picked_done, groups)

        @block.gpsimd
        def _(pool):
            nc.gpsimd.iota(rel_idx[:, :], [[1, R]], base=0, channel_multiplier=0,
                           allow_small_or_imprecise_dtypes=True).then_inc(iota_made, 1)
            gather_loop(nc, pool, ph, g.hrow, src_table, got, idx, gathered, got_used, idx_set, turn)

        @block.tensor
        def _(pe):
            registers = [pe.alloc_register(f"{ph.name}_pe_tile{u}") for u in range(U)]
            pe.wait_ge(split, 1)
            with pe.Fori(0, EC // U) as i:
                tiles = tiles_of(pe, g, registers, i)
                for b in range(groups):
                    pe.wait_ge(hot_ready, i * groups + (b + 1))
                    pe.wait_ge(copied, i * groups + (b + 1))
                    for u in range(b * G, (b + 1) * G):
                        ins = nc.tensor.transpose(p_hot[b][:, u % G, :], hot[:, u, :], g.ident_b[:, :])
                    ins.then_inc(turned, 1)
                for b in range(groups):
                    pe.wait_ge(picked_done, i * groups + (b + 1))
                    pe.wait_ge(copied, i * groups + (b + 1 + groups))
                    for u in range(b * G, (b + 1) * G):
                        for k in range(3):
                            ins = nc.tensor.matmul(p_dst[b][:, u % G, 0:S],
                                                   g.attrs_t[:, bass.ds(i * U + u, 1), :].rearrange("p a e -> p (a e)"),
                                                   parts[:, bass.ds(tiles[u], 1), k, :].rearrange("p a s -> p (a s)"),
                                                   start=(k == 0), stop=(k == 2))
                    ins.then_inc(dst_done, 1)

        @block.scalar
        def _(act):
            with act.Fori(0, EC // U) as i:
                for b in range(groups):
                    act.wait_ge(turned, i * groups + (b + 1 + groups))
                    act.sem_inc(turn, 1)
                    nc.scalar.copy(g.attrs_t[:, bass.ds(i * U + b * G, G), :], p_hot[b][:, :, :]).then_inc(copied, 1)

        @block.vector
        def _(v):
            split3(nc, v, score_dst[:, :, :], [parts[:, :, k, :] for k in range(3)], left[:, :, :])
            v.drain()
            v.sem_inc(split, 1)
            v.wait_ge(iota_made, 1)
            nc.vector.tensor_tensor(rel[:, :, :], rel_idx[:, :].unsqueeze(1).to_broadcast([P, EC, R]),
                                    g.etype[:, :].unsqueeze(2).to_broadcast([P, EC, R]), ALU.is_equal)
            v.drain()
            with v.Fori(0, EC // U) as i:
                for b in range(groups):
                    v.wait_ge(turned, i * groups + (b + 1))
                    for u in range(b * G, (b + 1) * G):
                        ins = nc.vector.tensor_scalar(hot[:, u, :], g.iota_free[:, :], g.dst[:, bass.ds(i * U + u, 1)], None,
                                                      ALU.is_equal)
                    ins.then_inc(hot_ready, 1)
                for b in range(groups):
                    some = slice(b * G, (b + 1) * G)
                    v.wait_ge(dst_done, i * groups + (b + 1))
                    nc.vector.tensor_tensor(picked[:, some, :, :], p_dst[b][:, :, 0:S].rearrange("p u (r h) -> p u r h", r=R),
                                            rel[:, bass.ds(i * U + b * G, G), :].unsqueeze(3).to_broadcast([P, G, R, HD]),
                                            ALU.mult).then_inc(picked_done, 1)
                v.drain()
                nc.vector.tensor_reduce(s[:, :, :], picked[:, :, :, :].rearrange("p u r h -> p u h r"), AX.X, ALU.add)
                v.drain()
                for u in range(U):
                    v.wait_ge(gathered[u], i * 16 + 16)
                    v.sem_inc(turn, 1)
                nc.vector.tensor_tensor(scores[:, bass.ds(i * U, U), :], s[:, :, :], got[:, :, :], ALU.add)
                v.drain()
                v.sem_inc(got_used, U)
            nc.vector.scalar_tensor_tensor(scores[:, :, :], scores[:, :, :], 0.2, scores[:, :, :], ALU.mult, ALU.max)


def find_runs(nc, g, scores, top, last, broken):
    K = 3
    EK = EC // K
    SL = K * HD
    with Phase(nc, "runs") as ph:
        turned_s, turned_d = ph.sb("turned_s", [EK, SL, P]), ph.sb("turned_d", [EK, K, P])
        same, ends = ph.sb("same", [EK, K, P]), ph.sb("ends", [EK, K, P])
        drops, drop_sum, total = ph.sb("drops", [EK, K, P]), ph.sb("drop_sum", [EK, 1]), ph.sb("total", [1, 1])
        p_turned, p_back = ph.ps("p_turned", [P, SL + K + 1, P]), ph.ps("p_total", [1, 1])
        turned, copied, scanned, returned, counted, total_done, back_free = (
            ph.sem(x) for x in ("turned", "copied", "scanned", "returned", "counted", "total_done", "back_free"))
        block = ph.block()

        @block.tensor
        def _(pe):
            for k in range(K):
                for h in range(HD):
                    nc.tensor.transpose(p_turned[0:EK, k * HD + h, :], scores[:, k * EK:(k + 1) * EK, h], g.ident[:, :])
                ins = nc.tensor.transpose(p_turned[0:EK, SL + k, :], g.dst[:, k * EK:(k + 1) * EK], g.ident[:, :])
            ins.then_inc(turned, 1)
            pe.wait_ge(copied, 2)
            pe.wait_ge(counted, 1)
            nc.tensor.matmul(p_back[:, :], drop_sum[:, :], g.ones[0:EK, 0:1], start=True, stop=True).then_inc(total_done, 1)
            pe.wait_ge(scanned, 1)
            for n in range(SL + K):
                given = turned_s[:, n, :] if n < SL else ends[:, n - SL, :]
                ins = nc.tensor.transpose(p_turned[:, n, 0:EK], given, g.ident[0:EK, 0:EK])
            ins.then_inc(returned, 1)

        @block.scalar
        def _(act):
            act.wait_ge(turned, 1)
            nc.scalar.copy(turned_s[:, 0:SL // 2, :], p_turned[0:EK, 0:SL // 2, :]).then_inc(copied, 1)

        @block.vector
        def _(v):
            v.wait_ge(turned, 1)
            nc.vector.tensor_copy(turned_d[:, :, :], p_turned[0:EK, SL:SL + K, :])
            nc.vector.tensor_copy(turned_s[:, SL // 2:SL, :], p_turned[0:EK, SL // 2:SL, :]).then_inc(copied, 1)
            v.drain()
            nc.vector.tensor_scalar(ends[:, :, :], turned_d[:, :, :], 0.0, float(2 * P), ALU.is_lt, ALU.mult)
            v.drain()
            nc.vector.tensor_tensor(turned_d[:, :, :], turned_d[:, :, :], ends[:, :, :], ALU.add)
            nc.vector.memset(same[:, :, 0:1], 0.0)
            nc.vector.memset(drops[:, :, 0:1], 0.0)
            v.drain()
            now, before = turned_d[:, :, 1:P], turned_d[:, :, 0:P - 1]
            nc.vector.tensor_tensor(same[:, :, 1:P], now, before, ALU.is_equal)
            nc.vector.tensor_tensor(drops[:, :, 1:P], now, before, ALU.is_lt)
            nc.vector.memset(ends[:, :, P - 1:P], 1.0)
            nc.vector.tensor_tensor(ends[:, :, 0:P - 1], now, before, ALU.not_equal)
            v.drain()
            nc.vector.tensor_reduce(drop_sum[:, :], drops[:, :, :].rearrange("p k e -> p (k e)"), AX.X, ALU.add).then_inc(counted, 1)
            v.wait_ge(copied, 2)
            for n in range(SL):
                ins = nc.vector.tensor_tensor_scan(turned_s[:, n, :], same[:, n // HD, :], turned_s[:, n, :], 0.0, ALU.mult, ALU.max)
            v.drain()
            v.sem_inc(scanned, 1)
            v.wait_ge(total_done, 1)
            nc.vector.tensor_copy(broken[:, :], p_back[:, :])
            v.wait_ge(returned, 1)
            for k in range(K):
                nc.vector.tensor_copy(top[:, k * EK:(k + 1) * EK, :], p_turned[:, k * HD:(k + 1) * HD, 0:EK].rearrange("p h c -> p c h"))
            nc.vector.tensor_copy(last[:, :].rearrange("p (k c) -> p k c", k=K), p_turned[:, SL:SL + K, 0:EK])


def peaks_of_runs(nc, g, top, last, amax):
    with Phase(nc, "peaks") as ph:
        hot = ph.sb("hot", [P, U, P])
        p_top = [ph.ps(f"p_top{b}", [P, 512]) for b in range(BANKS)]
        hot_ready, picked, taken, blanked = ph.sem("hot_ready"), ph.sem("picked"), ph.sem("taken"), ph.sem("blanked")
        block = ph.block()

        @block.sync
        def _(sp):
            sp.sem_inc(picked, U)

        @block.scalar
        def _(act):
            act.sem_inc(taken, U)

        @block.gpsimd
        def _(pool):
            nc.gpsimd.memset(amax[:, :, :], 0.0).then_inc(blanked, 1)

        @block.tensor
        def _(pe):
            with pe.Fori(0, EC // U) as i:
                for u in range(U):
                    pe.wait_ge(taken, i * U + (u - BANKS + 1 + U))
                    pe.wait_ge(hot_ready, i * U + (u + 1))
                    nc.tensor.matmul(p_top[u % BANKS][:, 0:HD], hot[:, u, :],
                                     top[:, bass.ds(i * U + u, 1), :].rearrange("p a h -> p (a h)"),
                                     start=True, stop=True).then_inc(picked, 1)

        @block.vector
        def _(v):
            v.wait_ge(blanked, 1)

            def each(i, u):
                v.wait_ge(picked, i * U + (u + 1))
                c = bass.ds(i * U + u, 1)
                nc.vector.tensor_scalar(hot[:, u, :], g.iota_free[:, :], g.dst[:, c], last[:, c], ALU.is_equal, ALU.mult)\
                    .then_inc(hot_ready, 1)

            def add(i, u, tile):
                v.drain()
                v.wait_ge(picked, i * U + (u + 1 + U))
                a = amax[:, bass.ds(tile, 1), :].rearrange("p a h -> p (a h)")
                nc.vector.tensor_tensor(a, a, p_top[u % BANKS][:, 0:HD], ALU.max).then_inc(taken, 1)

            add_loop(nc, v, g, ph, each, add)


def peaks_in_any_order(nc, g, scores, amax):
    HH = HD // 2
    with Phase(nc, "anyorder") as ph:
        hot = ph.sb("hot", [P, P])
        diag, peak = ph.sb("diag", [P, HD, P]), ph.sb("peak", [P, HD])
        p_max = ph.ps("p_max", [P, HD, P])
        ready, done, turn = ph.sem("ready"), ph.sem("done"), ph.sem("turn")
        block = ph.block()

        @block.tensor
        def _(pe):
            with pe.Fori(0, EC) as c:
                pe.wait_ge(ready, c + 1)
                for part in range(2):
                    some = slice(part * HH, (part + 1) * HH)
                    ins = nc.tensor.matmul(p_max[:, some, :].rearrange("p h e -> p (h e)"), hot[:, :],
                                           diag[:, some, :].rearrange("p h e -> p (h e)"), start=True, stop=True)
                ins.then_inc(done, 1)

        @block.vector
        def _(v):
            register = [v.alloc_register(f"{ph.name}_tile")]
            nc.vector.memset(amax[:, :, :], 0.0)
            with v.Fori(0, EC) as c:
                v.load(register, g.chunk_tile[0:1, bass.ds(c, 1)])
                tile = v.snap(register[0], min_val=0, max_val=T - 1)
                nc.vector.tensor_scalar(hot[:, :], g.iota_free[:, :], g.dst[:, bass.ds(c, 1)], None, ALU.is_equal)
                nc.vector.tensor_tensor(diag[:, :, :], g.ident[:, :].unsqueeze(1).to_broadcast([P, HD, P]),
                                        scores[:, bass.ds(c, 1), :].rearrange("p a h -> p (a h)").unsqueeze(2).to_broadcast([P, HD, P]),
                                        ALU.mult)
                v.drain()
                v.sem_inc(ready, 1)
                v.wait_ge(done, c + 1)
                v.sem_inc(turn, 1)
                nc.vector.tensor_reduce(peak[:, :], p_max[:, :, :], AX.X, ALU.max)
                v.drain()
                a = amax[:, bass.ds(tile, 1), :].rearrange("p a h -> p (a h)")
                nc.vector.tensor_tensor(a, a, peak[:, :], ALU.max)
                v.drain()


def edge_weights(nc, g, scores, amax, weights):
    with Phase(nc, "weigh") as ph:
        parts, left = ph.sb("parts", [P, T, 3, HD], BF16), ph.sb("left", [P, T, HD])
        p_amax = ph.ps("p_amax", [P, EC, HD])
        split, picked, less = ph.sem("split"), ph.sem("picked"), ph.sem("less")
        block = ph.block()

        @block.tensor
        def _(pe):
            registers = [pe.alloc_register(f"{ph.name}_pe_tile{u}") for u in range(U)]
            pe.wait_ge(split, 1)
            with pe.Fori(0, EC // U) as i:
                tiles = tiles_of(pe, g, registers, i)
                for u in range(U):
                    for k in range(3):
                        ins = nc.tensor.matmul(p_amax[:, bass.ds(i * U + u, 1), :].rearrange("p a h -> p (a h)"),
                                               g.attrs_t[:, bass.ds(i * U + u, 1), :].rearrange("p a e -> p (a e)"),
                                               parts[:, bass.ds(tiles[u], 1), k, :].rearrange("p a h -> p (a h)"),
                                               start=(k == 0), stop=(k == 2))
                ins.then_inc(picked, 1)

        @block.vector
        def _(v):
            split3(nc, v, amax[:, :, :], [parts[:, :, k, :] for k in range(3)], left[:, :, :])
            v.drain()
            v.sem_inc(split, 1)
            nc.vector.tensor_copy(weights[:, :, HD], g.weight[:, :])
            v.wait_ge(picked, EC // U)
            nc.vector.tensor_tensor(scores[:, :, :], scores[:, :, :], p_amax[:, :, :], ALU.subtract).then_inc(less, 1)

        @block.scalar
        def _(act):
            act.wait_ge(less, 1)
            nc.scalar.activation(weights[:, :, 0:HD], scores[:, :, :], ACT.Exp)


def attend(nc, g, h_table, weights, acc):
    with Phase(nc, "attend") as ph:
        idx = ph.sb("idx", [P, U], I32)
        got = ph.sb("got", [P, U, D])
        hot = ph.sb("hot", [P, U, P])
        msg = ph.sb("msg", [P, U, WIDE])
        p_sum = [ph.ps(f"p_sum{b}", [P, 512]) for b in range(BANKS)]
        idx_set, turn, hot_ready, tail_ready, msg_ready, agg_done, added = (
            ph.sem(x) for x in ("idx_set", "turn", "hot_ready", "tail_ready", "msg_ready", "agg_done", "added"))
        gathered = [ph.sem(f"gathered{u}") for u in range(U)]
        block = ph.block()

        @block.sync
        def _(sp):
            for s in (agg_done, added, msg_ready):
                sp.sem_inc(s, U)

        @block.gpsimd
        def _(pool):
            gather_loop(nc, pool, ph, g.hrow, h_table, got, idx, gathered, msg_ready, idx_set, turn)

        @block.tensor
        def _(pe):
            with pe.Fori(0, EC // U) as i:
                for u in range(U):
                    pe.wait_ge(added, i * U + (u - BANKS + 1 + U))
                    pe.wait_ge(hot_ready, i * U + (u + 1))
                    pe.wait_ge(tail_ready, i * U + (u + 1))
                    pe.wait_ge(msg_ready, i * U + (u + 1 + U))
                    nc.tensor.matmul(p_sum[u % BANKS][:, 0:WIDE], hot[:, u, :], msg[:, u, :], start=True, stop=True).then_inc(agg_done, 1)

        @block.scalar
        def _(act):
            with act.Fori(0, EC // U) as i:
                for u in range(U):
                    act.wait_ge(agg_done, i * U + (u + 1))
                    act.sem_inc(turn, 1)
                    nc.scalar.copy(msg[:, u, D:WIDE], weights[:, bass.ds(i * U + u, 1), :].rearrange("p a w -> p (a w)"))\
                        .then_inc(tail_ready, 1)

        @block.vector
        def _(v):
            nc.vector.memset(acc[:, :, :], 0.0)

            def each(i, u):
                v.wait_ge(agg_done, i * U + (u + 1))
                nc.vector.tensor_scalar(hot[:, u, :], g.iota_free[:, :], g.dst[:, bass.ds(i * U + u, 1)], None,
                                        ALU.is_equal).then_inc(hot_ready, 1)
                v.wait_ge(gathered[u], i * 16 + 16)
                w = weights[:, bass.ds(i * U + u, 1), 0:HD].rearrange("p a h -> p (a h)")
                nc.vector.tensor_tensor(msg[:, u, 0:D].rearrange("p (h d) -> p h d", h=HD),
                                        got[:, u, :].rearrange("p (h d) -> p h d", h=HD),
                                        w.unsqueeze(2).to_broadcast([P, HD, DH]), ALU.mult).then_inc(msg_ready, 1)

            def add(i, u, tile):
                v.wait_ge(added, i * U + (u + U))
                v.wait_ge(agg_done, i * U + (u + 1 + U))
                a = acc[:, bass.ds(tile, 1), :].rearrange("p a f -> p (a f)")
                nc.vector.tensor_tensor(a, a, p_sum[u % BANKS][:, 0:WIDE], ALU.add).then_inc(added, 1)

            add_loop(nc, v, g, ph, each, add)


def divide_into(nc, g, acc, into):
    with Phase(nc, "divide") as ph:
        total, share = ph.sb("total", [P, T, HD]), ph.sb("share", [P, T, HD])
        deg, positive, root = ph.sb("deg", [P, T]), ph.sb("positive", [P, T]), ph.sb("root", [P, T])
        deg_ready, root_ready = ph.sem("deg_ready"), ph.sem("root_ready")
        block = ph.block()

        @block.scalar
        def _(act):
            act.wait_ge(deg_ready, 1)
            nc.scalar.activation(root[:, :], deg[:, :], ACT.Sqrt).then_inc(root_ready, 1)

        @block.vector
        def _(v):
            nc.vector.tensor_scalar(positive[:, :], acc[:, :, D + HD], 1.0, 0.0, ALU.add, ALU.is_gt)
            nc.vector.tensor_scalar(deg[:, :], acc[:, :, D + HD], 1.0, 1e-30, ALU.add, ALU.max).then_inc(deg_ready, 1)
            nc.vector.tensor_scalar(total[:, :, :], acc[:, :, D:D + HD], 1e-12, None, ALU.add)
            v.drain()
            nc.vector.reciprocal(share[:, :, :], total[:, :, :])
            v.drain()
            for t in range(T):
                a = acc[:, t, 0:D].rearrange("p (h d) -> p h d", h=HD)
                nc.vector.tensor_tensor(a, a, share[:, t, :].unsqueeze(2).to_broadcast([P, HD, DH]), ALU.mult)
            v.wait_ge(root_ready, 1)
            nc.vector.reciprocal(g.dinv[:, :], root[:, :])
            v.drain()
            nc.vector.tensor_tensor(g.dinv[:, :], g.dinv[:, :], positive[:, :], ALU.mult)
            nc.vector.tensor_tensor(into[:, :, :], into[:, :, :], acc[:, :, 0:D], ALU.add)


def relational_attention(nc, g, i):
    h_table, src_table = g.dram("h_table", [R * NP, D]), g.dram("src_table", [R * NP, HD])
    with Phase(nc, "rgat") as ph:
        score_dst, amax = ph.sb("score_dst", [P, T, R * HD]), ph.sb("amax", [P, T, HD])
        scores = ph.sb("scores", [P, EC, HD])
        with Phase(nc, "rgat_in") as inner:
            xn, xt = inner.sb("xn", [P, T, D]), inner.sb("xt", [P, T, 2, P])
            layernorm(nc, g.X, xn)
            self_terms(nc, g, xn, xt)
            relation_tables(nc, g, xt, i["L1_gnn_W"], i["L1_gnn_W_turned"], i["L1_gnn_attn_src"], i["L1_gnn_attn_dst"],
                            h_table, src_table, score_dst)
        edge_scores(nc, g, src_table, score_dst, scores)
        top, last, broken = ph.sb("top", [P, EC, HD]), ph.sb("last", [P, EC]), ph.sb("broken", [1, 1], I32)
        find_runs(nc, g, scores, top, last, broken)
        count = nc.values_load(broken[0:1, 0:1], min_val=0, max_val=EC * P)
        Phase.branch = True
        with nc.If(count > 0):
            peaks_in_any_order(nc, g, scores, amax)
        with nc.Else():
            peaks_of_runs(nc, g, top, last, amax)
        Phase.branch = False
        weights, acc = ph.sb("weights", [P, EC, HD + 1]), ph.sb("acc", [P, T, WIDE])
        edge_weights(nc, g, scores, amax, weights)
        attend(nc, g, h_table, weights, acc)
        divide_into(nc, g, acc, g.X)


STAGES = [capacity_ffn, relational_attention, switch_ffn, gcn_softmax, top2_gelu_ffn, gcn_residual, top2_relu_ffn]
UNUSED = ("L0_ffn_attention_mask",)


def column(a):
    return a.reshape(*a.shape[:-1], -1, P).swapaxes(-1, -2)


LAYOUT = {"L0_gnn_b1": column, "L0_ffn_b1": lambda a: column(a[None]), "L1_ffn_b1": column, "L2_ffn_b1": column,
          "L3_ffn_b1": column, "L2_ffn_ln_g": column, "L2_ffn_ln_b": column, "L3_gnn_W": lambda a: a.T}


LAST_STAGE = 8
FIRST_STAGE = 1


def build(nc, i, out):
    Phase.count, Phase.spent = 0, []
    with ExitStack() as stack:
        g = Shared()

        def sb(name, shape, dt=F32):
            return stack.enter_context(nc.sbuf_tensor(name, shape, dt))

        g.dram = lambda name, shape, dt=F32: nc.dram_tensor(name, shape, dt, kind="Internal").ap()
        g.X = sb("X", [P, T, D])
        g.iota_free, g.iota_part = sb("iota_free", [P, P]), sb("iota_part", [P, 1])
        g.ident, g.upto, g.before, g.ones = (sb(s, [P, P]) for s in ("ident", "upto", "before", "ones"))
        g.ident_b = sb("ident_b", [P, P], BF16)
        g.zero_row = sb("zero_row", [P, 512])
        g.dinv = sb("dinv", [P, T])
        g.chunk_tile = sb("chunk_tile", [1, EC], I32)
        g.src, g.hrow = sb("src", [P, EC], I32), sb("hrow", [P, EC], I32)
        g.dst, g.weight, g.etype = sb("dst", [P, EC]), sb("weight", [P, EC]), sb("etype", [P, EC])
        constants(nc, g, i["x"])
        sorted_rows = g.dram("sorted_rows", [P * EC, ROW])
        sort_edges(nc, g, i["src"], i["dst"], i["edge_type_8"], i["edge_weight"], i["edge_attr_32"], sorted_rows)
        g.attrs_t = sb("attrs_t", [P, EC, P], BF16)
        load_sorted(nc, g, sorted_rows)
        if FIRST_STAGE == 1:
            gine_stack(nc, g, i)
        for s, stage in enumerate(STAGES):
            if FIRST_STAGE <= s + 2 <= LAST_STAGE:
                stage(nc, g, i)
        store(nc, g.X, out)


def kernel(**inputs):
    import numpy as np
    import concourse.bacc as bacc
    from concourse.bass_utils import run_bass_kernel_spmd

    nc = bacc.Bacc("TRN2", target_bir_lowering=False, num_devices=1)
    arrays, aps = {}, {}
    for name, given in inputs.items():
        a = np.ascontiguousarray(given)
        if a.ndim == 0 or name in UNUSED:
            continue
        if name == "L1_gnn_W":
            inputs_turned = np.ascontiguousarray(a.transpose(0, 2, 1))
            arrays["in_L1_gnn_W_turned"] = inputs_turned
            aps["L1_gnn_W_turned"] = nc.dram_tensor("in_L1_gnn_W_turned", a.shape, F32, kind="ExternalInput").ap()
        if name in LAYOUT:
            a = np.ascontiguousarray(LAYOUT[name](a))
        arrays[f"in_{name}"] = a
        aps[name] = nc.dram_tensor(f"in_{name}", a.shape, mybir.dt.from_np(a.dtype), kind="ExternalInput").ap()
    out = nc.dram_tensor("out", (N, D), F32, kind="ExternalOutput").ap()
    build(nc, aps, out)
    r = run_bass_kernel_spmd(nc, [arrays], core_ids=[0])
    return r.results[0]["out"]
```

```python
from contextlib import ExitStack

import concourse.bass as bass
from concourse import mybir

F32 = mybir.dt.float32
I32 = mybir.dt.int32
BF16 = mybir.dt.bfloat16
ALU = mybir.AluOpType
ACT = mybir.ActivationFunctionType
AX = mybir.AxisListType

P = 128
N = 1875
D = 256
T = (N + P - 1) // P
NP = T * P
TAIL = N - (T - 1) * P
E = 31875
EP = 125
EJ = E // EP
EC = 264
ED = 32
ROW = 40
C_SRC, C_DST, C_W, C_HROW, C_TYPE = 32, 33, 34, 35, 36
R = 8
HD, DH = 8, 32
U = 12
G = 4
LAG = 4
LN_EPS = 1e-5
assert EP * EJ == E and EC * P >= E + T * (P - 1) and EC % U == 0 and U % G == 0


class Phase:

    count = 0
    spent = []
    branch = False

    def __init__(self, nc, name):
        Phase.count += 1
        self.nc, self.name, self.stack = nc, f"{name}{Phase.count}", ExitStack()

    def __enter__(self):
        return self

    def __exit__(self, *what):
        self.stack.close()
        if len(Phase.spent) > 90 and not Phase.branch:
            self.nc.clear_and_free_semaphores(Phase.spent)
            self.nc.all_engine_barrier(sem_only=True)
            Phase.spent.clear()

    def sb(self, name, shape, dt=F32):
        return self.stack.enter_context(self.nc.sbuf_tensor(f"{self.name}_{name}", shape, dt))

    def ps(self, name, shape, dt=F32):
        return self.stack.enter_context(self.nc.psum_tensor(f"{self.name}_{name}", shape, dt))

    def sem(self, name):
        Phase.spent.append(self.nc.alloc_semaphore(f"{self.name}_{name}"))
        return Phase.spent[-1]

    def block(self):
        return self.stack.enter_context(self.nc.Block())


class Shared:
    pass


def row(ap):
    return ap.partition_broadcast(P)


def constants(nc, g, x):
    with Phase(nc, "const") as ph:
        tail_zeroed, iota_made, loaded = ph.sem("tail_zeroed"), ph.sem("iota_made"), ph.sem("loaded")
        block = ph.block()

        @block.sync
        def _(sp):
            sp.dma_start(g.X[:, 0:T - 1, :], x[0:(T - 1) * P, :].rearrange("(t p) f -> p t f", p=P)).then_inc(loaded, 16)
            sp.wait_ge(tail_zeroed, 1)
            sp.dma_start(g.X[0:TAIL, T - 1, :], x[(T - 1) * P:N, :]).then_inc(loaded, 16)
            sp.wait_ge(loaded, 32)

        @block.gpsimd
        def _(pool):
            nc.gpsimd.iota(g.iota_free[:, :], [[1, P]], base=0, channel_multiplier=0,
                           allow_small_or_imprecise_dtypes=True).then_inc(iota_made, 1)
            nc.gpsimd.iota(g.iota_part[:, :], [[0, 1]], base=0, channel_multiplier=1,
                           allow_small_or_imprecise_dtypes=True).then_inc(iota_made, 1)

        @block.vector
        def _(v):
            nc.vector.memset(g.X[:, T - 1, :], 0.0).then_inc(tail_zeroed, 1)
            nc.vector.memset(g.ones[:, :], 1.0)
            nc.vector.memset(g.zero_row[:, :], 0.0)
            v.wait_ge(iota_made, 2)
            nc.vector.tensor_scalar(g.ident[:, :], g.iota_free[:, :], g.iota_part[:, 0:1], None, ALU.is_equal)
            nc.vector.tensor_scalar(g.ident_b[:, :], g.iota_free[:, :], g.iota_part[:, 0:1], None, ALU.is_equal)
            nc.vector.tensor_scalar(g.upto[:, :], g.iota_free[:, :], g.iota_part[:, 0:1], None, ALU.is_ge)
            nc.vector.tensor_scalar(g.before[:, :], g.iota_free[:, :], g.iota_part[:, 0:1], None, ALU.is_gt)


def sort_edges(nc, g, src, dst, etype, weight, attr, sorted_rows):
    packed = g.dram("packed", [E + P, ROW])
    with Phase(nc, "sort") as ph:
        stage, slot_i = ph.sb("stage", [EP, EJ, ROW]), ph.sb("slot_i", [EP, EJ], I32)
        first_i, drops_i = ph.sb("first_i", [1, EC], I32), ph.sb("drops_i", [1, 1], I32)
        base, filled_to = ph.sb("base", [P, T]), ph.sb("filled_to", [P, T])
        with Phase(nc, "place") as inner:
            place_edges(nc, g, inner, src, dst, etype, weight, attr, stage, slot_i, first_i, drops_i, base, filled_to)
        drops = nc.values_load(drops_i[0:1, 0:1], min_val=0, max_val=E)
        Phase.branch = True
        with nc.If(drops > 0):
            move_rows(nc, g, stage, slot_i, sorted_rows)
        with nc.Else():
            move_chunks(nc, g, stage, first_i, base, filled_to, packed, sorted_rows)
        Phase.branch = False


def place_edges(nc, g, ph, src, dst, etype, weight, attr, stage, slot_i, first_i, drops_i, base, filled_to):
    src_i, typ_i = (ph.sb(n, [EP, EJ], I32) for n in ("src_i", "typ_i"))
    dst_i = ph.sb("dst_i", [EP, EJ + 1], I32)
    next_i = ph.sb("next_i", [EP, EJ], I32)
    wgt = ph.sb("wgt", [EP, EJ])
    tile_i, local_i = ph.sb("tile_i", [EP, EJ + 1], I32), ph.sb("local_i", [EP, EJ], I32)
    tile_f = ph.sb("tile_f", [EP, EJ + 1])
    member, rank = ph.sb("member", [EP, T, EJ]), ph.sb("rank", [EP, T, EJ])
    zeros = ph.sb("zeros", [EP, EJ])
    below = ph.sb("below", [EP, T])
    padded_i, padded = ph.sb("padded_i", [P, T], I32), ph.sb("padded", [P, T])
    end, spare = ph.sb("end", [P, T]), ph.sb("spare", [P, T])
    pos, pos_i = ph.sb("pos", [EP, EJ]), ph.sb("pos_i", [EP, EJ], I32)
    lane_i, chunk_i = ph.sb("lane_i", [EP, EJ], I32), ph.sb("chunk_i", [EP, EJ], I32)
    lane = ph.sb("lane", [EP, EJ])
    chunk0 = ph.sb("chunk0", [1, EC])
    passed, tile_of, first = ph.sb("passed", [1, EC, T]), ph.sb("tile_of", [1, EC]), ph.sb("first", [1, EC])
    drop, drop_sum = ph.sb("drop", [EP, EJ]), ph.sb("drop_sum", [EP, 1])
    p_below, p_total, p_drops = ph.ps("p_below", [P, T]), ph.ps("p_total", [P, T]), ph.ps("p_drops", [1, 1])
    loaded, beyond, ranked, counted, iota_made = (ph.sem(x) for x in ("loaded", "beyond", "ranked", "counted", "iota_made"))
    block = ph.block()
    edges = "(p j) -> p j"

    @block.sync
    def _(sp):
        for tile, ap in ((src_i, src), (typ_i, etype), (wgt, weight)):
            sp.dma_start(tile[:, :], ap.rearrange(edges, p=EP)).then_inc(loaded, 16)
        sp.dma_start(dst_i[:, 0:EJ], dst.rearrange(edges, p=EP)).then_inc(loaded, 16)
        sp.wait_ge(beyond, 1)
        sp.dma_start(next_i[0:EP - 1, :], dst.rearrange(edges, p=EP)[1:EP, :]).then_inc(loaded, 16)
        sp.dma_start(stage[:, :, 0:ED], attr.rearrange("(p j) c -> p j c", p=EP)).then_inc(loaded, 16)
        sp.wait_ge(loaded, 96)

    @block.tensor
    def _(pe):
        pe.wait_ge(ranked, 1)
        nc.tensor.matmul(p_drops[:, :], drop_sum[:, :], g.ones[0:EP, 0:1], start=True, stop=True)
        nc.tensor.matmul(p_below[:, :], g.before[0:EP, :], rank[:, :, EJ - 1], start=True, stop=True)
        nc.tensor.matmul(p_total[:, :], g.ones[0:EP, :], rank[:, :, EJ - 1], start=True, stop=True).then_inc(counted, 1)

    @block.gpsimd
    def _(pool):
        nc.gpsimd.memset(next_i[:, :], T * P).then_inc(beyond, 1)
        nc.gpsimd.iota(chunk0[:, :], [[P, EC]], base=0, channel_multiplier=0,
                       allow_small_or_imprecise_dtypes=True).then_inc(iota_made, 1)

    @block.vector
    def _(v):
        nc.vector.memset(zeros[:, :], 0.0)
        v.wait_ge(loaded, 96)
        nc.vector.tensor_copy(dst_i[:, EJ:EJ + 1], next_i[:, 0:1])
        v.drain()
        nc.vector.tensor_scalar(tile_i[:, :], dst_i[:, :], 7, None, ALU.arith_shift_right)
        nc.vector.tensor_scalar(local_i[:, :], dst_i[:, 0:EJ], P - 1, None, ALU.bitwise_and)
        v.drain()
        nc.vector.tensor_copy(tile_f[:, :], tile_i[:, :])
        nc.vector.tensor_copy(stage[:, :, C_DST], local_i[:, :])
        nc.vector.tensor_copy(stage[:, :, C_TYPE], typ_i[:, :])
        nc.vector.tensor_copy(stage[:, :, C_W], wgt[:, :])
        nc.vector.tensor_copy(stage[:, :, C_SRC].bitcast(I32), src_i[:, :])
        v.drain()
        nc.vector.scalar_tensor_tensor(stage[:, :, C_HROW].bitcast(I32), stage[:, :, C_TYPE], float(NP), src_i[:, :],
                                       ALU.mult, ALU.add)
        nc.vector.memset(stage[:, :, C_TYPE + 1:ROW], 0.0)
        nc.vector.tensor_tensor(drop[:, :], tile_f[:, 1:EJ + 1], tile_f[:, 0:EJ], ALU.is_lt)
        for t in range(T):
            nc.vector.tensor_scalar(member[:, t, :], tile_f[:, 0:EJ], float(t), None, ALU.is_equal)
        v.drain()
        nc.vector.tensor_reduce(drop_sum[:, :], drop[:, :], AX.X, ALU.add)
        for t in range(T):
            nc.vector.tensor_tensor_scan(rank[:, t, :], member[:, t, :], zeros[:, :], 0.0, ALU.add, ALU.add)
        v.drain()
        v.sem_inc(ranked, 1)
        v.wait_ge(counted, 1)
        nc.vector.tensor_copy(drops_i[:, :], p_drops[:, :])
        nc.vector.tensor_scalar(padded_i[:, :], p_total[:, :], float(P - 1), None, ALU.add)
        v.drain()
        nc.vector.tensor_scalar(padded_i[:, :], padded_i[:, :], 7, 7, ALU.arith_shift_right, ALU.arith_shift_left)
        v.drain()
        nc.vector.tensor_copy(padded[:, :], padded_i[:, :])
        v.drain()
        nc.vector.tensor_tensor_scan(end[:, :], padded[:, :], g.zero_row[:, 0:T], 0.0, ALU.add, ALU.add)
        nc.vector.tensor_tensor(spare[:, :], padded[:, :], p_total[:, :], ALU.subtract)
        v.drain()
        nc.vector.tensor_tensor(base[:, :], end[:, :], padded[:, :], ALU.subtract)
        nc.vector.tensor_tensor(filled_to[:, :], end[:, :], spare[:, :], ALU.subtract)
        v.drain()
        nc.vector.scalar_tensor_tensor(below[:, :], p_below[0:EP, :], -1.0, base[0:EP, :], ALU.add, ALU.add)
        v.drain()
        for t in range(T):
            nc.vector.scalar_tensor_tensor(member[:, t, :], rank[:, t, :], below[:, t:t + 1], member[:, t, :],
                                           ALU.add, ALU.mult)
        v.drain()
        nc.vector.tensor_reduce(pos[:, :], member[:, :, :].rearrange("p t j -> p j t"), AX.X, ALU.add)
        v.drain()
        nc.vector.tensor_copy(pos_i[:, :], pos[:, :])
        v.drain()
        nc.vector.tensor_scalar(chunk_i[:, :], pos_i[:, :], 7, None, ALU.arith_shift_right)
        nc.vector.tensor_scalar(lane_i[:, :], pos_i[:, :], P - 1, None, ALU.bitwise_and)
        v.drain()
        nc.vector.tensor_copy(lane[:, :], lane_i[:, :])
        v.drain()
        nc.vector.scalar_tensor_tensor(slot_i[:, :], lane[:, :], float(EC), chunk_i[:, :], ALU.mult, ALU.add)
        v.wait_ge(iota_made, 1)
        nc.vector.tensor_tensor(passed[:, :, :], chunk0[:, :].unsqueeze(2).to_broadcast([1, EC, T]),
                                end[0:1, :].unsqueeze(1).to_broadcast([1, EC, T]), ALU.is_ge)
        v.drain()
        nc.vector.tensor_reduce(tile_of[:, :], passed[:, :, :], AX.X, ALU.add)
        v.drain()
        nc.vector.tensor_scalar(g.chunk_tile[:, :], tile_of[:, :], float(T - 1), None, ALU.min)
        nc.vector.tensor_tensor(passed[:, :, :], passed[:, :, :], spare[0:1, :].unsqueeze(1).to_broadcast([1, EC, T]), ALU.mult)
        v.drain()
        nc.vector.tensor_reduce(first[:, :], passed[:, :, :], AX.X, ALU.add)
        v.drain()
        nc.vector.tensor_tensor(first[:, :], chunk0[:, :], first[:, :], ALU.subtract)
        v.drain()
        nc.vector.tensor_scalar(first_i[:, :], first[:, :], float(E), None, ALU.min)


def move_rows(nc, g, stage, slot_i, sorted_rows):
    with Phase(nc, "moverows") as ph:
        NB = 5
        blank = ph.sb("blank", [P, EC, ROW])
        out_row, out_slot = ph.sb("out_row", [EP, NB, ROW]), ph.sb("out_slot", [EP, NB], I32)
        blanked, prefilled, turn = ph.sem("blanked"), ph.sem("prefilled"), ph.sem("turn")
        row_ready, scattered = ph.sem("row_ready"), [ph.sem(f"scattered{u}") for u in range(NB)]
        block = ph.block()

        @block.sync
        def _(sp):
            sp.wait_ge(blanked, 2)
            sp.dma_start(sorted_rows.rearrange("(p c) w -> p c w", p=P), blank[:, :, :]).then_inc(prefilled, 16)
            sp.wait_ge(prefilled, 16)

        @block.gpsimd
        def _(pool):
            nc.gpsimd.memset(blank[:, :, :], 0.0).then_inc(blanked, 1)
            pool.wait_ge(blanked, 1)
            nc.gpsimd.memset(blank[:, :, C_DST:C_DST + 1], -1.0).then_inc(blanked, 1)
            pool.wait_ge(prefilled, 16)
            with pool.Fori(0, EJ // NB) as i:
                for u in range(NB):
                    pool.wait_ge(row_ready, i * NB + u + 1)
                    pool.sem_inc(turn, 1)
                    pool.indirect_dma_start(sorted_rows, bass.IndirectOffsetOnAxis(ap=out_slot[:, u:u + 1], axis=0),
                                            out_row[:, u, :], None).then_inc(scattered[u], 16)
            for u in range(NB):
                pool.wait_ge(scattered[u], 16 * (EJ // NB))

        @block.vector
        def _(v):
            nc.vector.memset(g.valid[:, :], 1.0)

            def fill(i):
                for u in range(NB):
                    if not isinstance(i, int):
                        v.wait_ge(scattered[u], i * 16)
                    nc.vector.tensor_copy(out_row[:, u, :], stage[:, bass.ds(i * NB + u, 1), :].rearrange("p a w -> p (a w)"))
                    nc.vector.tensor_copy(out_slot[:, u:u + 1], slot_i[:, bass.ds(i * NB + u, 1)])
                    v.drain()
                    v.sem_inc(row_ready, 1)

            fill(0)
            with v.Fori(1, EJ // NB) as i:
                fill(i)


def move_chunks(nc, g, stage, first_i, base, filled_to, packed, sorted_rows):
    with Phase(nc, "movechunks") as ph:
        slot, at_or_past = ph.sb("slot", [P, EC]), [ph.sb(f"at_or_past{n}", [P, EC, T]) for n in range(2)]
        iota_made, staged = ph.sem("iota_made"), ph.sem("staged")
        moved = [ph.sem(f"moved{n}") for n in range(3)]
        block = ph.block()
        view = sorted_rows.rearrange("(p c) w -> p c w", p=P)
        passes = [0, EC // U * 7 // 22, EC // U * 14 // 22, EC // U]

        def move(eng, n):
            registers = [eng.alloc_register(f"{ph.name}_first{n}_{u}") for u in range(U)]
            eng.wait_ge(staged, 32)
            with eng.Fori(passes[n], passes[n + 1]) as i:
                eng.load(registers, first_i[0:1, bass.ds(i * U, U)])
                firsts = [eng.snap(r, min_val=0, max_val=E) for r in registers]
                for u in range(U):
                    eng.dma_start(view[:, bass.ds(i * U + u, 1), :].rearrange("p a w -> p (a w)"),
                                  packed[bass.ds(firsts[u], P), :]).then_inc(moved[n], 16)
            eng.wait_ge(moved[n], 16 * U * (passes[n + 1] - passes[n]))

        @block.sync
        def _(sp):
            sp.dma_start(packed[0:E, :].rearrange("(p j) w -> p j w", p=EP), stage[:, :, :]).then_inc(staged, 16)
            sp.dma_start(packed[E:E + P, :], g.zero_row[:, 0:ROW]).then_inc(staged, 16)
            move(sp, 0)

        @block.scalar
        def _(act):
            move(act, 1)

        @block.gpsimd
        def _(pool):
            nc.gpsimd.iota(slot[:, :], [[P, EC]], base=0, channel_multiplier=1,
                           allow_small_or_imprecise_dtypes=True).then_inc(iota_made, 1)
            move(pool, 2)

        @block.tensor
        def _(pe):
            pe.wait_ge(iota_made, 1)

        @block.vector
        def _(v):
            v.wait_ge(iota_made, 1)
            for n, edge in enumerate((base, filled_to)):
                nc.vector.tensor_tensor(at_or_past[n][:, :, :], slot[:, :].unsqueeze(2).to_broadcast([P, EC, T]),
                                        edge[:, :].unsqueeze(1).to_broadcast([P, EC, T]), ALU.is_ge)
            v.drain()
            nc.vector.tensor_tensor(at_or_past[0][:, :, :], at_or_past[0][:, :, :], at_or_past[1][:, :, :], ALU.subtract)
            v.drain()
            nc.vector.tensor_reduce(g.valid[:, :], at_or_past[0][:, :, :], AX.X, ALU.add)


def split3(nc, eng, x, parts, left):
    nc.vector.tensor_copy(parts[0], x)
    eng.drain()
    nc.vector.tensor_tensor(left, x, parts[0], ALU.subtract)
    eng.drain()
    nc.vector.tensor_copy(parts[1], left)
    eng.drain()
    nc.vector.tensor_tensor(parts[2], left, parts[1], ALU.subtract)


def load_sorted(nc, g, sorted_rows):
    with Phase(nc, "unpack") as ph:
        B = EC // 2
        rows = ph.sb("rows", [P, B, ROW])
        left = ph.sb("left", [P, B, ED])
        parts = ph.sb("parts", [P, B, 4, ED], BF16)
        p_turned = [ph.ps(f"p_turned{b}", [P, 4, P], BF16) for b in range(8)]
        loaded, packed, turned = ph.sem("loaded"), ph.sem("packed"), ph.sem("turned")
        stored = [ph.sem("stored_a"), ph.sem("stored_v")]
        block = ph.block()
        batches = [(h, q) for h in range(2) for q in range(B // 4)]

        @block.sync
        def _(sp):
            view = sorted_rows.rearrange("(p c) w -> p c w", p=P)
            sp.dma_start(rows[:, :, :], view[:, 0:B, :]).then_inc(loaded, 16)
            sp.wait_ge(packed, 1)
            sp.dma_start(rows[:, :, :], view[:, B:EC, :]).then_inc(loaded, 16)

        def store(eng, copy, who, some):
            for n in some:
                if n % 2 != who:
                    continue
                h, q = batches[n]
                eng.wait_ge(turned, n + 1)
                c = h * B + 4 * q
                copy(g.attrs_t[:, c:c + 4, :], p_turned[n % 8][:, :, :]).then_inc(stored[who], 1)

        @block.vector
        def _(v):
            for h in range(2):
                v.wait_ge(loaded, 16 * (h + 1))
                if h:
                    v.wait_ge(turned, len(batches) // 2)
                a = rows[:, :, 0:ED]
                split3(nc, v, a, [parts[:, :, k, :] for k in range(3)], left[:, :, :])
                nc.vector.tensor_copy(parts[:, :, 3, :], a)
                half = slice(h * B, (h + 1) * B)
                nc.vector.tensor_copy(g.src[:, half], rows[:, :, C_SRC].bitcast(I32))
                nc.vector.tensor_copy(g.hrow[:, half], rows[:, :, C_HROW].bitcast(I32))
                nc.vector.scalar_tensor_tensor(g.dst[:, half], rows[:, :, C_DST], 1.0, g.valid[:, half], ALU.add, ALU.mult)
                v.drain()
                nc.vector.tensor_scalar(g.dst[:, half], g.dst[:, half], -1.0, None, ALU.add)
                nc.vector.tensor_copy(g.weight[:, half], rows[:, :, C_W])
                nc.vector.tensor_copy(g.etype[:, half], rows[:, :, C_TYPE])
                v.drain()
                v.sem_inc(packed, 1)
                store(v, nc.vector.tensor_copy, 1, range(h * B // 4, (h + 1) * B // 4))

        @block.tensor
        def _(pe):
            for n, (h, q) in enumerate(batches):
                pe.wait_ge(packed, h + 1)
                if n >= 8:
                    pe.wait_ge(stored[n % 2], (n - 8) // 2 + 1)
                for k in range(4):
                    ins = nc.tensor.transpose(p_turned[n % 8][:, k, :], parts[:, 4 * q + k, :, :].rearrange("p a w -> p (a w)"),
                                              g.ident_b[:, :])
                ins.then_inc(turned, 1)

        @block.scalar
        def _(act):
            store(act, nc.scalar.copy, 0, range(len(batches)))


class Turn:

    groups = [range(a, min(a + 6, T)) for a in range(0, T, 6)]

    def __init__(self, nc, g, ph, y, acc, eps=None):
        self.nc, self.g, self.y, self.acc, self.eps = nc, g, y, acc, eps
        self.scale, self.scaled = ph.sb("scale", [P, 1]), ph.sb("scaled", [P, P])
        self.p_turned = ph.ps("p_turned", [P, (T + 1) // 2, 2, 2, P])
        self.eps_in, self.scaled_ready, self.turned = ph.sem("eps_in"), ph.sem("scaled_ready"), ph.sem("turned")

    def load(self, sp):
        if self.eps is not None:
            sp.dma_start(self.scale[:, :], row(self.eps)).then_inc(self.eps_in, 16)

    def set_scale(self, v):
        if self.eps is not None:
            v.wait_ge(self.eps_in, 16)
            self.nc.vector.tensor_scalar(self.scale[:, :], self.scale[:, :], 1.0, None, ALU.add)
            v.drain()
            self.nc.vector.tensor_scalar(self.scaled[:, :], self.g.ident[:, :], self.scale[:, 0:1], None, ALU.mult)\
                .then_inc(self.scaled_ready, 1)

    def turn(self, pe, y_ready):
        if self.eps is not None:
            pe.wait_ge(self.scaled_ready, 1)
        diag = self.g.ident if self.eps is None else self.scaled
        for n, tiles in enumerate(self.groups):
            pe.wait_ge(y_ready, n + 1)
            for t in tiles:
                for half in range(2):
                    ins = self.nc.tensor.matmul(self.p_turned[:, t // 2, t % 2, half, :], self.y[:, t, half * P:(half + 1) * P],
                                                diag[:, :], start=True, stop=True)
            ins.then_inc(self.turned, 1)

    def take(self, act, n):
        act.wait_ge(self.turned, n + 1)
        a, size = self.groups[n][0], len(self.groups[n])
        flat = self.p_turned[:, :, :, :, :].rearrange("p b t h n -> p (b t) h n")
        self.nc.scalar.copy(self.acc[:, a:a + size, :, :], flat[:, a:a + size, :, :])


def layernorm(nc, g, h, y, gamma=None, beta=None, relu=False, add=None, table=None, addrow=None, turned=None, eps=None):
    groups = Turn.groups
    with Phase(nc, "ln") as ph:
        stats, mv = ph.sb("stats", [P, T, 6]), ph.sb("mv", [P, T, 2])
        var, std, rstd = ph.sb("var", [P, T]), ph.sb("std", [P, T]), ph.sb("rstd", [P, T])
        vec = ph.sb("vec", [P, 3, D])
        pre = ph.sb("pre", [P, T, D]) if relu and add is None else y
        rows = ph.sb("rows", [P, T, D]) if addrow is not None else y
        turn = Turn(nc, g, ph, y, turned, eps) if turned is not None else None
        loaded, var_ready, std_ready = ph.sem("loaded"), ph.sem("var_ready"), ph.sem("std_ready")
        pre_ready, y_ready, rows_ready, written = ph.sem("pre_ready"), ph.sem("y_ready"), ph.sem("rows_ready"), ph.sem("written")
        block = ph.block()
        given = [(i, a) for i, a in enumerate((gamma, beta, addrow)) if a is not None]

        @block.sync
        def _(sp):
            if turn:
                turn.load(sp)
            for i, a in given:
                sp.dma_start(vec[:, i, :], row(a)).then_inc(loaded, 16)
            if table is not None:
                for n, tiles in enumerate(groups):
                    sp.wait_ge(rows_ready, n + 1)
                    sp.dma_start(table.rearrange("(t p) f -> p t f", p=P)[:, tiles[0]:tiles[-1] + 1, :],
                                 rows[:, tiles[0]:tiles[-1] + 1, :]).then_inc(written, 16)
                sp.wait_ge(written, 16 * len(groups))

        @block.tensor
        def _(pe):
            if turn:
                turn.turn(pe, y_ready)

        @block.scalar
        def _(act):
            act.wait_ge(var_ready, 1)
            nc.scalar.activation(std[:, :], var[:, :], ACT.Sqrt).then_inc(std_ready, 1)
            for n, tiles in enumerate(groups):
                if pre is not y:
                    some = slice(tiles[0], tiles[-1] + 1)
                    act.wait_ge(pre_ready, n + 1)
                    nc.scalar.activation(y[:, some, :], pre[:, some, :], ACT.Relu).then_inc(y_ready, 1)
                if turn and n:
                    turn.take(act, n - 1)
            if turn:
                turn.take(act, len(groups) - 1)

        @block.vector
        def _(v):
            for t in range(T):
                nc.vector.bn_stats(stats[:, t, :], h[:, t, :])
            if turn:
                turn.set_scale(v)
            v.drain()
            for t in range(T):
                nc.vector.bn_aggr(mv[:, t, :], stats[:, t, :])
            v.drain()
            nc.vector.tensor_scalar(var[:, :], mv[:, :, 1], LN_EPS, None, ALU.add).then_inc(var_ready, 1)
            v.wait_ge(std_ready, 1)
            nc.vector.reciprocal(rstd[:, :], std[:, :])
            v.drain()
            for n, tiles in enumerate(groups):
                some = slice(tiles[0], tiles[-1] + 1)
                wide = [P, len(tiles), D]
                for t in tiles:
                    ins = nc.vector.tensor_scalar(pre[:, t, :], h[:, t, :], mv[:, t, 0:1], rstd[:, t:t + 1], ALU.subtract, ALU.mult)
                if given and n == 0:
                    v.wait_ge(loaded, 16 * len(given))
                if gamma is not None:
                    v.drain()
                    nc.vector.tensor_tensor(pre[:, some, :], pre[:, some, :], vec[:, 0, :].unsqueeze(1).to_broadcast(wide), ALU.mult)
                    v.drain()
                    ins = nc.vector.tensor_tensor(pre[:, some, :], pre[:, some, :], vec[:, 1, :].unsqueeze(1).to_broadcast(wide), ALU.add)
                ins.then_inc(pre_ready if pre is not y else y_ready, 1)
                if add is not None:
                    v.drain()
                    if relu:
                        nc.vector.scalar_tensor_tensor(add[:, some, :], pre[:, some, :], 0.0, add[:, some, :], ALU.max, ALU.add)
                    else:
                        nc.vector.tensor_tensor(add[:, some, :], pre[:, some, :], add[:, some, :], ALU.add)
                if addrow is not None:
                    v.drain()
                    x, b = pre[:, some, :], vec[:, 2, :].unsqueeze(1).to_broadcast(wide)
                    if relu:
                        ins = nc.vector.scalar_tensor_tensor(rows[:, some, :], x, 0.0, b, ALU.max, ALU.add)
                    else:
                        ins = nc.vector.tensor_tensor(rows[:, some, :], x, b, ALU.add)
                    ins.then_inc(rows_ready, 1)


def tiles_of(eng, g, registers, i):
    eng.load(registers, g.chunk_tile[0:1, bass.ds(i * U, U)])
    return [eng.snap(r, min_val=0, max_val=T - 1) for r in registers]


def gather_loop(nc, pool, ph, rows, table, got, idx, gathered, freed, idx_set, turn):
    with pool.Fori(0, EC // U) as i:
        for b in range(U // G):
            pool.wait_ge(freed, i * U + G * (b + 1))
            pool.sem_inc(turn, 1)
            nc.gpsimd.tensor_copy(idx[:, b * G:(b + 1) * G], rows[:, bass.ds(i * U + b * G, G)]).then_inc(idx_set, 1)
            pool.wait_ge(idx_set, i * (U // G) + (b + 1))
            pool.sem_inc(turn, 1)
            for u in range(b * G, (b + 1) * G):
                pool.indirect_dma_start(got[:, u, :], None, table,
                                        bass.IndirectOffsetOnAxis(ap=idx[:, u:u + 1], axis=0)).then_inc(gathered[u], 16)


def add_loop(nc, v, g, ph, each, add):
    registers = [v.alloc_register(f"{ph.name}_tile{u}") for u in range(U)]

    def tail(i):
        last = [v.snap(r, min_val=0, max_val=T - 1) for r in registers[U - LAG:]]
        return lambda n: add(i, n - LAG, last[n])

    def one_pass(i):
        left = tail(i) if not isinstance(i, int) else None
        for u in range(U):
            each(i, u)
            if u < LAG and left:
                left(u)
            if u == LAG - 1:
                tiles = tiles_of(v, g, registers, i)
            if u >= LAG:
                add(i, u - LAG, tiles[u - LAG])

    one_pass(0)
    with v.Fori(1, EC // U) as i:
        one_pass(i)
    left = tail(EC // U)
    for n in range(LAG):
        left(n)
    v.drain()


def lagged(eng, ahead, behind, lag):
    def one_pass(i):
        for u in range(U):
            ahead(i, u)
            if u >= lag or not isinstance(i, int):
                behind(i, u - lag)

    one_pass(0)
    with eng.Fori(1, EC // U) as i:
        one_pass(i)
    for u in range(lag):
        behind(EC // U, u - lag)


def gine_edges(nc, g, table, edge_w, acc):
    with Phase(nc, "gine") as ph:
        ew, left = ph.sb("ew", [P, D]), ph.sb("left", [P, D])
        parts = ph.sb("parts", [P, 3, D], BF16)
        w_a, w_b = ph.sb("w_a", [P, D], BF16), ph.sb("w_b", [P, D], BF16)
        idx = ph.sb("idx", [P, U], I32)
        got = ph.sb("got", [P, U, D])
        hot = ph.sb("hot", [P, U, P])
        msg = ph.sb("msg", [P, U, D])
        p_edge = [ph.ps(f"p_edge{b}", [P, 512]) for b in range(4)]
        p_sum = [ph.ps(f"p_sum{b}", [P, 512]) for b in range(4)]
        loaded, split, idx_set, turn = ph.sem("loaded"), ph.sem("split"), ph.sem("idx_set"), ph.sem("turn")
        gathered = [ph.sem(f"gathered{u}") for u in range(U)]
        edge_done, summed, msg_ready, hot_ready = ph.sem("edge_done"), ph.sem("summed"), ph.sem("msg_ready"), ph.sem("hot_ready")
        agg_done, added = ph.sem("agg_done"), ph.sem("added")
        block = ph.block()

        @block.sync
        def _(sp):
            for q in range(4):
                sp.dma_start(ew[q * ED:(q + 1) * ED, :], edge_w).then_inc(loaded, 16)
            for s in (summed, agg_done, added, msg_ready):
                sp.sem_inc(s, U)

        @block.gpsimd
        def _(pool):
            gather_loop(nc, pool, ph, g.src, table, got, idx, gathered, msg_ready, idx_set, turn)

        @block.tensor
        def _(pe):
            pe.wait_ge(split, 1)

            def edge(i, u):
                pe.wait_ge(summed, i * U + (u - 4 + 1 + U))
                a = g.attrs_t[:, bass.ds(i * U + u, 1), :].rearrange("p a e -> p (a e)")
                nc.tensor.matmul(p_edge[u % 4][:, 0:D], a, w_a[:, :], start=True, stop=False)
                nc.tensor.matmul(p_edge[u % 4][:, 0:D], a, w_b[:, :], start=False, stop=True).then_inc(edge_done, 1)

            def aggregate(i, u):
                pe.wait_ge(hot_ready, i * U + (u + 1))
                pe.wait_ge(added, i * U + (u - 4 + 1 + U))
                pe.wait_ge(msg_ready, i * U + (u + 1 + U))
                for half in range(2):
                    ins = nc.tensor.matmul(p_sum[u % 4][:, half * P:(half + 1) * P], msg[:, u % U, half * P:(half + 1) * P],
                                           hot[:, u % U, :], start=True, stop=True)
                ins.then_inc(agg_done, 1)

            lagged(pe, edge, aggregate, 3)

        @block.scalar
        def _(act):
            with act.Fori(0, EC // U) as i:
                for u in range(U):
                    act.wait_ge(agg_done, i * U + (u + 1))
                    act.wait_ge(summed, i * U + (u + 1 + U))
                    nc.scalar.activation(msg[:, u, :], got[:, u, :], ACT.Relu).then_inc(msg_ready, 1)

        @block.vector
        def _(v):
            v.wait_ge(loaded, 64)
            split3(nc, v, ew[:, :], [parts[:, k, :] for k in range(3)], left[:, :])
            nc.vector.memset(w_b[:, :], 0.0)
            v.drain()
            for q, part in enumerate((0, 0, 0, 1)):
                nc.vector.tensor_copy(w_a[q * ED:(q + 1) * ED, :], parts[q * ED:(q + 1) * ED, part, :])
            for q, part in enumerate((2, 1)):
                nc.vector.tensor_copy(w_b[q * ED:(q + 1) * ED, :], parts[q * ED:(q + 1) * ED, part, :])
            v.drain()
            v.sem_inc(split, 1)

            def each(i, u):
                v.wait_ge(agg_done, i * U + (u + 1))
                nc.vector.tensor_scalar(hot[:, u, :], g.iota_free[:, :], g.dst[:, bass.ds(i * U + u, 1)], None,
                                        ALU.is_equal).then_inc(hot_ready, 1)
                v.wait_ge(edge_done, i * U + (u + 1))
                v.wait_ge(gathered[u], i * 16 + 16)
                nc.vector.tensor_tensor(got[:, u, :], got[:, u, :], p_edge[u % 4][:, 0:D], ALU.add).then_inc(summed, 1)

            def add(i, u, tile):
                v.wait_ge(added, i * U + (u + U))
                v.wait_ge(agg_done, i * U + (u + 1 + U))
                a = acc[:, bass.ds(tile, 1), :, :].rearrange("p a h n -> p (a h n)")
                nc.vector.tensor_tensor(a, a, p_sum[u % 4][:, 0:D], ALU.add).then_inc(added, 1)

            add_loop(nc, v, g, ph, each, add)


def gine_mlp(nc, g, agg, h, w1, b1, w2, b2, first):
    with Phase(nc, "mlp") as ph:
        w1_sb, w2_sb = ph.sb("w1", [P, 2, D]), ph.sb("w2", [P, 2, D])
        b1_sb, b2_row = ph.sb("b1", [P, 2]), ph.sb("b2", [P, D])
        z = ph.sb("z", [P, 2, T, P])
        p_z = [ph.ps(f"p_z{b}", [P, 4, P]) for b in range(4)]
        p_h = [ph.ps(f"p_h{b}", [P, 512]) for b in range(4)]
        loaded, z_done, z_ready, h_done, h_added = (ph.sem(s) for s in ("loaded", "z_done", "z_ready", "h_done", "h_added"))
        block = ph.block()
        groups = [(t, min(4, T - t)) for t in range(0, T, 4)]
        steps = [(t, k, m) for t, k in groups for m in range(2)]

        @block.sync
        def _(sp):
            sp.dma_start(w1_sb[:, :, :], w1.rearrange("(k p) n -> p k n", p=P)).then_inc(loaded, 16)
            sp.dma_start(w2_sb[:, :, :], w2.rearrange("(k p) n -> p k n", p=P)).then_inc(loaded, 16)
            sp.dma_start(b1_sb[:, :], b1).then_inc(loaded, 16)
            sp.dma_start(b2_row[:, :], row(b2)).then_inc(loaded, 16)

        @block.tensor
        def _(pe):
            pe.wait_ge(loaded, 64)
            for s, (t, n, m) in enumerate(steps):
                if s >= 4:
                    pe.wait_ge(z_ready, s - 3)
                for k in range(2):
                    ins = nc.tensor.matmul(p_z[s % 4][:, 0:n, :], w1_sb[:, k, m * P:(m + 1) * P], agg[:, t:t + n, k, :],
                                           start=(k == 0), stop=(k == 1))
                ins.then_inc(z_done, 1)
            for t in range(T):
                pe.wait_ge(z_ready, 2 * (t // 4 + 1))
                if t >= 4:
                    pe.wait_ge(h_added, t - 3)
                for k in range(2):
                    ins = nc.tensor.matmul(p_h[t % 4][:, 0:D], z[:, k, t, :], w2_sb[:, k, :], start=(k == 0), stop=(k == 1))
                ins.then_inc(h_done, 1)

        @block.scalar
        def _(act):
            act.wait_ge(loaded, 64)
            for s, (t, n, m) in enumerate(steps):
                act.wait_ge(z_done, s + 1)
                nc.scalar.activation(z[:, m, t:t + n, :], p_z[s % 4][:, 0:n, :], ACT.Relu, bias=b1_sb[:, m:m + 1]).then_inc(z_ready, 1)

        @block.vector
        def _(v):
            v.wait_ge(loaded, 64)
            if not first:
                nc.vector.tensor_tensor(h[:, :, :], h[:, :, :], b2_row[:, :].unsqueeze(1).to_broadcast([P, T, D]), ALU.add)
                v.drain()
            for t in range(T):
                v.wait_ge(h_done, t + 1)
                nc.vector.tensor_tensor(h[:, t, :], p_h[t % 4][:, 0:D], b2_row[:, :] if first else h[:, t, :],
                                        ALU.add).then_inc(h_added, 1)


def store(nc, x, out):
    with Phase(nc, "store") as ph:
        written = ph.sem("written")
        block = ph.block()

        @block.sync
        def _(sp):
            sp.dma_start(out[0:(T - 1) * P, :].rearrange("(t p) f -> p t f", p=P), x[:, 0:T - 1, :]).then_inc(written, 16)
            sp.dma_start(out[(T - 1) * P:N, :], x[0:TAIL, T - 1, :]).then_inc(written, 16)
            sp.wait_ge(written, 32)


def gine_stack(nc, g, i):
    with Phase(nc, "stack") as ph:
        h, y, acc = ph.sb("h", [P, T, D]), ph.sb("y", [P, T, D]), ph.sb("acc", [P, T, 2, P])
        L = i["L0_gnn_W1"].shape[0]
        for k in range(L):
            table = g.dram(f"gine_table{k}", [NP, D])
            affine = {} if k == 0 else dict(gamma=i["L0_gnn_gamma"][k, :], beta=i["L0_gnn_beta"][k, :], relu=True)
            layernorm(nc, g, g.X if k == 0 else h, y, table=table, addrow=i["L0_gnn_eb"][k, :], turned=acc,
                      eps=i["L0_gnn_eps"][k:k + 1], **affine)
            gine_edges(nc, g, table, i["L0_gnn_eW"][k, :, :], acc)
            gine_mlp(nc, g, acc, h, i["L0_gnn_W1"][k, :, :], i["L0_gnn_b1"][k, :, :], i["L0_gnn_W2"][k, :, :],
                     i["L0_gnn_b2"][k, :], first=(k == 0))
        layernorm(nc, g, h, y, gamma=i["L0_gnn_gamma"][0, :], beta=i["L0_gnn_beta"][0, :], relu=True, add=g.X)


class Routes:

    def __init__(self, ph, k, blocks):
        self.slot, self.gate = ph.sb("slot", [P, k, T], I32), ph.sb("gate", [P, k, T])
        self.expert = ph.sb("expert", [1, blocks], I32)
        self.blocks, self.choices = blocks, k


def rank_tokens(nc, g, xn, wr, br, chosen, r):
    weights = g.dram("router_weights", [NP])
    last = r.blocks * P - 1
    with Phase(nc, "rank") as ph:
        prod, wr_row, br_col = ph.sb("prod", [P, T, D]), ph.sb("wr", [P, D]), ph.sb("br", [P, 1])
        w, turned, every = ph.sb("w", [P, T]), ph.sb("turned", [P, P]), ph.sb("every", [P, NP])
        junk, valid, gone = ph.sb("junk", [P, NP]), ph.sb("valid", [P, 1]), ph.sb("gone", [P, 1])
        lower, over, above, ties = ph.sb("lower", [P, P]), ph.sb("over", [P, T]), ph.sb("above", [P, T]), ph.sb("ties", [P, T])
        rank = ph.sb("rank", [P, T])
        p_turned = ph.ps("p_turned", [T, P])
        loaded, w_ready, w_turned, w_copied = (ph.sem(s) for s in ("loaded", "w_ready", "w_turned", "w_copied"))
        w_written, w_spread = ph.sem("w_written"), ph.sem("w_spread")
        block = ph.block()

        @block.sync
        def _(sp):
            sp.dma_start(wr_row[:, :], row(wr)).then_inc(loaded, 16)
            sp.dma_start(br_col[:, :], row(br)).then_inc(loaded, 16)
            sp.wait_ge(w_copied, 1)
            sp.dma_start(weights.rearrange("(t p) -> t p", p=P), turned[0:T, :]).then_inc(w_written, 16)
            sp.wait_ge(w_written, 16)
            sp.dma_start(every[:, :], row(weights)).then_inc(w_spread, 16)

        @block.tensor
        def _(pe):
            pe.wait_ge(w_ready, 1)
            nc.tensor.transpose(p_turned[:, :], w[:, :], g.ident[:, :]).then_inc(w_turned, 1)

        @block.vector
        def _(v):
            nc.vector.tensor_scalar(lower[:, :], g.iota_free[:, :], g.iota_part[:, 0:1], None, ALU.is_lt)
            nc.vector.tensor_scalar(valid[:, :], g.iota_part[:, :], float(TAIL), None, ALU.is_lt)
            nc.vector.tensor_scalar(gone[:, :], g.iota_part[:, :], float(TAIL), -3e38, ALU.is_ge, ALU.mult)
            v.wait_ge(loaded, 32)
            nc.vector.tensor_tensor(prod[:, :, :], xn[:, :, :], wr_row[:, :].unsqueeze(1).to_broadcast([P, T, D]), ALU.mult)
            v.drain()
            nc.vector.tensor_reduce(w[:, :], prod[:, :, :], AX.X, ALU.add)
            v.drain()
            nc.vector.tensor_scalar(w[:, :], w[:, :], br_col[:, 0:1], None, ALU.add)
            v.drain()
            nc.vector.tensor_scalar(w[:, T - 1:T], w[:, T - 1:T], valid[:, 0:1], gone[:, 0:1], ALU.mult, ALU.add).then_inc(w_ready, 1)
            v.wait_ge(w_turned, 1)
            nc.vector.tensor_copy(turned[0:T, :], p_turned[:, :]).then_inc(w_copied, 1)
            v.wait_ge(w_spread, 16)
            nc.vector.memset(over[:, 0:1], 0.0)
            for t in range(T):
                if t:
                    nc.vector.tensor_scalar(junk[:, 0:t * P], every[:, 0:t * P], w[:, t:t + 1], 0.0, ALU.is_ge, ALU.add,
                                            accum_out=over[:, t:t + 1])
                nc.vector.tensor_scalar(junk[:, t * P:NP], every[:, t * P:NP], w[:, t:t + 1], 0.0, ALU.is_gt, ALU.add,
                                        accum_out=above[:, t:t + 1])
                v.drain()
                nc.vector.scalar_tensor_tensor(junk[:, 0:P], every[:, t * P:(t + 1) * P], w[:, t:t + 1], lower[:, :],
                                               ALU.is_equal, ALU.mult, accum_out=ties[:, t:t + 1])
                v.drain()
            nc.vector.tensor_tensor(rank[:, :], over[:, :], above[:, :], ALU.add)
            v.drain()
            nc.vector.tensor_tensor(rank[:, :], rank[:, :], ties[:, :], ALU.add)
            v.drain()
            nc.vector.tensor_copy(r.slot[:, 0, :], rank[:, :])
            nc.vector.tensor_scalar(r.source[:, :], rank[:, :], float(last), None, ALU.min)
            nc.vector.scalar_tensor_tensor(r.gate[:, 0, :], rank[:, :], float(chosen), w[:, :], ALU.is_lt, ALU.mult)


def choose_experts(nc, g, xt, gate_w, gate_b, r, slots, capacity=None):
    ne, k_all, nb = gate_w.shape[1], r.choices, r.blocks
    with Phase(nc, "route") as ph:
        gw, gb = ph.sb("gw", [P, 2, ne]), ph.sb("gb", [P, ne])
        lg, eq, e_idx = ph.sb("lg", [P, T, ne]), ph.sb("eq", [P, T, ne]), ph.sb("e_idx", [P, ne])
        top, first = ph.sb("top", [P, k_all, T]), ph.sb("first", [P, T])
        hot = ph.sb("hot", [P, k_all, T, ne])
        ex, total = ph.sb("ex", [P, T, ne]), ph.sb("total", [P, T])
        count = [ph.sb(f"count{b}", [P, k_all * T, ne]) for b in range(2)]
        before, place = ph.sb("before", [P, k_all * T, ne]), ph.sb("place", [P, k_all * T, ne])
        padded_i, padded, end, base = ph.sb("padded_i", [P, ne], I32), ph.sb("padded", [P, ne]), ph.sb("end", [P, ne]), ph.sb("base", [P, ne])
        slot, pos = ph.sb("slot_f", [P, k_all * T]), ph.sb("pos", [P, k_all * T])
        block0, passed, owner = ph.sb("block0", [1, nb]), ph.sb("passed", [1, nb, ne]), ph.sb("owner", [1, nb])
        p_lg = ph.ps("p_lg", [P, T, ne])
        p_in, p_all = ph.ps("p_in", [P, k_all * T, ne]), ph.ps("p_all", [P, k_all * T, ne])
        loaded, iota_made, lg_done, ex_in, ex_done = (ph.sem(s) for s in ("loaded", "iota_made", "lg_done", "ex_in", "ex_done"))
        hot_ready, counted, filled = ph.sem("hot_ready"), ph.sem("counted"), ph.sem("filled")
        block = ph.block()
        big = 1000.0
        wide = [P, T, ne]

        @block.sync
        def _(sp):
            sp.dma_start(gw[:, :, :], gate_w.rearrange("(k p) e -> p k e", p=P)).then_inc(loaded, 16)
            sp.dma_start(gb[:, :], row(gate_b)).then_inc(loaded, 16)
            sp.dma_start(slots.rearrange("(b p) f -> p b f", p=P), g.zero_row[:, 0:D].unsqueeze(1).to_broadcast([P, nb, D])).then_inc(filled, 16)
            sp.wait_ge(filled, 16)

        @block.gpsimd
        def _(pool):
            nc.gpsimd.iota(e_idx[:, :], [[1, ne]], base=0, channel_multiplier=0,
                           allow_small_or_imprecise_dtypes=True).then_inc(iota_made, 1)
            nc.gpsimd.iota(block0[:, :], [[P, nb]], base=0, channel_multiplier=0,
                           allow_small_or_imprecise_dtypes=True).then_inc(iota_made, 1)

        @block.tensor
        def _(pe):
            pe.wait_ge(loaded, 32)
            for t in range(T):
                for k in range(2):
                    ins = nc.tensor.matmul(p_lg[:, t, :], xt[:, t, k, :], gw[:, k, :], start=(k == 0), stop=(k == 1))
            ins.then_inc(lg_done, 1)
            pe.wait_ge(hot_ready, 1)
            flat = hot[:, :, :, :].rearrange("p k t e -> p (k t e)")
            nc.tensor.matmul(p_in[:, :, :].rearrange("p a e -> p (a e)"), g.upto[:, :], flat, start=True, stop=True)
            nc.tensor.matmul(p_all[:, :, :].rearrange("p a e -> p (a e)"), g.ones[:, :], flat, start=True, stop=True).then_inc(counted, 1)

        @block.scalar
        def _(act):
            act.wait_ge(ex_in, 1)
            if k_all == 1:
                nc.scalar.activation(ex[:, :, :], ex[:, :, :], ACT.Exp).then_inc(ex_done, 1)
            else:
                nc.scalar.activation(total[:, :], total[:, :], ACT.Exp).then_inc(ex_done, 1)

        @block.vector
        def _(v):
            v.wait_ge(loaded, 32)
            v.wait_ge(lg_done, 1)
            nc.vector.tensor_tensor(lg[:, :, :], p_lg[:, :, :], gb[:, :].unsqueeze(1).to_broadcast(wide), ALU.add)
            v.wait_ge(iota_made, 2)
            nc.vector.tensor_scalar(e_idx[:, :], e_idx[:, :], -big, None, ALU.add)
            v.drain()
            for k in range(k_all):
                nc.vector.tensor_reduce(top[:, k, :], lg[:, :, :], AX.X, ALU.max)
                v.drain()
                if k_all == 1:
                    nc.vector.tensor_tensor(ex[:, :, :], lg[:, :, :], top[:, k, :].unsqueeze(2).to_broadcast(wide),
                                            ALU.subtract)
                nc.vector.tensor_tensor(eq[:, :, :], lg[:, :, :], top[:, k, :].unsqueeze(2).to_broadcast(wide), ALU.not_equal)
                v.drain()
                nc.vector.scalar_tensor_tensor(eq[:, :, :], eq[:, :, :], big, e_idx[:, :].unsqueeze(1).to_broadcast(wide),
                                               ALU.mult, ALU.add)
                v.drain()
                nc.vector.tensor_reduce(first[:, :], eq[:, :, :], AX.X, ALU.min)
                v.drain()
                nc.vector.tensor_tensor(hot[:, k, :, :], e_idx[:, :].unsqueeze(1).to_broadcast(wide),
                                        first[:, :].unsqueeze(2).to_broadcast(wide), ALU.is_equal)
                v.drain()
                if k + 1 < k_all:
                    nc.vector.scalar_tensor_tensor(lg[:, :, :], hot[:, k, :, :], -1e30, lg[:, :, :], ALU.mult, ALU.add)
                    v.drain()
            if k_all == 2:
                nc.vector.tensor_tensor(total[:, :], top[:, 1, :], top[:, 0, :], ALU.subtract)
                v.drain()
            v.sem_inc(ex_in, 1)
            v.sem_inc(hot_ready, 1)
            v.wait_ge(ex_done, 1)
            if k_all == 1:
                nc.vector.tensor_reduce(total[:, :], ex[:, :, :], AX.X, ALU.add)
                v.drain()
                nc.vector.reciprocal(r.gate[:, 0, :], total[:, :])
            else:
                nc.vector.tensor_scalar(first[:, :], total[:, :], 1.0, None, ALU.add)
                v.drain()
                nc.vector.reciprocal(r.gate[:, 0, :], first[:, :])
                v.drain()
                nc.vector.tensor_tensor(r.gate[:, 1, :], total[:, :], r.gate[:, 0, :], ALU.mult)
            v.wait_ge(counted, 1)
            kt = k_all * T
            nc.vector.tensor_copy(count[0][:, :, :], p_all[:, :, :])
            v.drain()
            s, a = 1, 0
            while s < kt:
                nc.vector.tensor_tensor(count[1 - a][:, s:kt, :], count[a][:, s:kt, :], count[a][:, 0:kt - s, :], ALU.add)
                nc.vector.tensor_copy(count[1 - a][:, 0:s, :], count[a][:, 0:s, :])
                v.drain()
                s, a = 2 * s, 1 - a
            nc.vector.tensor_tensor(before[:, :, :], count[a][:, :, :], p_all[:, :, :], ALU.subtract)
            nc.vector.tensor_scalar(padded_i[:, :], count[a][:, kt - 1, :], float(P - 1), None, ALU.add)
            v.drain()
            nc.vector.tensor_scalar(padded_i[:, :], padded_i[:, :], 7, 7, ALU.arith_shift_right, ALU.arith_shift_left)
            v.drain()
            nc.vector.tensor_copy(padded[:, :], padded_i[:, :])
            v.drain()
            nc.vector.tensor_tensor_scan(end[:, :], padded[:, :], g.zero_row[:, 0:ne], 0.0, ALU.add, ALU.add)
            nc.vector.scalar_tensor_tensor(place[:, :, :], p_in[:, :, :], -1.0, before[:, :, :], ALU.add, ALU.add)
            v.drain()
            nc.vector.tensor_tensor(base[:, :], end[:, :], padded[:, :], ALU.subtract)
            if capacity is not None:
                nc.vector.tensor_tensor(eq[:, :, :], place[:, :, :], hot[:, 0, :, :], ALU.mult)
                v.drain()
                nc.vector.tensor_reduce(pos[:, :], eq[:, :, :], AX.X, ALU.add)
                v.drain()
                nc.vector.scalar_tensor_tensor(r.gate[:, 0, :], pos[:, :], float(capacity), r.gate[:, 0, :], ALU.is_lt, ALU.mult)
            v.drain()
            nc.vector.tensor_tensor(place[:, :, :], place[:, :, :], base[:, :].unsqueeze(1).to_broadcast([P, kt, ne]), ALU.add)
            v.drain()
            nc.vector.tensor_tensor(place[:, :, :], place[:, :, :], hot[:, :, :, :].rearrange("p k t e -> p (k t) e"), ALU.mult)
            v.drain()
            nc.vector.tensor_reduce(slot[:, :], place[:, :, :], AX.X, ALU.add)
            v.drain()
            nc.vector.tensor_copy(r.slot[:, :, :].rearrange("p k t -> p (k t)"), slot[:, :])
            nc.vector.tensor_tensor(passed[:, :, :], block0[:, :].unsqueeze(2).to_broadcast([1, nb, ne]),
                                    end[0:1, :].unsqueeze(1).to_broadcast([1, nb, ne]), ALU.is_ge)
            v.drain()
            nc.vector.tensor_reduce(owner[:, :], passed[:, :, :], AX.X, ALU.add)
            v.drain()
            nc.vector.tensor_scalar(r.expert[:, :], owner[:, :], float(ne - 1), None, ALU.min)


def scatter_tokens(nc, g, rows, r, slots):
    with Phase(nc, "spread") as ph:
        sent = ph.sem("sent")
        block = ph.block()

        @block.gpsimd
        def _(pool):
            for k in range(r.choices):
                for t in range(T):
                    pool.indirect_dma_start(slots, bass.IndirectOffsetOnAxis(ap=r.slot[:, k, t:t + 1], axis=0),
                                            rows[:, t, :], None).then_inc(sent, 16)
            pool.wait_ge(sent, 16 * r.choices * T)


def expert_blocks(nc, g, slots, results, r, w1, b1, w2, b2, func, affine=None):
    ne, _, fm = w1.shape
    m_all = fm // P
    banks = m_all // 4
    nb = r.blocks
    assert nb % 2 == 0
    with Phase(nc, "ffn") as ph:
        x = ph.sb("x", [P, 2, D])
        w1_sb, w2_sb = ph.sb("w1", [P, 2, 2, fm]), ph.sb("w2", [P, 2, m_all, D])
        b1_sb, b2_sb, aff = ph.sb("b1", [P, 2, m_all]), ph.sb("b2", [P, 2, D]), ph.sb("aff", [P, 2, 4])
        xt = ph.sb("xt", [P, 2, 2, P])
        ht = ph.sb("ht", [P, 2, m_all, P])
        y = ph.sb("y", [P, 2, D])
        p_x = [ph.ps(f"p_x{u}", [P, 2, 2, P]) for u in range(2)]
        p_h = [[ph.ps(f"p_h{u}{b}", [P, 4, P]) for b in range(2)] for u in range(2)]
        p_y = [ph.ps(f"p_y{u}", [P, 512]) for u in range(2)]
        x_in, w1_in, w2_in = ([ph.sem(f"{s}{u}") for u in range(2)] for s in ("x_in", "w1_in", "w2_in"))
        turned, xt_ready, h_done, h_ready, y_done, y_ready = (ph.sem(s) for s in ("turned", "xt_ready", "h_done", "h_ready", "y_done", "y_ready"))
        stored = [ph.sem(f"stored{u}") for u in range(2)]
        turn, y_free = ph.sem("turn"), ph.sem("y_free")
        block = ph.block()
        n_w1 = 2 if affine is None else 4

        @block.sync
        def _(sp):
            sp.sem_inc(h_ready, 2 * banks)
            sp.sem_inc(y_done, 2)
            sp.sem_inc(y_ready, 2)
            sp.sem_inc(y_free, 2)
            registers = [sp.alloc_register(f"{ph.name}_expert{u}") for u in range(2)]
            with sp.Fori(0, nb // 2) as i:
                if ne > 1:
                    sp.load(registers, r.expert[0:1, bass.ds(i * 2, 2)])
                    experts = [sp.snap(e, min_val=0, max_val=ne - 1) for e in registers]
                else:
                    experts = [0, 0]
                for u in range(2):
                    one = bass.ds(experts[u], 1)
                    sp.wait_ge(h_ready, i * (2 * banks) + (u + 1) * banks)
                    sp.sem_inc(turn, 1)
                    sp.dma_start(x[:, u, :], slots[bass.ds((i * 2 + u) * P, P), :]).then_inc(x_in[u], 16)
                    sp.dma_start(w1_sb[:, u, :, :], w1[one, :, :].rearrange("a (k p) n -> p (a k) n", p=P)).then_inc(w1_in[u], 16)
                    sp.dma_start(b1_sb[:, u, :], b1[one, :, :].rearrange("a p m -> p (a m)")).then_inc(w1_in[u], 16)
                    if affine is not None:
                        for n in range(2):
                            sp.dma_start(aff[:, u, 2 * n:2 * n + 2], affine[n][one, :, :].rearrange("a p m -> p (a m)")).then_inc(w1_in[u], 16)
                for u in range(2):
                    one = bass.ds(experts[u], 1)
                    sp.wait_ge(y_ready, i * 2 + (u + 1))
                    sp.sem_inc(turn, 1)
                    sp.dma_start(w2_sb[:, u, :, :], w2[one, :, :].rearrange("a (k p) n -> p (a k) n", p=P)).then_inc(w2_in[u], 16)
                    sp.dma_start(b2_sb[:, u, :], b2[one, :].rearrange("a n -> (a n)").partition_broadcast(P)).then_inc(w2_in[u], 16)

        @block.gpsimd
        def _(pool):
            with pool.Fori(0, nb // 2) as i:
                for u in range(2):
                    pool.wait_ge(y_ready, i * 2 + (u + 3))
                    pool.sem_inc(turn, 1)
                    pool.dma_start(results[bass.ds((i * 2 + u) * P, P), :], y[:, u, :]).then_inc(stored[u], 16)
                    pool.wait_ge(stored[u], i * 16 + 16)
                    pool.sem_inc(y_free, 1)

        @block.tensor
        def _(pe):
            with pe.Fori(0, nb // 2) as i:
                for u in range(2):
                    pe.wait_ge(x_in[u], i * 16 + 16)
                    for k in range(2):
                        ins = nc.tensor.transpose(p_x[u][:, 0, k, :], x[:, u, k * P:(k + 1) * P], g.ident[:, :])
                    ins.then_inc(turned, 1)
                for u in range(2):
                    pe.wait_ge(w1_in[u], i * (16 * n_w1) + 16 * n_w1)
                    pe.wait_ge(xt_ready, i * 2 + (u + 1))
                    for m in range(m_all):
                        for k in range(2):
                            ins = nc.tensor.matmul(p_h[u][m // 4][:, m % 4, :], w1_sb[:, u, k, m * P:(m + 1) * P], xt[:, u, k, :],
                                                   start=(k == 0), stop=(k == 1))
                        if m % 4 == 3:
                            ins.then_inc(h_done, 1)
                for u in range(2):
                    pe.wait_ge(w2_in[u], i * 32 + 32)
                    for m in range(m_all):
                        if m % 4 == 0:
                            pe.wait_ge(h_ready, i * (2 * banks) + (2 * banks + u * banks + m // 4 + 1))
                        ins = nc.tensor.matmul(p_y[u][:, 0:D], ht[:, u, m, :], w2_sb[:, u, m, :], start=(m == 0), stop=(m == m_all - 1))
                    ins.then_inc(y_done, 1)

        @block.scalar
        def _(act):
            with act.Fori(0, nb // 2) as i:
                for u in range(2):
                    act.wait_ge(y_done, i * 2 + (u + 1))
                    for b in range(banks):
                        act.wait_ge(h_done, i * (2 * banks) + (u * banks + b + 1))
                        for m in range(4 * b, 4 * b + 4):
                            ins = nc.scalar.activation(ht[:, u, m, :], p_h[u][b][:, m % 4, :], func, bias=b1_sb[:, u, m:m + 1])
                        ins.then_inc(h_ready, 1)

        @block.vector
        def _(v):
            with v.Fori(0, nb // 2) as i:
                for u in range(2):
                    v.wait_ge(turned, i * 2 + (u + 1))
                    if affine is None:
                        nc.vector.tensor_copy(xt[:, u, :, :], p_x[u][:, 0, :, :]).then_inc(xt_ready, 1)
                    else:
                        v.wait_ge(w1_in[u], i * (16 * n_w1) + 16 * n_w1)
                        for k in range(2):
                            ins = nc.vector.tensor_scalar(xt[:, u, k, :], p_x[u][:, 0, k, :], aff[:, u, k:k + 1], aff[:, u, 2 + k:3 + k],
                                                          ALU.mult, ALU.add)
                        ins.then_inc(xt_ready, 1)
                for u in range(2):
                    v.wait_ge(y_free, i * 2 + (u + 1))
                    v.wait_ge(y_done, i * 2 + (u + 3))
                    nc.vector.tensor_tensor(y[:, u, :], p_y[u][:, 0:D], b2_sb[:, u, :], ALU.add).then_inc(y_ready, 1)


def combine(nc, g, results, source, r, into, xn=None, guard=False):
    with Phase(nc, "gather") as ph:
        got = ph.sb("got", [P, r.choices, T, D])
        S = 5
        ok, high, low = (ph.sb(s, [P, S, D], I32) for s in ("ok", "high", "low"))
        clean, top, bottom = ph.sb("clean", [P, T, D]), ph.sb("top", [P, S, D]), ph.sb("bottom", [P, S, D])
        assert T % S == 0
        arrived = [ph.sem(f"arrived{n}") for n in range(r.choices * T)]
        block = ph.block()

        @block.gpsimd
        def _(pool):
            for k in range(r.choices):
                for t in range(T):
                    pool.indirect_dma_start(got[:, k, t, :], None, results,
                                            bass.IndirectOffsetOnAxis(ap=source[:, k, t:t + 1], axis=0)).then_inc(arrived[k * T + t], 16)

        @block.vector
        def _(v):
            if guard:
                nc.vector.memset(clean[:, :, :], 0.0)
                nc.vector.memset(top[:, :, :], 1e4)
                nc.vector.memset(bottom[:, :, :], -1e4)
                v.drain()
            if xn is not None:
                nc.vector.tensor_tensor(into[:, :, :], into[:, :, :], xn[:, :, :], ALU.add)
            for k in range(r.choices):
                v.drain()
                for t in range(T):
                    v.wait_ge(arrived[k * T + t], 16)
                    if not guard:
                        nc.vector.scalar_tensor_tensor(into[:, t, :], got[:, k, t, :], r.gate[:, k, t:t + 1], into[:, t, :], ALU.mult, ALU.add)
                        continue
                    nc.vector.tensor_scalar(got[:, k, t, :], got[:, k, t, :], r.gate[:, k, t:t + 1], None, ALU.mult)
                    if (t + 1) % S:
                        continue
                    some = slice(t + 1 - S, t + 1)
                    y = got[:, k, some, :]
                    v.drain()
                    nc.vector.tensor_tensor(ok[:, :, :], y, y, ALU.is_equal)
                    nc.vector.tensor_scalar(high[:, :, :], y, 3.4028234e38, None, ALU.is_gt)
                    nc.vector.tensor_scalar(low[:, :, :], y, -3.4028234e38, None, ALU.is_lt)
                    v.drain()
                    nc.vector.copy_predicated(clean[:, some, :], ok[:, :, :], y)
                    v.drain()
                    nc.vector.copy_predicated(clean[:, some, :], high[:, :, :], top[:, :, :])
                    v.drain()
                    nc.vector.copy_predicated(clean[:, some, :], low[:, :, :], bottom[:, :, :])
                    v.drain()
                    nc.vector.tensor_tensor(into[:, some, :], into[:, some, :], clean[:, some, :], ALU.add)


def capacity_ffn(nc, g, i):
    chosen = max(max(1, int(0.5 * N)) - 1, 1)
    with Phase(nc, "cap") as ph:
        xn = ph.sb("xn", [P, T, D])
        r = Routes(ph, 1, (chosen + P - 1) // P)
        source = ph.sb("source_i", [P, 1, T], I32)
        r.source = source[:, 0, :]
        slots, results = g.dram("cap_slots", [NP, D]), g.dram("cap_results", [r.blocks * P, D])
        layernorm(nc, g, g.X, xn)
        rank_tokens(nc, g, xn, i["L0_ffn_wr"].rearrange("d o -> (d o)"), i["L0_ffn_br"], chosen, r)
        scatter_tokens(nc, g, xn, r, slots)
        expert_blocks(nc, g, slots, results, r, i["L0_ffn_w1"].rearrange("(a d) f -> a d f", a=1), i["L0_ffn_b1"],
                      i["L0_ffn_w2"].rearrange("(a d) f -> a d f", a=1), i["L0_ffn_b2"].rearrange("(a d) -> a d", a=1),
                      ACT.Gelu_apprx_tanh)
        combine(nc, g, results, source, r, g.X, xn=xn)


def blocks_for(choices, experts):
    need = (NP * choices + experts * (P - 1)) // P
    return need + need % 2


def switch_ffn(nc, g, i):
    ne = i["L1_ffn_gate_w"].shape[1]
    capacity = -(-5 * N // (4 * ne))
    with Phase(nc, "switch") as ph:
        xn, xt = ph.sb("xn", [P, T, D]), ph.sb("xt", [P, T, 2, P])
        r = Routes(ph, 1, blocks_for(1, ne))
        slots, results = g.dram("switch_slots", [r.blocks * P, D]), g.dram("switch_results", [r.blocks * P, D])
        layernorm(nc, g, g.X, xn, turned=xt)
        choose_experts(nc, g, xt, i["L1_ffn_gate_w"], i["L1_ffn_gate_b"], r, slots, capacity=capacity)
        scatter_tokens(nc, g, xn, r, slots)
        expert_blocks(nc, g, slots, results, r, i["L1_ffn_w1"], i["L1_ffn_b1"], i["L1_ffn_w2"], i["L1_ffn_b2"], ACT.Relu)
        combine(nc, g, results, r.slot, r, g.X, guard=True)


def top2_gelu_ffn(nc, g, i):
    ne = i["L2_ffn_Wr"].shape[1]
    with Phase(nc, "top2") as ph:
        xn, xt = ph.sb("xn", [P, T, D]), ph.sb("xt", [P, T, 2, P])
        r = Routes(ph, 2, blocks_for(2, ne))
        slots, results = g.dram("gelu_slots", [r.blocks * P, D]), g.dram("gelu_results", [r.blocks * P, D])
        layernorm(nc, g, g.X, xn, turned=xt)
        choose_experts(nc, g, xt, i["L2_ffn_Wr"], i["L2_ffn_br"], r, slots)
        layernorm(nc, g, xn, xn)
        scatter_tokens(nc, g, xn, r, slots)
        expert_blocks(nc, g, slots, results, r, i["L2_ffn_W1"], i["L2_ffn_b1"], i["L2_ffn_W2"], i["L2_ffn_b2"], ACT.Gelu,
                      affine=(i["L2_ffn_ln_g"], i["L2_ffn_ln_b"]))
        combine(nc, g, results, r.slot, r, g.X)


def top2_relu_ffn(nc, g, i):
    ne = i["L3_ffn_gate_w"].shape[1]
    with Phase(nc, "moe") as ph:
        xn, xt = ph.sb("xn", [P, T, D]), ph.sb("xt", [P, T, 2, P])
        r = Routes(ph, 2, blocks_for(2, ne))
        slots, results = g.dram("relu_slots", [r.blocks * P, D]), g.dram("relu_results", [r.blocks * P, D])
        layernorm(nc, g, g.X, xn, turned=xt)
        choose_experts(nc, g, xt, i["L3_ffn_gate_w"], i["L3_ffn_gate_b"], r, slots)
        scatter_tokens(nc, g, xn, r, slots)
        expert_blocks(nc, g, slots, results, r, i["L3_ffn_w1"], i["L3_ffn_b1"], i["L3_ffn_w2"], i["L3_ffn_b2"], ACT.Relu)
        combine(nc, g, results, r.slot, r, xn)
        layernorm(nc, g, xn, xn, gamma=i["L3_ffn_gamma"], beta=i["L3_ffn_beta"], add=g.X)


BANKS = 6
WIDE = D + HD + 1
assert U % BANKS == 0


def scale_rows(nc, g, x, y, acc, table, relu=False):
    groups = Turn.groups
    with Phase(nc, "scale") as ph:
        turn = Turn(nc, g, ph, y, acc)
        ready, written = ph.sem("ready"), ph.sem("written")
        block = ph.block()

        @block.vector
        def _(v):
            for tiles in groups:
                for t in tiles:
                    if relu:
                        ins = nc.vector.tensor_scalar(y[:, t, :], x[:, t, :], 0.0, g.dinv[:, t:t + 1], ALU.max, ALU.mult)
                    else:
                        ins = nc.vector.tensor_scalar(y[:, t, :], x[:, t, :], g.dinv[:, t:t + 1], None, ALU.mult)
                ins.then_inc(ready, 1)

        @block.sync
        def _(sp):
            for n, tiles in enumerate(groups):
                some = slice(tiles[0], tiles[-1] + 1)
                sp.wait_ge(ready, n + 1)
                sp.dma_start(table.rearrange("(t p) f -> p t f", p=P)[:, some, :], y[:, some, :]).then_inc(written, 16)
            sp.wait_ge(written, 16 * len(groups))

        @block.tensor
        def _(pe):
            turn.turn(pe, ready)

        @block.scalar
        def _(act):
            for n in range(len(groups)):
                turn.take(act, n)


def gcn_edges(nc, g, table, acc):
    with Phase(nc, "gcn") as ph:
        idx = ph.sb("idx", [P, U], I32)
        got = ph.sb("got", [P, U, D])
        hot = ph.sb("hot", [P, U, P])
        p_sum = [ph.ps(f"p_sum{b}", [P, 512]) for b in range(BANKS)]
        idx_set, turn, hot_ready, agg_done, added = (ph.sem(s) for s in ("idx_set", "turn", "hot_ready", "agg_done", "added"))
        gathered = [ph.sem(f"gathered{u}") for u in range(U)]
        block = ph.block()

        @block.sync
        def _(sp):
            sp.sem_inc(agg_done, U)
            sp.sem_inc(added, U)

        @block.gpsimd
        def _(pool):
            gather_loop(nc, pool, ph, g.src, table, got, idx, gathered, agg_done, idx_set, turn)

        @block.tensor
        def _(pe):
            with pe.Fori(0, EC // U) as i:
                for u in range(U):
                    pe.wait_ge(added, i * U + (u - BANKS + 1 + U))
                    pe.wait_ge(hot_ready, i * U + (u + 1))
                    pe.wait_ge(gathered[u], i * 16 + 16)
                    for half in range(2):
                        ins = nc.tensor.matmul(p_sum[u % BANKS][:, half * P:(half + 1) * P], got[:, u, half * P:(half + 1) * P],
                                               hot[:, u, :], start=True, stop=True)
                    ins.then_inc(agg_done, 1)

        @block.vector
        def _(v):
            def each(i, u):
                v.wait_ge(agg_done, i * U + (u + 1))
                c = bass.ds(i * U + u, 1)
                nc.vector.tensor_scalar(hot[:, u, :], g.iota_free[:, :], g.dst[:, c], g.weight[:, c], ALU.is_equal, ALU.mult)\
                    .then_inc(hot_ready, 1)

            def add(i, u, tile):
                v.wait_ge(added, i * U + (u + U))
                v.wait_ge(agg_done, i * U + (u + 1 + U))
                a = acc[:, bass.ds(tile, 1), :, :].rearrange("p a h n -> p (a h n)")
                nc.vector.tensor_tensor(a, a, p_sum[u % BANKS][:, 0:D], ALU.add).then_inc(added, 1)

            add_loop(nc, v, g, ph, each, add)


def gcn_linear(nc, g, agg, w, b, z):
    with Phase(nc, "lin") as ph:
        w_sb, b_row = ph.sb("w", [P, 2, D]), ph.sb("b", [P, D])
        p_z = [ph.ps(f"p_z{n}", [P, 512]) for n in range(4)]
        loaded, done, taken = ph.sem("loaded"), ph.sem("done"), ph.sem("taken")
        block = ph.block()

        @block.sync
        def _(sp):
            sp.dma_start(w_sb[:, :, :], w.rearrange("(k p) n -> p k n", p=P)).then_inc(loaded, 16)
            sp.dma_start(b_row[:, :], row(b)).then_inc(loaded, 16)

        @block.tensor
        def _(pe):
            pe.wait_ge(loaded, 32)
            for t in range(T):
                if t >= 4:
                    pe.wait_ge(taken, t - 3)
                for k in range(2):
                    ins = nc.tensor.matmul(p_z[t % 4][:, 0:D], agg[:, t, k, :], w_sb[:, k, :], start=(k == 0), stop=(k == 1))
                ins.then_inc(done, 1)

        @block.vector
        def _(v):
            v.wait_ge(loaded, 32)
            for t in range(T):
                v.wait_ge(done, t + 1)
                nc.vector.scalar_tensor_tensor(z[:, t, :], p_z[t % 4][:, 0:D], g.dinv[:, t:t + 1], b_row[:, :], ALU.mult, ALU.add)\
                    .then_inc(taken, 1)


def softmax_into(nc, g, z, into):
    with Phase(nc, "soft") as ph:
        top, total = ph.sb("top", [P, T]), ph.sb("total", [P, T])
        ready, done = ph.sem("ready"), ph.sem("done")
        block = ph.block()

        @block.vector
        def _(v):
            nc.vector.tensor_reduce(top[:, :], z[:, :, :], AX.X, ALU.max)
            v.drain()
            nc.vector.tensor_scalar(top[:, :], top[:, :], -1.0, None, ALU.mult).then_inc(ready, 1)
            v.wait_ge(done, T)
            nc.vector.reciprocal(total[:, :], total[:, :])
            v.drain()
            for t in range(T):
                nc.vector.scalar_tensor_tensor(into[:, t, :], z[:, t, :], total[:, t:t + 1], into[:, t, :], ALU.mult, ALU.add)

        @block.scalar
        def _(act):
            act.wait_ge(ready, 1)
            for t in range(T):
                nc.scalar.activation(z[:, t, :], z[:, t, :], ACT.Exp, bias=top[:, t:t + 1], accum_out=total[:, t:t + 1]).then_inc(done, 1)


def relu_into(nc, g, z, xn, into):
    with Phase(nc, "relu") as ph:
        block = ph.block()

        @block.vector
        def _(v):
            nc.vector.tensor_tensor(into[:, :, :], into[:, :, :], xn[:, :, :], ALU.add)
            v.drain()
            nc.vector.scalar_tensor_tensor(into[:, :, :], z[:, :, :], 0.0, into[:, :, :], ALU.max, ALU.add)


def gcn_softmax(nc, g, i):
    with Phase(nc, "gcn2") as ph:
        y, z, acc = ph.sb("y", [P, T, D]), ph.sb("z", [P, T, D]), ph.sb("acc", [P, T, 2, P])
        layernorm(nc, g, g.X, z)
        for n in (1, 2):
            table = g.dram(f"gcn_table{n}", [NP, D])
            scale_rows(nc, g, z, y, acc, table, relu=(n == 2))
            gcn_edges(nc, g, table, acc)
            gcn_linear(nc, g, acc, i[f"L2_gnn_W{n}"], i[f"L2_gnn_b{n}"], z)
        softmax_into(nc, g, z, g.X)


def gcn_residual(nc, g, i):
    with Phase(nc, "gcn1") as ph:
        xn, y, z, acc = ph.sb("xn", [P, T, D]), ph.sb("y", [P, T, D]), ph.sb("z", [P, T, D]), ph.sb("acc", [P, T, 2, P])
        table = g.dram("gcn_table3", [NP, D])
        layernorm(nc, g, g.X, xn)
        scale_rows(nc, g, xn, y, acc, table)
        gcn_edges(nc, g, table, acc)
        gcn_linear(nc, g, acc, i["L3_gnn_W"], i["L3_gnn_b"], z)
        relu_into(nc, g, z, xn, g.X)


def relation_tables(nc, g, xt, w, wt, attn_src, attn_dst, h_table, src_table, score_dst):
    S2 = 2 * HD
    with Phase(nc, "rel") as ph:
        w_sb, wt_sb = ph.sb("w", [P, R, 2, D]), ph.sb("wt", [P, R, 2, D])
        heads = ph.sb("heads", [P, 2, S2])
        proj = ph.sb("proj", [P, 2, R, S2])
        rows = ph.sb("rows", [P, 2, R, D])
        scores = ph.sb("scores", [P, T, R, HD])
        p_proj = ph.ps("p_proj", [P, 2, R, S2])
        p_score = [ph.ps(f"p_score{b}", [P, 512]) for b in range(2)]
        p_rows = [ph.ps(f"p_rows{b}", [P, 2, D]) for b in range(4)]
        blanked, heads_in, w_in, wt_in = ph.sem("blanked"), ph.sem("heads_in"), ph.sem("w_in"), ph.sem("wt_in")
        proj_done, proj_ready, score_done, score_taken = (ph.sem(s) for s in ("proj_done", "proj_ready", "score_done", "score_taken"))
        rows_done, rows_taken, scores_written = ph.sem("rows_done"), ph.sem("rows_taken"), ph.sem("scores_written")
        written = [ph.sem(f"written{b}") for b in range(2)]
        block = ph.block()
        per_tile = R // 2

        @block.sync
        def _(sp):
            sp.dma_start(w_sb[:, :, :, :], w.rearrange("r (k p) f -> p (r k) f", p=P)).then_inc(w_in, 16)
            sp.wait_ge(blanked, 1)
            for n, attn in enumerate((attn_src, attn_dst)):
                for h in range(HD):
                    p0 = h * DH % P
                    sp.dma_start(heads[p0:p0 + DH, h * DH // P, n * HD + h:n * HD + h + 1],
                                 attn[h:h + 1, :].rearrange("a d -> d a")).then_inc(heads_in, 16)
            sp.dma_start(wt_sb[:, :, :, :], wt.rearrange("r (k p) o -> p (r k) o", p=P)).then_inc(wt_in, 16)
            h_view = h_table.rearrange("(r t p) f -> t p r f", r=R, p=P)
            for t in range(T):
                sp.wait_ge(rows_taken, per_tile * (t + 1))
                sp.dma_start(h_view[t, :, :, :], rows[:, t % 2, :, :]).then_inc(written[t % 2], 16)
            sp.wait_ge(score_taken, 2 * T)
            for r in range(R):
                sp.dma_start(src_table[r * NP:(r + 1) * NP, :].rearrange("(t p) h -> p t h", p=P), scores[:, :, r, :])\
                    .then_inc(scores_written, 16)
            sp.wait_ge(scores_written, 16 * R)
            for b in range(2):
                sp.wait_ge(written[b], 16 * ((T + 1 - b) // 2))

        @block.tensor
        def _(pe):
            pe.wait_ge(w_in, 16)
            pe.wait_ge(heads_in, 16 * S2)
            for half in range(2):
                for r in range(R):
                    for k in range(2):
                        ins = nc.tensor.matmul(p_proj[:, half, r, :], w_sb[:, r, k, half * P:(half + 1) * P], heads[:, k, :],
                                               start=(k == 0), stop=(k == 1))
            ins.then_inc(proj_done, 1)
            pe.wait_ge(proj_ready, 1)
            for t in range(T):
                if t >= 2:
                    pe.wait_ge(score_taken, 2 * (t - 1))
                for k in range(2):
                    ins = nc.tensor.matmul(p_score[t % 2][:, 0:R * S2], xt[:, t, k, :], proj[:, k, :, :].rearrange("p r s -> p (r s)"),
                                           start=(k == 0), stop=(k == 1))
                ins.then_inc(score_done, 1)
            pe.wait_ge(wt_in, 16)
            for t in range(T):
                for b in range(per_tile):
                    n = t * per_tile + b
                    if n >= 4:
                        pe.wait_ge(rows_taken, n - 3)
                    for r in range(2):
                        for k in range(2):
                            ins = nc.tensor.matmul(p_rows[n % 4][:, r, :], xt[:, t, k, :], wt_sb[:, 2 * b + r, k, :],
                                                   start=(k == 0), stop=(k == 1))
                    ins.then_inc(rows_done, 1)

        def take(n, copy, eng):
            t, b = n // per_tile, n % per_tile
            if t >= 2:
                eng.wait_ge(written[t % 2], 16 * (t // 2))
            eng.wait_ge(rows_done, n + 1)
            if n:
                eng.wait_ge(rows_taken, n)
            copy(rows[:, t % 2, 2 * b:2 * b + 2, :], p_rows[n % 4][:, :, :]).then_inc(rows_taken, 1)

        @block.scalar
        def _(act):
            for n in range(1, T * per_tile, 2):
                take(n, nc.scalar.copy, act)

        @block.vector
        def _(v):
            nc.vector.memset(heads[:, :, :], 0.0).then_inc(blanked, 1)
            v.wait_ge(proj_done, 1)
            nc.vector.tensor_copy(proj[:, :, :, :], p_proj[:, :, :, :]).then_inc(proj_ready, 1)
            for t in range(T):
                v.wait_ge(score_done, t + 1)
                both = p_score[t % 2][:, 0:R * S2].rearrange("p (r s) -> p r s", r=R)
                nc.vector.tensor_copy(scores[:, t, :, :], both[:, :, 0:HD]).then_inc(score_taken, 1)
                nc.vector.tensor_copy(score_dst[:, t, :].rearrange("p (r h) -> p r h", r=R), both[:, :, HD:S2]).then_inc(score_taken, 1)
            for n in range(0, T * per_tile, 2):
                take(n, nc.vector.tensor_copy, v)


def edge_scores(nc, g, src_table, score_dst, scores):
    S = R * HD
    with Phase(nc, "score") as ph:
        idx = ph.sb("idx", [P, U], I32)
        got = ph.sb("got", [P, U, HD])
        hot = ph.sb("hot", [P, U, P], BF16)
        parts, left = ph.sb("parts", [P, T, 3, S], BF16), ph.sb("left", [P, T, S])
        rel_idx = ph.sb("rel_idx", [P, R])
        rel, picked, s = ph.sb("rel", [P, EC, R]), ph.sb("picked", [P, U, R, HD]), ph.sb("s", [P, U, HD])
        groups = U // G
        p_hot = [ph.ps(f"p_hot{b}", [P, G, P], BF16) for b in range(groups)]
        p_dst = [ph.ps(f"p_dst{b}", [P, G, 2 * S]) for b in range(groups)]
        idx_set, turn, hot_ready, turned, copied = (ph.sem(x) for x in ("idx_set", "turn", "hot_ready", "turned", "copied"))
        split, dst_done, picked_done, got_used, iota_made = (
            ph.sem(x) for x in ("split", "dst_done", "picked_done", "got_used", "iota_made"))
        gathered = [ph.sem(f"gathered{u}") for u in range(U)]
        block = ph.block()

        @block.sync
        def _(sp):
            sp.sem_inc(got_used, U)
            sp.sem_inc(turned, groups)
            sp.sem_inc(copied, groups)
            sp.sem_inc(picked_done, groups)

        @block.gpsimd
        def _(pool):
            nc.gpsimd.iota(rel_idx[:, :], [[1, R]], base=0, channel_multiplier=0,
                           allow_small_or_imprecise_dtypes=True).then_inc(iota_made, 1)
            gather_loop(nc, pool, ph, g.hrow, src_table, got, idx, gathered, got_used, idx_set, turn)

        @block.tensor
        def _(pe):
            registers = [pe.alloc_register(f"{ph.name}_pe_tile{u}") for u in range(U)]
            pe.wait_ge(split, 1)
            with pe.Fori(0, EC // U) as i:
                tiles = tiles_of(pe, g, registers, i)
                for b in range(groups):
                    pe.wait_ge(hot_ready, i * groups + (b + 1))
                    pe.wait_ge(copied, i * groups + (b + 1))
                    for u in range(b * G, (b + 1) * G):
                        ins = nc.tensor.transpose(p_hot[b][:, u % G, :], hot[:, u, :], g.ident_b[:, :])
                    ins.then_inc(turned, 1)
                for b in range(groups):
                    pe.wait_ge(picked_done, i * groups + (b + 1))
                    pe.wait_ge(copied, i * groups + (b + 1 + groups))
                    for u in range(b * G, (b + 1) * G):
                        for k in range(3):
                            ins = nc.tensor.matmul(p_dst[b][:, u % G, 0:S],
                                                   g.attrs_t[:, bass.ds(i * U + u, 1), :].rearrange("p a e -> p (a e)"),
                                                   parts[:, bass.ds(tiles[u], 1), k, :].rearrange("p a s -> p (a s)"),
                                                   start=(k == 0), stop=(k == 2))
                    ins.then_inc(dst_done, 1)

        @block.scalar
        def _(act):
            with act.Fori(0, EC // U) as i:
                for b in range(groups):
                    act.wait_ge(turned, i * groups + (b + 1 + groups))
                    act.sem_inc(turn, 1)
                    nc.scalar.copy(g.attrs_t[:, bass.ds(i * U + b * G, G), :], p_hot[b][:, :, :]).then_inc(copied, 1)

        @block.vector
        def _(v):
            split3(nc, v, score_dst[:, :, :], [parts[:, :, k, :] for k in range(3)], left[:, :, :])
            v.drain()
            v.sem_inc(split, 1)
            v.wait_ge(iota_made, 1)
            nc.vector.tensor_tensor(rel[:, :, :], rel_idx[:, :].unsqueeze(1).to_broadcast([P, EC, R]),
                                    g.etype[:, :].unsqueeze(2).to_broadcast([P, EC, R]), ALU.is_equal)
            v.drain()
            with v.Fori(0, EC // U) as i:
                for b in range(groups):
                    v.wait_ge(turned, i * groups + (b + 1))
                    for u in range(b * G, (b + 1) * G):
                        ins = nc.vector.tensor_scalar(hot[:, u, :], g.iota_free[:, :], g.dst[:, bass.ds(i * U + u, 1)], None,
                                                      ALU.is_equal)
                    ins.then_inc(hot_ready, 1)
                for b in range(groups):
                    some = slice(b * G, (b + 1) * G)
                    v.wait_ge(dst_done, i * groups + (b + 1))
                    nc.vector.tensor_tensor(picked[:, some, :, :], p_dst[b][:, :, 0:S].rearrange("p u (r h) -> p u r h", r=R),
                                            rel[:, bass.ds(i * U + b * G, G), :].unsqueeze(3).to_broadcast([P, G, R, HD]),
                                            ALU.mult).then_inc(picked_done, 1)
                    v.drain()
                    nc.vector.tensor_reduce(s[:, some, :], picked[:, some, :, :].rearrange("p u r h -> p u h r"), AX.X, ALU.add)
                    v.drain()
                    for u in range(b * G, (b + 1) * G):
                        v.wait_ge(gathered[u], i * 16 + 16)
                        v.sem_inc(turn, 1)
                    nc.vector.tensor_tensor(scores[:, bass.ds(i * U + b * G, G), :], s[:, some, :], got[:, some, :], ALU.add)
                    v.drain()
                    v.sem_inc(got_used, G)
            v.drain()
            nc.vector.scalar_tensor_tensor(scores[:, :, :], scores[:, :, :], 0.2, scores[:, :, :], ALU.mult, ALU.max)


def find_runs(nc, g, scores, top, last, broken):
    K = 3
    EK = EC // K
    SL = K * HD
    with Phase(nc, "runs") as ph:
        turned_s, turned_d = ph.sb("turned_s", [EK, SL, P]), ph.sb("turned_d", [EK, K, P])
        same, ends = ph.sb("same", [EK, K, P]), ph.sb("ends", [EK, K, P])
        drops, drop_sum, total = ph.sb("drops", [EK, K, P]), ph.sb("drop_sum", [EK, 1]), ph.sb("total", [1, 1])
        p_turned, p_back = ph.ps("p_turned", [P, SL + K + 1, P]), ph.ps("p_total", [1, 1])
        turned, copied, scanned, returned, counted, total_done, back_free = (
            ph.sem(x) for x in ("turned", "copied", "scanned", "returned", "counted", "total_done", "back_free"))
        block = ph.block()

        @block.tensor
        def _(pe):
            for k in range(K):
                for h in range(HD):
                    nc.tensor.transpose(p_turned[0:EK, k * HD + h, :], scores[:, k * EK:(k + 1) * EK, h], g.ident[:, :])
                ins = nc.tensor.transpose(p_turned[0:EK, SL + k, :], g.dst[:, k * EK:(k + 1) * EK], g.ident[:, :])
            ins.then_inc(turned, 1)
            pe.wait_ge(copied, 2)
            pe.wait_ge(counted, 1)
            nc.tensor.matmul(p_back[:, :], drop_sum[:, :], g.ones[0:EK, 0:1], start=True, stop=True).then_inc(total_done, 1)
            pe.wait_ge(scanned, 1)
            for n in range(SL + K):
                given = turned_s[:, n, :] if n < SL else ends[:, n - SL, :]
                ins = nc.tensor.transpose(p_turned[:, n, 0:EK], given, g.ident[0:EK, 0:EK])
            ins.then_inc(returned, 1)

        @block.scalar
        def _(act):
            act.wait_ge(turned, 1)
            nc.scalar.copy(turned_s[:, 0:SL // 2, :], p_turned[0:EK, 0:SL // 2, :]).then_inc(copied, 1)

        @block.vector
        def _(v):
            v.wait_ge(turned, 1)
            nc.vector.tensor_copy(turned_d[:, :, :], p_turned[0:EK, SL:SL + K, :])
            nc.vector.tensor_copy(turned_s[:, SL // 2:SL, :], p_turned[0:EK, SL // 2:SL, :]).then_inc(copied, 1)
            v.drain()
            nc.vector.tensor_scalar(ends[:, :, :], turned_d[:, :, :], 0.0, float(2 * P), ALU.is_lt, ALU.mult)
            v.drain()
            nc.vector.tensor_tensor(turned_d[:, :, :], turned_d[:, :, :], ends[:, :, :], ALU.add)
            nc.vector.memset(same[:, :, 0:1], 0.0)
            nc.vector.memset(drops[:, :, 0:1], 0.0)
            v.drain()
            now, before = turned_d[:, :, 1:P], turned_d[:, :, 0:P - 1]
            nc.vector.tensor_tensor(same[:, :, 1:P], now, before, ALU.is_equal)
            nc.vector.tensor_tensor(drops[:, :, 1:P], now, before, ALU.is_lt)
            nc.vector.memset(ends[:, :, P - 1:P], 1.0)
            nc.vector.tensor_tensor(ends[:, :, 0:P - 1], now, before, ALU.not_equal)
            v.drain()
            nc.vector.tensor_reduce(drop_sum[:, :], drops[:, :, :].rearrange("p k e -> p (k e)"), AX.X, ALU.add).then_inc(counted, 1)
            v.wait_ge(copied, 2)
            for n in range(SL):
                ins = nc.vector.tensor_tensor_scan(turned_s[:, n, :], same[:, n // HD, :], turned_s[:, n, :], 0.0, ALU.mult, ALU.max)
            v.drain()
            v.sem_inc(scanned, 1)
            v.wait_ge(total_done, 1)
            nc.vector.tensor_copy(broken[:, :], p_back[:, :])
            v.wait_ge(returned, 1)
            for k in range(K):
                nc.vector.tensor_copy(top[:, k * EK:(k + 1) * EK, :], p_turned[:, k * HD:(k + 1) * HD, 0:EK].rearrange("p h c -> p c h"))
            nc.vector.tensor_copy(last[:, :].rearrange("p (k c) -> p k c", k=K), p_turned[:, SL:SL + K, 0:EK])


def peaks_of_runs(nc, g, top, last, amax):
    with Phase(nc, "peaks") as ph:
        hot = ph.sb("hot", [P, U, P])
        ends = ph.sb("ends", [P, EC])
        peak = ph.sb("peak", [P, G, T, HD])
        p_top = [ph.ps(f"p_top{b}", [P, 512]) for b in range(BANKS)]
        hot_ready, picked, taken, blanked = ph.sem("hot_ready"), ph.sem("picked"), ph.sem("taken"), ph.sem("blanked")
        block = ph.block()

        @block.sync
        def _(sp):
            sp.sem_inc(picked, U)

        @block.scalar
        def _(act):
            act.sem_inc(taken, U)

        @block.gpsimd
        def _(pool):
            nc.gpsimd.memset(peak[:, :, :, :], 0.0).then_inc(blanked, 1)

        @block.tensor
        def _(pe):
            with pe.Fori(0, EC // U) as i:
                for u in range(U):
                    pe.wait_ge(taken, i * U + (u - BANKS + 1 + U))
                    if u % G == 0:
                        pe.wait_ge(hot_ready, i * (U // G) + (u // G + 1))
                    nc.tensor.matmul(p_top[u % BANKS][:, 0:HD], hot[:, u, :],
                                     top[:, bass.ds(i * U + u, 1), :].rearrange("p a h -> p (a h)"),
                                     start=True, stop=True).then_inc(picked, 1)

        @block.vector
        def _(v):
            nc.vector.scalar_tensor_tensor(ends[:, :], g.dst[:, :], 1.0, last[:, :], ALU.add, ALU.mult)
            v.drain()
            nc.vector.tensor_scalar(ends[:, :], ends[:, :], -1.0, None, ALU.add)
            v.wait_ge(blanked, 1)
            v.drain()

            def each(i, u):
                if u % G == 0:
                    v.wait_ge(picked, i * U + (u + G))
                    nc.vector.tensor_tensor(hot[:, u:u + G, :], g.iota_free[:, :].unsqueeze(1).to_broadcast([P, G, P]),
                                            ends[:, bass.ds(i * U + u, G)].unsqueeze(2).to_broadcast([P, G, P]),
                                            ALU.is_equal).then_inc(hot_ready, 1)

            def add(i, u, tile):
                v.wait_ge(taken, i * U + (u - G + 1 + U))
                v.wait_ge(picked, i * U + (u + 1 + U))
                a = peak[:, u % G, bass.ds(tile, 1), :].rearrange("p a h -> p (a h)")
                nc.vector.tensor_tensor(a, a, p_top[u % BANKS][:, 0:HD], ALU.max).then_inc(taken, 1)

            add_loop(nc, v, g, ph, each, add)
            nc.vector.tensor_reduce(amax[:, :, :], peak[:, :, :, :].rearrange("p g t h -> p t h g"), AX.X, ALU.max)


def peaks_in_any_order(nc, g, scores, amax):
    HH = HD // 2
    with Phase(nc, "anyorder") as ph:
        hot = ph.sb("hot", [P, P])
        diag, peak = ph.sb("diag", [P, HD, P]), ph.sb("peak", [P, HD])
        p_max = ph.ps("p_max", [P, HD, P])
        ready, done, turn = ph.sem("ready"), ph.sem("done"), ph.sem("turn")
        block = ph.block()

        @block.tensor
        def _(pe):
            with pe.Fori(0, EC) as c:
                pe.wait_ge(ready, c + 1)
                for part in range(2):
                    some = slice(part * HH, (part + 1) * HH)
                    ins = nc.tensor.matmul(p_max[:, some, :].rearrange("p h e -> p (h e)"), hot[:, :],
                                           diag[:, some, :].rearrange("p h e -> p (h e)"), start=True, stop=True)
                ins.then_inc(done, 1)

        @block.vector
        def _(v):
            register = [v.alloc_register(f"{ph.name}_tile")]
            nc.vector.memset(amax[:, :, :], 0.0)
            with v.Fori(0, EC) as c:
                v.load(register, g.chunk_tile[0:1, bass.ds(c, 1)])
                tile = v.snap(register[0], min_val=0, max_val=T - 1)
                nc.vector.tensor_scalar(hot[:, :], g.iota_free[:, :], g.dst[:, bass.ds(c, 1)], None, ALU.is_equal)
                nc.vector.tensor_tensor(diag[:, :, :], g.ident[:, :].unsqueeze(1).to_broadcast([P, HD, P]),
                                        scores[:, bass.ds(c, 1), :].rearrange("p a h -> p (a h)").unsqueeze(2).to_broadcast([P, HD, P]),
                                        ALU.mult)
                v.drain()
                v.sem_inc(ready, 1)
                v.wait_ge(done, c + 1)
                v.sem_inc(turn, 1)
                nc.vector.tensor_reduce(peak[:, :], p_max[:, :, :], AX.X, ALU.max)
                v.drain()
                a = amax[:, bass.ds(tile, 1), :].rearrange("p a h -> p (a h)")
                nc.vector.tensor_tensor(a, a, peak[:, :], ALU.max)
                v.drain()


def edge_weights(nc, g, scores, amax, weights):
    with Phase(nc, "weigh") as ph:
        parts, left = ph.sb("parts", [P, T, 3, HD], BF16), ph.sb("left", [P, T, HD])
        sums = ph.sb("sums", [P, 2, U, HD])
        p_amax = [ph.ps(f"p_amax{b}", [P, U, 3, HD]) for b in range(2)]
        split, picked, taken, less = ph.sem("split"), ph.sem("picked"), ph.sem("taken"), ph.sem("less")
        block = ph.block()
        assert EC // U % 2 == 0

        @block.tensor
        def _(pe):
            registers = [pe.alloc_register(f"{ph.name}_pe_tile{u}") for u in range(U)]
            pe.wait_ge(split, 1)
            with pe.Fori(0, EC // U // 2) as i:
                for b in range(2):
                    tiles = tiles_of(pe, g, registers, i * 2 + b)
                    pe.wait_ge(taken, i * 2 + (b + 1))
                    for u in range(U):
                        ins = nc.tensor.matmul(p_amax[b][:, u, :, :].rearrange("p k h -> p (k h)"),
                                               g.attrs_t[:, bass.ds(i * (2 * U) + (b * U + u), 1), :].rearrange("p a e -> p (a e)"),
                                               parts[:, bass.ds(tiles[u], 1), :, :].rearrange("p a k h -> p (a k h)"),
                                               start=True, stop=True)
                    ins.then_inc(picked, 1)

        @block.vector
        def _(v):
            split3(nc, v, amax[:, :, :], [parts[:, :, k, :] for k in range(3)], left[:, :, :])
            v.drain()
            v.sem_inc(split, 1)
            v.sem_inc(taken, 2)
            nc.vector.tensor_copy(weights[:, :, HD], g.weight[:, :])
            with v.Fori(0, EC // U // 2) as i:
                for b in range(2):
                    v.wait_ge(picked, i * 2 + (b + 1))
                    nc.vector.tensor_reduce(sums[:, b, :, :], p_amax[b][:, :, :, :].rearrange("p u k h -> p u h k"), AX.X, ALU.add)                        .then_inc(taken, 1)
                    v.drain()
                    some = scores[:, bass.ds(i * (2 * U) + b * U, U), :]
                    nc.vector.tensor_tensor(some, some, sums[:, b, :, :], ALU.subtract)
            v.drain()
            v.sem_inc(less, 1)

        @block.scalar
        def _(act):
            act.wait_ge(less, 1)
            nc.scalar.activation(weights[:, :, 0:HD], scores[:, :, :], ACT.Exp)


def attend(nc, g, h_table, weights, acc):
    with Phase(nc, "attend") as ph:
        idx = ph.sb("idx", [P, U], I32)
        got = ph.sb("got", [P, U, D])
        hot = ph.sb("hot", [P, U, P])
        msg = ph.sb("msg", [P, U, WIDE])
        p_sum = [ph.ps(f"p_sum{b}", [P, 512]) for b in range(BANKS)]
        idx_set, turn, hot_ready, tail_ready, msg_ready, agg_done, added = (
            ph.sem(x) for x in ("idx_set", "turn", "hot_ready", "tail_ready", "msg_ready", "agg_done", "added"))
        gathered = [ph.sem(f"gathered{u}") for u in range(U)]
        block = ph.block()

        @block.sync
        def _(sp):
            for s in (agg_done, added, msg_ready):
                sp.sem_inc(s, U)

        @block.gpsimd
        def _(pool):
            gather_loop(nc, pool, ph, g.hrow, h_table, got, idx, gathered, msg_ready, idx_set, turn)

        @block.tensor
        def _(pe):
            with pe.Fori(0, EC // U) as i:
                for u in range(U):
                    pe.wait_ge(added, i * U + (u - BANKS + 1 + U))
                    pe.wait_ge(hot_ready, i * U + (u + 1))
                    pe.wait_ge(tail_ready, i * U + (u + 1))
                    pe.wait_ge(msg_ready, i * U + (u + 1 + U))
                    nc.tensor.matmul(p_sum[u % BANKS][:, 0:WIDE], hot[:, u, :], msg[:, u, :], start=True, stop=True).then_inc(agg_done, 1)

        @block.scalar
        def _(act):
            with act.Fori(0, EC // U) as i:
                for u in range(U):
                    act.wait_ge(agg_done, i * U + (u + 1))
                    act.sem_inc(turn, 1)
                    nc.scalar.copy(msg[:, u, D:WIDE], weights[:, bass.ds(i * U + u, 1), :].rearrange("p a w -> p (a w)"))\
                        .then_inc(tail_ready, 1)

        @block.vector
        def _(v):
            nc.vector.memset(acc[:, :, :], 0.0)

            def each(i, u):
                v.wait_ge(agg_done, i * U + (u + 1))
                nc.vector.tensor_scalar(hot[:, u, :], g.iota_free[:, :], g.dst[:, bass.ds(i * U + u, 1)], None,
                                        ALU.is_equal).then_inc(hot_ready, 1)
                v.wait_ge(gathered[u], i * 16 + 16)
                w = weights[:, bass.ds(i * U + u, 1), 0:HD].rearrange("p a h -> p (a h)")
                nc.vector.tensor_tensor(msg[:, u, 0:D].rearrange("p (h d) -> p h d", h=HD),
                                        got[:, u, :].rearrange("p (h d) -> p h d", h=HD),
                                        w.unsqueeze(2).to_broadcast([P, HD, DH]), ALU.mult).then_inc(msg_ready, 1)

            def add(i, u, tile):
                v.wait_ge(added, i * U + (u + U))
                v.wait_ge(agg_done, i * U + (u + 1 + U))
                a = acc[:, bass.ds(tile, 1), :].rearrange("p a f -> p (a f)")
                nc.vector.tensor_tensor(a, a, p_sum[u % BANKS][:, 0:WIDE], ALU.add).then_inc(added, 1)

            add_loop(nc, v, g, ph, each, add)


def divide_into(nc, g, acc, into):
    with Phase(nc, "divide") as ph:
        total, share = ph.sb("total", [P, T, HD]), ph.sb("share", [P, T, HD])
        deg, positive, root = ph.sb("deg", [P, T]), ph.sb("positive", [P, T]), ph.sb("root", [P, T])
        deg_ready, root_ready = ph.sem("deg_ready"), ph.sem("root_ready")
        block = ph.block()

        @block.scalar
        def _(act):
            act.wait_ge(deg_ready, 1)
            nc.scalar.activation(root[:, :], deg[:, :], ACT.Sqrt).then_inc(root_ready, 1)

        @block.vector
        def _(v):
            nc.vector.tensor_scalar(positive[:, :], acc[:, :, D + HD], 1.0, 0.0, ALU.add, ALU.is_gt)
            nc.vector.tensor_scalar(deg[:, :], acc[:, :, D + HD], 1.0, 1e-30, ALU.add, ALU.max).then_inc(deg_ready, 1)
            nc.vector.tensor_scalar(total[:, :, :], acc[:, :, D:D + HD], 1e-12, None, ALU.add)
            v.drain()
            nc.vector.reciprocal(share[:, :, :], total[:, :, :])
            v.drain()
            for t in range(T):
                a = acc[:, t, 0:D].rearrange("p (h d) -> p h d", h=HD)
                nc.vector.tensor_tensor(a, a, share[:, t, :].unsqueeze(2).to_broadcast([P, HD, DH]), ALU.mult)
            v.wait_ge(root_ready, 1)
            nc.vector.reciprocal(g.dinv[:, :], root[:, :])
            v.drain()
            nc.vector.tensor_tensor(g.dinv[:, :], g.dinv[:, :], positive[:, :], ALU.mult)
            nc.vector.tensor_tensor(into[:, :, :], into[:, :, :], acc[:, :, 0:D], ALU.add)


def relational_attention(nc, g, i):
    h_table, src_table = g.dram("h_table", [R * NP, D]), g.dram("src_table", [R * NP, HD])
    with Phase(nc, "rgat") as ph:
        score_dst, amax = ph.sb("score_dst", [P, T, R * HD]), ph.sb("amax", [P, T, HD])
        scores = ph.sb("scores", [P, EC, HD])
        with Phase(nc, "rgat_in") as inner:
            xn, xt = inner.sb("xn", [P, T, D]), inner.sb("xt", [P, T, 2, P])
            layernorm(nc, g, g.X, xn, turned=xt)
            relation_tables(nc, g, xt, i["L1_gnn_W"], i["L1_gnn_W_turned"], i["L1_gnn_attn_src"], i["L1_gnn_attn_dst"],
                            h_table, src_table, score_dst)
        edge_scores(nc, g, src_table, score_dst, scores)
        top, last, broken = ph.sb("top", [P, EC, HD]), ph.sb("last", [P, EC]), ph.sb("broken", [1, 1], I32)
        find_runs(nc, g, scores, top, last, broken)
        count = nc.values_load(broken[0:1, 0:1], min_val=0, max_val=EC * P)
        Phase.branch = True
        with nc.If(count > 0):
            peaks_in_any_order(nc, g, scores, amax)
        with nc.Else():
            peaks_of_runs(nc, g, top, last, amax)
        Phase.branch = False
        weights, acc = ph.sb("weights", [P, EC, HD + 1]), ph.sb("acc", [P, T, WIDE])
        edge_weights(nc, g, scores, amax, weights)
        attend(nc, g, h_table, weights, acc)
        divide_into(nc, g, acc, g.X)


STAGES = [capacity_ffn, relational_attention, switch_ffn, gcn_softmax, top2_gelu_ffn, gcn_residual, top2_relu_ffn]
UNUSED = ("L0_ffn_attention_mask",)


def column(a):
    return a.reshape(*a.shape[:-1], -1, P).swapaxes(-1, -2)


LAYOUT = {"L0_gnn_b1": column, "L0_ffn_b1": lambda a: column(a[None]), "L1_ffn_b1": column, "L2_ffn_b1": column,
          "L3_ffn_b1": column, "L2_ffn_ln_g": column, "L2_ffn_ln_b": column, "L3_gnn_W": lambda a: a.T}


def build(nc, i, out):
    Phase.count, Phase.spent = 0, []
    with ExitStack() as stack:
        g = Shared()

        def sb(name, shape, dt=F32):
            return stack.enter_context(nc.sbuf_tensor(name, shape, dt))

        g.dram = lambda name, shape, dt=F32: nc.dram_tensor(name, shape, dt, kind="Internal").ap()
        g.X = sb("X", [P, T, D])
        g.iota_free, g.iota_part = sb("iota_free", [P, P]), sb("iota_part", [P, 1])
        g.ident, g.upto, g.before, g.ones = (sb(s, [P, P]) for s in ("ident", "upto", "before", "ones"))
        g.ident_b = sb("ident_b", [P, P], BF16)
        g.zero_row = sb("zero_row", [P, 512])
        g.dinv = sb("dinv", [P, T])
        g.chunk_tile = sb("chunk_tile", [1, EC], I32)
        g.src, g.hrow = sb("src", [P, EC], I32), sb("hrow", [P, EC], I32)
        g.valid = sb("valid", [P, EC])
        g.dst, g.weight, g.etype = sb("dst", [P, EC]), sb("weight", [P, EC]), sb("etype", [P, EC])
        constants(nc, g, i["x"])
        sorted_rows = g.dram("sorted_rows", [P * EC, ROW])
        sort_edges(nc, g, i["src"], i["dst"], i["edge_type_8"], i["edge_weight"], i["edge_attr_32"], sorted_rows)
        g.attrs_t = sb("attrs_t", [P, EC, P], BF16)
        load_sorted(nc, g, sorted_rows)
        gine_stack(nc, g, i)
        for stage in STAGES:
            stage(nc, g, i)
        store(nc, g.X, out)


def kernel(**inputs):
    import numpy as np
    import concourse.bacc as bacc
    from concourse.bass_utils import run_bass_kernel_spmd

    nc = bacc.Bacc("TRN2", target_bir_lowering=False, num_devices=1)
    arrays, aps = {}, {}
    for name, given in inputs.items():
        a = np.ascontiguousarray(given)
        if a.ndim == 0 or name in UNUSED:
            continue
        if name == "L1_gnn_W":
            inputs_turned = np.ascontiguousarray(a.transpose(0, 2, 1))
            arrays["in_L1_gnn_W_turned"] = inputs_turned
            aps["L1_gnn_W_turned"] = nc.dram_tensor("in_L1_gnn_W_turned", a.shape, F32, kind="ExternalInput").ap()
        if name in LAYOUT:
            a = np.ascontiguousarray(LAYOUT[name](a))
        arrays[f"in_{name}"] = a
        aps[name] = nc.dram_tensor(f"in_{name}", a.shape, mybir.dt.from_np(a.dtype), kind="ExternalInput").ap()
    out = nc.dram_tensor("out", (N, D), F32, kind="ExternalOutput").ap()
    build(nc, aps, out)
    r = run_bass_kernel_spmd(nc, [arrays], core_ids=[0])
    return r.results[0]["out"]
```
